# Optimizing a Trainium2 kernel written in Bass

```python
import numpy as np
import jax
import jax.numpy as jnp

def _softmax(x, axis=-1):
    return jax.nn.softmax(x, axis=axis)

def _gelu(x):
    return jax.nn.gelu(x, approximate=True)

def _silu(x):
    return jax.nn.silu(x)

def _sigmoid(x):
    return jax.nn.sigmoid(x)

def _layernorm(x, axis=-1, eps=1e-05):
    m = jnp.mean(x, axis=axis, keepdims=True)
    v = jnp.var(x, axis=axis, keepdims=True)
    return (x - m) / jnp.sqrt(v + eps)

def _scatter_add(tgt, idx, src, axis=0):
    return tgt.at[idx].add(src)

def _segment_sum(src, seg, n):
    return jax.ops.segment_sum(src, seg, n)
kernel_name = 'mk_sandwich_d2_jaxref_r4_d745db'

def setup_inputs(seed: int=0):
    np.random.seed(seed)
    _w = jnp.asarray

    def _L0_attn_setup():
        import jax, jax.numpy as jnp
        import numpy as np
        HEADS = 16

        def _fm(t):
            return jax.nn.elu(t) + 1.0
        key = jax.random.key(seed)
        ks = jax.random.split(key, 9)
        B, N, D = (4, 2048, 256)
        s = 1.0 / np.sqrt(D)
        return {'x': jax.random.normal(ks[0], (B, N, D), dtype=jnp.float32), 'wq': jax.random.normal(ks[1], (D, D), dtype=jnp.float32) * s, 'bq': jnp.zeros((D,), dtype=jnp.float32), 'wk': jax.random.normal(ks[2], (D, D), dtype=jnp.float32) * s, 'bk': jnp.zeros((D,), dtype=jnp.float32), 'wv': jax.random.normal(ks[3], (D, D), dtype=jnp.float32) * s, 'bv': jnp.zeros((D,), dtype=jnp.float32), 'wo': jax.random.normal(ks[4], (D, D), dtype=jnp.float32) * s, 'bo': jnp.zeros((D,), dtype=jnp.float32)}
    _L0_attn_in = _L0_attn_setup()

    def _L0_ffn_setup():
        import jax, jax.numpy as jnp
        import numpy as np
        H = 256
        I = 512
        E = 8
        TOP_K = 2
        NUM_SHARED = 1
        key = jax.random.key(seed)
        ks = jax.random.split(key, 9)
        s = 0.02
        x = jax.random.normal(ks[0], (2, 512, H), dtype=jnp.float32)
        sg_w = jax.random.normal(ks[1], (I, H), dtype=jnp.float32) * s
        su_w = jax.random.normal(ks[2], (I, H), dtype=jnp.float32) * s
        sd_w = jax.random.normal(ks[3], (H, I), dtype=jnp.float32) * s
        router_w = jax.random.normal(ks[4], (E, H), dtype=jnp.float32) * s
        routing_bias = jnp.zeros((E,), dtype=jnp.float32)
        wg = jax.random.normal(ks[5], (E, I, H), dtype=jnp.float32) * s
        wu = jax.random.normal(ks[6], (E, I, H), dtype=jnp.float32) * s
        wd = jax.random.normal(ks[7], (E, H, I), dtype=jnp.float32) * s
        return {'x': x, 'sg_w': sg_w, 'su_w': su_w, 'sd_w': sd_w, 'router_w': router_w, 'routing_bias': routing_bias, 'wg': wg, 'wu': wu, 'wd': wd}
    _L0_ffn_in = _L0_ffn_setup()

    def _L1_attn_setup():
        import jax, jax.numpy as jnp
        import numpy as np
        HIDDEN = 256
        NUM_HEADS = 16
        NUM_KV = 4
        HEAD_DIM = HIDDEN // NUM_HEADS
        GROUPS = NUM_HEADS // NUM_KV
        SCALE = HEAD_DIM ** 0.5
        key = jax.random.key(seed)
        ks = jax.random.split(key, 9)
        s = 0.02
        B, N = (4, 512)
        return {'x': jax.random.normal(ks[0], (B, N, HIDDEN), dtype=jnp.float32), 'Wq': jax.random.normal(ks[1], (HIDDEN, NUM_HEADS * HEAD_DIM), dtype=jnp.float32) * s, 'bq': jnp.zeros((NUM_HEADS * HEAD_DIM,), dtype=jnp.float32), 'Wk': jax.random.normal(ks[2], (HIDDEN, NUM_KV * HEAD_DIM), dtype=jnp.float32) * s, 'bk': jnp.zeros((NUM_KV * HEAD_DIM,), dtype=jnp.float32), 'Wv': jax.random.normal(ks[3], (HIDDEN, NUM_KV * HEAD_DIM), dtype=jnp.float32) * s, 'bv': jnp.zeros((NUM_KV * HEAD_DIM,), dtype=jnp.float32), 'Wo': jax.random.normal(ks[4], (NUM_HEADS * HEAD_DIM, HIDDEN), dtype=jnp.float32) * s, 'bo': jnp.zeros((HIDDEN,), dtype=jnp.float32)}
    _L1_attn_in = _L1_attn_setup()

    def _L1_ffn_setup():
        import jax, jax.numpy as jnp
        import numpy as np
        D = 256
        H = 192
        E = 8
        K = 2
        NS = 2
        ROUTE_SCALE = 1.0

        def _gated_mlp(x, w1, w2):
            h = x @ w1.T
            y, g = jnp.split(h, 2, axis=-1)
            return y * jax.nn.silu(g) @ w2.T
        key = jax.random.key(seed)
        ks = jax.random.split(key, 6)
        s = 0.02
        return {'x': jax.random.normal(ks[0], (2, 256, D), jnp.float32), 'gate_w': jax.random.normal(ks[1], (E, D), jnp.float32) * s, 'W1': jax.random.normal(ks[2], (E, 2 * H, D), jnp.float32) * s, 'W2': jax.random.normal(ks[3], (E, D, H), jnp.float32) * s, 'Ws1': jax.random.normal(ks[4], (2 * NS * H, D), jnp.float32) * s, 'Ws2': jax.random.normal(ks[5], (D, NS * H), jnp.float32) * s}
    _L1_ffn_in = _L1_ffn_setup()
    _d = {'L0_attn_x': _L0_attn_in['x'], 'L0_attn_wq': _L0_attn_in['wq'], 'L0_attn_bq': _L0_attn_in['bq'], 'L0_attn_wk': _L0_attn_in['wk'], 'L0_attn_bk': _L0_attn_in['bk'], 'L0_attn_wv': _L0_attn_in['wv'], 'L0_attn_bv': _L0_attn_in['bv'], 'L0_attn_wo': _L0_attn_in['wo'], 'L0_attn_bo': _L0_attn_in['bo'], 'L0_ffn_sg_w': _L0_ffn_in['sg_w'], 'L0_ffn_su_w': _L0_ffn_in['su_w'], 'L0_ffn_sd_w': _L0_ffn_in['sd_w'], 'L0_ffn_router_w': _L0_ffn_in['router_w'], 'L0_ffn_routing_bias': _L0_ffn_in['routing_bias'], 'L0_ffn_wg': _L0_ffn_in['wg'], 'L0_ffn_wu': _L0_ffn_in['wu'], 'L0_ffn_wd': _L0_ffn_in['wd'], 'L1_attn_Wq': _L1_attn_in['Wq'], 'L1_attn_bq': _L1_attn_in['bq'], 'L1_attn_Wk': _L1_attn_in['Wk'], 'L1_attn_bk': _L1_attn_in['bk'], 'L1_attn_Wv': _L1_attn_in['Wv'], 'L1_attn_bv': _L1_attn_in['bv'], 'L1_attn_Wo': _L1_attn_in['Wo'], 'L1_attn_bo': _L1_attn_in['bo'], 'L1_ffn_gate_w': _L1_ffn_in['gate_w'], 'L1_ffn_W1': _L1_ffn_in['W1'], 'L1_ffn_W2': _L1_ffn_in['W2'], 'L1_ffn_Ws1': _L1_ffn_in['Ws1'], 'L1_ffn_Ws2': _L1_ffn_in['Ws2']}
    _x0 = _d['L0_attn_x']
    _d['L0_attn_x'] = jax.random.normal(jax.random.fold_in(jax.random.key(seed), 1), (4, 1024, 256), dtype=_x0.dtype)
    del _x0
    return _d

def reference(L0_attn_x, L0_attn_wq, L0_attn_bq, L0_attn_wk, L0_attn_bk, L0_attn_wv, L0_attn_bv, L0_attn_wo, L0_attn_bo, L0_ffn_sg_w, L0_ffn_su_w, L0_ffn_sd_w, L0_ffn_router_w, L0_ffn_routing_bias, L0_ffn_wg, L0_ffn_wu, L0_ffn_wd, L1_attn_Wq, L1_attn_bq, L1_attn_Wk, L1_attn_bk, L1_attn_Wv, L1_attn_bv, L1_attn_Wo, L1_attn_bo, L1_ffn_gate_w, L1_ffn_W1, L1_ffn_W2, L1_ffn_Ws1, L1_ffn_Ws2):

    def _L0_attn_ref(x, wq, bq, wk, bk, wv, bv, wo, bo):
        import jax, jax.numpy as jnp
        import numpy as np
        HEADS = 16

        def _fm(t):
            return jax.nn.elu(t) + 1.0
        B, N, D = x.shape
        H = HEADS
        Dh = D // H
        q = _fm((x @ wq + bq).reshape(B, N, H, Dh))
        k = _fm((x @ wk + bk).reshape(B, N, H, Dh))
        v = (x @ wv + bv).reshape(B, N, H, Dh)
        kv = jnp.einsum('bnhd,bnhe->bhde', k, v)
        z = 1.0 / (jnp.einsum('bnhd,bhd->bnh', q, k.sum(axis=1)) + 1e-06)
        scores = jnp.einsum('bnhd,bhde,bnh->bnhe', q, kv, z)
        out = scores.reshape(B, N, D) @ wo + bo
        return out

    def _L0_ffn_ref(x, sg_w, su_w, sd_w, router_w, routing_bias, wg, wu, wd):
        import jax, jax.numpy as jnp
        import numpy as np
        H = 256
        I = 512
        E = 8
        TOP_K = 2
        NUM_SHARED = 1
        orig_shape = x.shape
        xt = x.reshape(-1, H)
        T = xt.shape[0]
        shared = jax.nn.silu(xt @ sg_w.T) * (xt @ su_w.T) @ sd_w.T
        shared = shared / NUM_SHARED
        logits = xt @ router_w.T + routing_bias
        probs = jax.nn.sigmoid(logits)
        topk_p, topk_idx = jax.lax.top_k(probs, TOP_K)
        topk_p = topk_p / jnp.sum(topk_p, axis=-1, keepdims=True)
        w = jnp.zeros((T, E), dtype=xt.dtype)
        w = w.at[jnp.arange(T)[:, None], topk_idx].add(topk_p)
        g = jnp.einsum('th,eih->tei', xt, wg)
        u = jnp.einsum('th,eih->tei', xt, wu)
        h = jax.nn.silu(g) * u
        y = jnp.einsum('tei,ehi->teh', h, wd)
        routed = jnp.einsum('te,teh->th', w, y)
        return (shared + routed).reshape(orig_shape)

    def _L1_attn_ref(x, Wq, bq, Wk, bk, Wv, bv, Wo, bo):
        import jax, jax.numpy as jnp
        import numpy as np
        HIDDEN = 256
        NUM_HEADS = 16
        NUM_KV = 4
        HEAD_DIM = HIDDEN // NUM_HEADS
        GROUPS = NUM_HEADS // NUM_KV
        SCALE = HEAD_DIM ** 0.5
        B, N, _ = x.shape
        q = x @ Wq + bq
        k = x @ Wk + bk
        v = x @ Wv + bv
        q = q.reshape(B, N, NUM_HEADS, HEAD_DIM).transpose(0, 2, 1, 3)
        q = q.reshape(B, NUM_KV, GROUPS, N, HEAD_DIM).transpose(0, 2, 1, 3, 4)
        k = k.reshape(B, N, NUM_KV, HEAD_DIM).transpose(0, 2, 1, 3)
        v = v.reshape(B, N, NUM_KV, HEAD_DIM).transpose(0, 2, 1, 3)
        scores = jnp.einsum('bghnd,bhsd->bghns', q, k)
        attn = jax.nn.softmax(scores / SCALE, axis=-1)
        out = jnp.einsum('bghns,bhsd->bghnd', attn, v)
        out = out.transpose(0, 3, 1, 2, 4).reshape(B, N, NUM_HEADS * HEAD_DIM)
        return out @ Wo + bo

    def _L1_ffn_ref(x, gate_w, W1, W2, Ws1, Ws2):
        import jax, jax.numpy as jnp
        import numpy as np
        D = 256
        H = 192
        E = 8
        K = 2
        NS = 2
        ROUTE_SCALE = 1.0

        def _gated_mlp(x, w1, w2):
            h = x @ w1.T
            y, g = jnp.split(h, 2, axis=-1)
            return y * jax.nn.silu(g) @ w2.T
        x_shape = x.shape
        xf = x.reshape(-1, D)
        T = xf.shape[0]
        scores = jax.nn.softmax((xf @ gate_w.T).astype(jnp.float32), axis=-1)
        top_vals, top_idx = jax.lax.top_k(scores, K)
        weights = (top_vals * ROUTE_SCALE).astype(x.dtype)
        w_dense = jnp.zeros((T, E), x.dtype).at[jnp.arange(T)[:, None], top_idx].set(weights)
        h = jnp.einsum('td,ehd->teh', xf, W1)
        y, g = jnp.split(h, 2, axis=-1)
        eo = jnp.einsum('teh,edh->ted', y * jax.nn.silu(g), W2)
        z = jnp.einsum('te,ted->td', w_dense, eo)
        z = z + _gated_mlp(xf, Ws1, Ws2)
        return z.reshape(x_shape)
    x = L0_attn_x
    x = x + _layernorm(_L0_attn_ref(_layernorm(x, axis=-1), L0_attn_wq, L0_attn_bq, L0_attn_wk, L0_attn_bk, L0_attn_wv, L0_attn_bv, L0_attn_wo, L0_attn_bo), axis=-1)
    x = x + _layernorm(_L0_ffn_ref(_layernorm(x, axis=-1), L0_ffn_sg_w, L0_ffn_su_w, L0_ffn_sd_w, L0_ffn_router_w, L0_ffn_routing_bias, L0_ffn_wg, L0_ffn_wu, L0_ffn_wd), axis=-1)
    x = x + _layernorm(_L1_attn_ref(_layernorm(x, axis=-1), L1_attn_Wq, L1_attn_bq, L1_attn_Wk, L1_attn_bk, L1_attn_Wv, L1_attn_bv, L1_attn_Wo, L1_attn_bo), axis=-1)
    x = x + _layernorm(_L1_ffn_ref(_layernorm(x, axis=-1), L1_ffn_gate_w, L1_ffn_W1, L1_ffn_W2, L1_ffn_Ws1, L1_ffn_Ws2), axis=-1)
    return x

_drawn_inputs = setup_inputs


def setup_inputs(seed=0):
    import zlib

    import numpy as np

    out = dict(_drawn_inputs(seed))
    spreads = {'L0_attn_bq': (0.0, 0.306),
     'L0_attn_bk': (0.0, 0.484),
     'L0_attn_bv': (0.0, 0.1),
     'L0_attn_bo': (0.0, 0.1),
     'L0_ffn_routing_bias': (0.0, 0.1),
     'L1_attn_bq': (0.0, 0.8),
     'L1_attn_bk': (0.0, 0.8),
     'L1_attn_bv': (0.0, 0.1),
     'L1_attn_bo': (0.0, 0.1)}
    factors = {'L1_attn_Wq': 8.0, 'L1_attn_Wk': 8.0}
    for name, (base, spread) in spreads.items():
        noise = np.random.default_rng([zlib.crc32(name.encode()), seed]).standard_normal(out[name].shape)
        drawn = base * np.exp(spread * noise) if base else spread * noise
        out[name] = jnp.asarray(drawn.astype(out[name].dtype))
    for name, factor in factors.items():
        out[name] = (out[name] * factor).astype(out[name].dtype)
    return out
```

```python
import concourse.bass as bass
from concourse import mybir
from contextlib import ExitStack

F32 = mybir.dt.float32
F32R = mybir.dt.float32r
BF16 = mybir.dt.bfloat16
I32 = mybir.dt.int32
ALU = mybir.AluOpType
ACT = mybir.ActivationFunctionType
AX = mybir.AxisListType

P = 128
B, N, D = 4, 1024, 256
T = B * N // P
TB = N // P
KD = D // P
EPS = 1e-5
HEADS, DH = 16, 16
HPB = P // DH
NKV, GROUPS = 4, 4


def ge(eng, sem, value):
    if not (isinstance(value, int) and value <= 0):
        eng.wait_ge(sem, value)


def tiles(eng, n, unroll, step):
    for u in range(unroll):
        step(u, u)
    if n > unroll:
        with eng.Fori(1, n // unroll) as k:
            for u in range(unroll):
                step(k * unroll + u, u)


class Core:

    def __init__(self, nc, ctx):
        self.nc = nc
        self.x = ctx.enter_context(nc.sbuf_tensor("x", [P, T, D], F32))
        self.y = ctx.enter_context(nc.sbuf_tensor("y", [P, T, D], F32))
        self.mean_var = ctx.enter_context(nc.sbuf_tensor("mean_var", [P, T, 2], F32))
        self.rstd = ctx.enter_context(nc.sbuf_tensor("rstd", [P, T], F32))
        self.minus_half = ctx.enter_context(nc.sbuf_tensor("minus_half", [P, T], F32))
        self.ident = ctx.enter_context(nc.sbuf_tensor("ident", [P, P], F32))
        Phase.psum = ctx.enter_context(nc.psum_tensor("psum", [P, 8 * 512], F32))


class Phase:

    def __init__(self, nc, name):
        self.nc, self.name, self.ctx, self.next_bank = nc, name, ExitStack(), 0

    def __enter__(self):
        return self

    def __exit__(self, *e):
        self.ctx.close()

    def sb(self, name, shape, dt=F32):
        return self.ctx.enter_context(self.nc.sbuf_tensor(f"{self.name}_{name}", shape, dt))

    def ps(self, banks=1):
        first, self.next_bank = self.next_bank, self.next_bank + banks
        return self.psum[:, first * 512:(first + banks) * 512]

    def sem(self, name):
        sem = self.nc.alloc_semaphore(f"{self.name}_{name}")
        self.taken_semaphores.append(sem)
        return sem

    taken_semaphores = []

    @classmethod
    def clear_semaphores(cls, nc):
        nc.all_engine_barrier()
        nc.clear_and_free_semaphores(cls.taken_semaphores)
        nc.all_engine_barrier()
        cls.taken_semaphores = []

    def block(self):
        return self.nc.Block()


def constants(core):
    nc = core.nc
    with Phase(nc, "const") as ph:
        zeroed = ph.sem("zeroed")
        with ph.block() as block:
            @block.gpsimd
            def _(pool):
                nc.gpsimd.memset(core.minus_half[:, :], -0.5)
                nc.gpsimd.memset(core.ident[:, :], 0.0).then_inc(zeroed, 1)
                pool.wait_ge(zeroed, 1)
                nc.gpsimd.affine_select(out=core.ident[:, :], in_=core.ident[:, :], compare_op=ALU.not_equal,
                                        fill=1.0, base=0, pattern=[[-1, P]], channel_multiplier=1).then_inc(zeroed, 1)
                pool.wait_ge(zeroed, 2)


def split_weights(core, name, parts):
    nc = core.nc
    with Phase(nc, name) as ph:
        stage = ph.sb("stage", [P, 2, 2048])
        loaded = [ph.sem("loaded0"), ph.sem("loaded1")]
        high_done, low_done = ph.sem("high_done"), ph.sem("low_done")

        def staged(i):
            src = parts[i][0]
            return stage[0:src.shape[0], i % 2, 0:src.shape[1]]

        with ph.block() as block:
            @block.sync
            def _(sp):
                for i, (src, _, _) in enumerate(parts):
                    ge(sp, low_done, i - 1)
                    sp.dma_start(staged(i), src).then_inc(loaded[i % 2], 16)

            @block.scalar
            def _(act):
                for i, (_, high, _) in enumerate(parts):
                    act.wait_ge(loaded[i % 2], 16 * (i // 2 + 1))
                    nc.scalar.activation(high, staged(i), ACT.Copy).then_inc(high_done, 1)

            @block.vector
            def _(dve):
                for i, (_, high, low) in enumerate(parts):
                    dve.wait_ge(high_done, i + 1)
                    nc.vector.tensor_tensor(low, staged(i), high.bitcast(F32), ALU.subtract).then_inc(low_done, 1)


def residual_and_stats(core, name, x_dram=None, out_dram=None):
    nc = core.nc
    with Phase(nc, name) as ph:
        stats = ph.sb("stats", [P, T, 6])
        spread = ph.sb("spread", [P, T])
        var_eps = ph.sb("var_eps", [P, T])
        x_in, y_stats, x_ready = ph.sem("x_in"), ph.sem("y_stats"), ph.sem("x_ready")
        rstd_y, normed, stored = ph.sem("rstd_y"), ph.sem("normed"), ph.sem("stored")
        halves, stats_done, eps_added = ph.sem("halves"), ph.sem("stats_done"), ph.sem("eps_added")

        def aggregate(dve, n):
            dve.wait_ge(stats_done, (n + 1) * T)
            mean, var = core.mean_var[:, :, 0], core.mean_var[:, :, 1]
            nc.vector.tensor_tensor(spread[:, :], stats[:, :, 1], stats[:, :, 4], ALU.subtract)
            nc.vector.tensor_tensor(mean, stats[:, :, 1], stats[:, :, 4], ALU.add)
            nc.vector.tensor_tensor(var, stats[:, :, 2], stats[:, :, 5], ALU.add).then_inc(halves, 1)
            dve.wait_ge(halves, 3 * n + 1)
            nc.vector.scalar_tensor_tensor(out=spread[:, :], in0=spread[:, :], scalar=0.25, in1=spread[:, :],
                                           op0=ALU.mult, op1=ALU.mult)
            nc.vector.tensor_scalar(var, var, 1.0 / D, None, ALU.mult)
            nc.vector.tensor_scalar(mean, mean, 0.5, None, ALU.mult).then_inc(halves, 1)
            dve.wait_ge(halves, 3 * n + 2)
            nc.vector.tensor_tensor(var, var, spread[:, :], ALU.add).then_inc(halves, 1)
            dve.wait_ge(halves, 3 * n + 3)

        def pool_rstd(pool, wait_for, eps_count):
            pool.wait_ge(halves, 3 * wait_for)
            nc.gpsimd.tensor_scalar(var_eps[:, :], core.mean_var[:, :, 1], EPS, 1.0, ALU.add, ALU.mult)\
                .then_inc(eps_added, 1)
            pool.wait_ge(eps_added, eps_count)
            nc.gpsimd.tensor_tensor(core.rstd[:, :], var_eps[:, :], core.minus_half[:, :], ALU.pow)\
                .then_inc(rstd_y, 1)

        with ph.block() as block:
            @block.sync
            def _(sp):
                if x_dram is not None:
                    for b in range(B):
                        sp.dma_start(core.x[:, b * TB:(b + 1) * TB, :], x_dram[b, :, :, :]).then_inc(x_in, 16)
                        sp.wait_ge(x_in, b * 16 + 16)
                if out_dram is not None:
                    for b in range(B):
                        sp.wait_ge(x_ready, (b + 1) * TB)
                        sp.dma_start(out_dram[b, :, :, :], core.x[:, b * TB:(b + 1) * TB, :]).then_inc(stored, 16)
                    sp.wait_ge(stored, 16 * B)

            @block.gpsimd
            def _(pool):
                if x_dram is None:
                    pool_rstd(pool, 1, 1)

                    def add(i, u):
                        pool.wait_ge(normed, i + 1)
                        nc.gpsimd.tensor_tensor(core.x[:, i, :], core.x[:, i, :], core.y[:, i, :], ALU.add)\
                            .then_inc(x_ready, 1)
                    tiles(pool, T, 4, add)
                if out_dram is None:
                    pool_rstd(pool, 1 if x_dram is not None else 2, 1 if x_dram is not None else 2)

            @block.vector
            def _(dve):
                done = 0
                if x_dram is None:
                    def y_stats_of(i, u):
                        nc.vector.bn_stats(stats[:, i, :], core.y[:, i, :]).then_inc(stats_done, 1)

                    tiles(dve, T, 4, y_stats_of)
                    aggregate(dve, 0)
                    done = 1
                    dve.wait_ge(rstd_y, 1)

                    def norm(i, u):
                        nc.vector.tensor_scalar(core.y[:, i, :], core.y[:, i, :], core.mean_var[:, i, 0:1],
                                                core.rstd[:, bass.ds(i, 1)], ALU.subtract, ALU.mult).then_inc(normed, 1)
                    tiles(dve, T, 4, norm)
                if out_dram is None:
                    def x_stats_of(i, u):
                        if x_dram is not None:
                            if u == 0:
                                dve.wait_ge(x_in, i * 2 + 16)
                        else:
                            dve.wait_ge(x_ready, i + 1)
                        nc.vector.bn_stats(stats[:, i, :], core.x[:, i, :]).then_inc(stats_done, 1)

                    tiles(dve, T, TB, x_stats_of)
                    if done:
                        dve.wait_ge(normed, T)
                    aggregate(dve, done)


def normalised_transposed(core, ph, block_fns=None):
    pass


def linear_attention(core, w, qkv_high, qkv_low, bias_qk_v, y_out):
    nc = core.nc
    with Phase(nc, "la") as ph:
        xhat = [ph.sb(f"xhat{j}", [P, D]) for j in range(2)]
        xt_high = [ph.sb(f"xt_high{j}", [P, KD, P], F32R) for j in range(2)]
        xt_low = [ph.sb(f"xt_low{j}", [P, KD, P], F32R) for j in range(2)]
        qk_lin = [ph.sb(f"qk_lin{j}", [P, 2 * D]) for j in range(2)]
        qk_exp = [ph.sb(f"qk_exp{j}", [P, 2 * D]) for j in range(2)]
        qk_relu = [ph.sb(f"qk_relu{j}", [P, 2 * D]) for j in range(2)]
        qk = [ph.sb(f"qk{j}", [P, 2 * D]) for j in range(2)]
        v1 = [ph.sb(f"v1{j}", [P, KD, P + 1]) for j in range(2)]
        qT = ph.sb("qT", [P, KD, N])
        kv = ph.sb("kv", [P, KD, P + HPB])
        head_mask = ph.sb("head_mask", [P, P])
        zcol_mask = ph.sb("zcol_mask", [P, HPB])
        zcol_work = ph.sb("zcol_work", [P, HPB])
        z = [ph.sb(f"z{j}", [P, HEADS]) for j in range(2)]
        bias = ph.sb("bias", [P, 3 * D])

        turn_ps = ph.ps()
        proj_ps = ph.ps()
        projv_ps = ph.ps()
        kv_ps = [ph.ps() for j in range(KD)]
        q_turn_ps = ph.ps()
        num_ps = [ph.ps() for j in range(2)]

        s = {n: ph.sem(n) for n in ("bias_in", "ones_set", "masks", "xhat_done", "turned", "high", "low",
                                    "projected", "linear", "v_done", "expd", "relud", "qk_done", "summed",
                                    "kv_done", "q_turned", "q_copied", "numer", "z_eps", "z_done", "y_done")}

        with ph.block() as block:
            @block.sync
            def _(sp):
                sp.dma_start(bias[:, :], bias_qk_v.to_broadcast([P, 3 * D])).then_inc(s["bias_in"], 16)

            @block.gpsimd
            def _(pool):
                for j in range(2):
                    nc.gpsimd.memset(v1[j][:, :, P:P + 1], 1.0).then_inc(s["ones_set"], 1)
                nc.gpsimd.memset(head_mask[:, :], 1.0).then_inc(s["masks"], 1)
                nc.gpsimd.memset(zcol_mask[:, :], 1.0).then_inc(s["masks"], 1)
                done = 2
                for m, pattern in ((head_mask, [[DH, HPB], [0, DH]]), (zcol_mask, [[DH, HPB]])):
                    view = m[:, :].rearrange("p (h c) -> p h c", c=DH) if m is head_mask else m[:, :]
                    neg = [[-st, n] for st, n in pattern]
                    pool.wait_ge(s["masks"], done)
                    nc.gpsimd.affine_select(out=view, in_=view, compare_op=ALU.is_ge, fill=0.0, base=0,
                                            pattern=neg, channel_multiplier=1).then_inc(s["masks"], 1)
                    pool.wait_ge(s["masks"], done + 1)
                    nc.gpsimd.affine_select(out=view, in_=view, compare_op=ALU.is_ge, fill=0.0, base=DH - 1,
                                            pattern=pattern, channel_multiplier=-1).then_inc(s["masks"], 1)
                    done += 2

            @block.vector
            def _(dve):
                dve.wait_ge(s["bias_in"], 16)
                dve.wait_ge(s["ones_set"], 2)
                dve.wait_ge(s["masks"], 6)

                def norm(i, j):
                    ge(dve, s["turned"], i - 1)
                    nc.vector.tensor_scalar(xhat[j][:, :], core.x[:, i, :], core.mean_var[:, i, 0:1],
                                            core.rstd[:, bass.ds(i, 1)], ALU.subtract, ALU.mult)\
                        .then_inc(s["xhat_done"], 1)

                def low(i, j):
                    dve.wait_ge(s["high"], i + 1)
                    ge(dve, s["projected"], i - 1)
                    nc.vector.tensor_tensor(xt_low[j][:, :, :], turn_ps[:, 0:D].rearrange("p (k t) -> p k t", k=KD),
                                            xt_high[j][:, :, :].bitcast(F32), ALU.subtract).then_inc(s["low"], 1)

                def add_bias(i, j):
                    dve.wait_ge(s["projected"], i + 1)
                    ge(dve, s["expd"], i - 1)
                    ge(dve, s["relud"], i - 1)
                    nc.vector.tensor_tensor(qk_lin[j][:, :], proj_ps[:, :], bias[:, 0:2 * D], ALU.add)\
                        .then_inc(s["linear"], 1)
                    ge(dve, s["summed"], i - 1)
                    nc.vector.tensor_tensor(v1[j][:, :, 0:P], projv_ps[:, 0:D].rearrange("p (k c) -> p k c", k=KD),
                                            bias[:, 2 * D:].rearrange("p (k c) -> p k c", k=KD), ALU.add)\
                        .then_inc(s["v_done"], 1)

                def feature_map(i, j):
                    dve.wait_ge(s["expd"], i + 1)
                    dve.wait_ge(s["relud"], i + 1)
                    ge(dve, s["q_turned"], i - 1)
                    nc.vector.scalar_tensor_tensor(out=qk[j][:, :], in0=qk_exp[j][:, :], scalar=1.0,
                                                   in1=qk_relu[j][:, :], op0=ALU.min, op1=ALU.add)\
                        .then_inc(s["qk_done"], 1)

                def keep_kv(b):
                    dve.wait_ge(s["summed"], b * TB + TB)
                    ge(dve, s["numer"], b * TB)
                    for k in range(KD):
                        nc.vector.tensor_tensor(kv[:, k, 0:P], kv_ps[k][:, 0:P], head_mask[:, :], ALU.mult)
                        nc.vector.tensor_scalar(kv[:, k, P:P + HPB], zcol_mask[:, :], kv_ps[k][:, P:P + 1], None,
                                                ALU.mult).then_inc(s["kv_done"], 1)

                def scores(i, j):
                    dve.wait_ge(s["numer"], i + 1)
                    ps = num_ps[j][:, 0:KD * (P + HPB)].rearrange("p (k c) -> p k c", k=KD)
                    zj = z[j][:, :].rearrange("p (k h) -> p k h", k=KD)
                    nc.vector.tensor_scalar(zj, ps[:, :, P:P + HPB], 1e-6, None, ALU.add).then_inc(s["z_eps"], 1)
                    dve.wait_ge(s["z_eps"], i + 1)
                    nc.vector.reciprocal(z[j][:, :], z[j][:, :]).then_inc(s["z_done"], 1)
                    dve.wait_ge(s["z_done"], i + 1)
                    for k in range(KD):
                        last = nc.vector.tensor_tensor(
                            y_out[:, i, k * P:(k + 1) * P].rearrange("p (h c) -> p h c", c=DH),
                            ps[:, k, 0:P].rearrange("p (h c) -> p h c", c=DH),
                            z[j][:, k * HPB:(k + 1) * HPB].unsqueeze(2).to_broadcast([P, HPB, DH]), ALU.mult)
                    last.then_inc(s["y_done"], 1)

                def batch(b):
                    for u in range(TB + 1):
                        i, j = b * TB + u, u % 2
                        if u < TB:
                            norm(i, j)
                            low(i, j)
                        if u >= 1:
                            add_bias(i - 1, 1 - j)
                            feature_map(i - 1, 1 - j)
                    keep_kv(b)
                    for u in range(TB):
                        scores(b * TB + u, u % 2)
                batch(0)
                with dve.Fori(1, B) as b:
                    batch(b)

            @block.scalar
            def _(act):
                def high(i, j):
                    act.wait_ge(s["turned"], i + 1)
                    ge(act, s["projected"], i - 1)
                    nc.scalar.activation(xt_high[j][:, :, :], turn_ps[:, 0:D].rearrange("p (k t) -> p k t", k=KD),
                                         ACT.Copy).then_inc(s["high"], 1)

                def parts(i, j):
                    act.wait_ge(s["linear"], i + 1)
                    ge(act, s["qk_done"], i - 1)
                    nc.scalar.activation(qk_exp[j][:, :], qk_lin[j][:, :], ACT.Exp).then_inc(s["expd"], 1)
                    nc.scalar.activation(qk_relu[j][:, :], qk_lin[j][:, :], ACT.Relu).then_inc(s["relud"], 1)

                def q_copy(i, u):
                    act.wait_ge(s["q_turned"], i + 1)
                    if u == 0:
                        ge(act, s["numer"], i)
                    nc.scalar.activation(qT[:, :, u * P:(u + 1) * P],
                                         q_turn_ps[:, 0:D].rearrange("p (k t) -> p k t", k=KD), ACT.Copy)\
                        .then_inc(s["q_copied"], 1)

                def batch(b):
                    for u in range(TB + 1):
                        i, j = b * TB + u, u % 2
                        if u < TB:
                            high(i, j)
                        if u >= 1:
                            parts(i - 1, 1 - j)
                            q_copy(i - 1, u - 1)
                batch(0)
                with act.Fori(1, B) as b:
                    batch(b)

            @block.tensor
            def _(pe):
                def turn(i, j):
                    pe.wait_ge(s["xhat_done"], i + 1)
                    ge(pe, s["low"], i)
                    for k in range(KD):
                        last = nc.tensor.transpose(turn_ps[:, k * P:(k + 1) * P], xhat[j][:, k * P:(k + 1) * P],
                                                   core.ident[:, :])
                    last.then_inc(s["turned"], 1)

                def project(i, j):
                    pe.wait_ge(s["low"], i + 1)
                    ge(pe, s["linear"], i)
                    ge(pe, s["v_done"], i)
                    for out, lo, hi in ((proj_ps[:, :], 0, 2 * D), (projv_ps[:, 0:D], 2 * D, 3 * D)):
                        n = 0
                        for k in range(KD):
                            for xt, wt in ((xt_high, qkv_high), (xt_low, qkv_high), (xt_high, qkv_low)):
                                n += 1
                                last = nc.tensor.matmul(out, xt[j][:, k, :], wt[:, k, lo:hi], start=(n == 1),
                                                        stop=(n == 3 * KD))
                    last.then_inc(s["projected"], 1)

                def sum_kv(i, j, u):
                    pe.wait_ge(s["qk_done"], i + 1)
                    pe.wait_ge(s["v_done"], i + 1)
                    if u == 0:
                        if not isinstance(i, int):
                            pe.wait_ge(s["kv_done"], i * KD // TB if isinstance(i, int) else b_of["b"] * KD)
                    for k in range(KD):
                        last = nc.tensor.matmul(kv_ps[k][:, 0:P + 1], qk[j][:, D + k * P:D + (k + 1) * P],
                                                v1[j][:, k, :], start=(u == 0), stop=(u == TB - 1))
                    last.then_inc(s["summed"], 1)
                    ge(pe, s["q_copied"], i)
                    for k in range(KD):
                        last = nc.tensor.transpose(q_turn_ps[:, k * P:(k + 1) * P], qk[j][:, k * P:(k + 1) * P],
                                                   core.ident[:, :])
                    last.then_inc(s["q_turned"], 1)

                b_of = {}

                def score(b, u):
                    i = b * TB + u
                    ge(pe, s["y_done"], i - 1)
                    for k in range(KD):
                        last = nc.tensor.matmul(num_ps[u % 2][:, k * (P + HPB):(k + 1) * (P + HPB)],
                                                qT[:, k, u * P:(u + 1) * P], kv[:, k, :], start=True, stop=True)
                    last.then_inc(s["numer"], 1)

                def batch(b):
                    b_of["b"] = b
                    for u in range(TB + 2):
                        i = b * TB + u
                        if u < TB:
                            turn(i, u % 2)
                        if 1 <= u <= TB:
                            project(i - 1, (u - 1) % 2)
                        if u >= 2:
                            sum_kv(i - 2, u % 2, u - 2)
                    pe.wait_ge(s["kv_done"], b * KD + KD)
                    pe.wait_ge(s["q_copied"], b * TB + TB)
                    for u in range(TB):
                        score(b, u)
                batch(0)
                with pe.Fori(1, B) as b:
                    batch(b)


def output_projection(core, name, wo_high, wo_low, bias_row):
    nc = core.nc
    with Phase(nc, name) as ph:
        at_high = [ph.sb(f"at_high{j}", [P, KD, P], F32R) for j in range(2)]
        at_low = [ph.sb(f"at_low{j}", [P, KD, P], F32R) for j in range(2)]
        bias = ph.sb("bias", [P, D])
        turn_ps = [ph.ps() for j in range(2)]
        out_ps = [ph.ps() for j in range(2)]
        s = {n: ph.sem(n) for n in ("bias_in", "turned", "high", "low", "projected", "done")}
        with ph.block() as block:
            @block.sync
            def _(sp):
                sp.dma_start(bias[:, :], bias_row.to_broadcast([P, D])).then_inc(s["bias_in"], 16)

            @block.tensor
            def _(pe):
                def turn(i, j):
                    ge(pe, s["low"], i - 1)
                    for k in range(KD):
                        last = nc.tensor.transpose(turn_ps[j][:, k * P:(k + 1) * P],
                                                   core.y[:, i, k * P:(k + 1) * P], core.ident[:, :])
                    last.then_inc(s["turned"], 1)

                def project(i, j):
                    pe.wait_ge(s["low"], i + 1)
                    ge(pe, s["done"], i - 1)
                    n = 0
                    for k in range(KD):
                        for at, wt in ((at_high, wo_high), (at_low, wo_high), (at_high, wo_low)):
                            n += 1
                            last = nc.tensor.matmul(out_ps[j][:, 0:D], at[j][:, k, :], wt[:, k, :], start=(n == 1),
                                                    stop=(n == 3 * KD))
                    last.then_inc(s["projected"], 1)

                for i in range(T + 1):
                    if i < T:
                        turn(i, i % 2)
                    if i >= 1:
                        project(i - 1, (i - 1) % 2)

            @block.scalar
            def _(act):
                def high(i, u):
                    j = u % 2
                    act.wait_ge(s["turned"], i + 1)
                    ge(act, s["projected"], i - 1)
                    nc.scalar.activation(at_high[j][:, :, :], turn_ps[j][:, 0:D].rearrange("p (k t) -> p k t", k=KD),
                                         ACT.Copy).then_inc(s["high"], 1)
                tiles(act, T, 2, high)

            @block.vector
            def _(dve):
                dve.wait_ge(s["bias_in"], 16)

                def low(i, j):
                    dve.wait_ge(s["high"], i + 1)
                    ge(dve, s["projected"], i - 1)
                    nc.vector.tensor_tensor(at_low[j][:, :, :], turn_ps[j][:, 0:D].rearrange("p (k t) -> p k t", k=KD),
                                            at_high[j][:, :, :].bitcast(F32), ALU.subtract).then_inc(s["low"], 1)

                def finish(i, j):
                    dve.wait_ge(s["projected"], i + 1)
                    nc.vector.tensor_tensor(core.y[:, i, :], out_ps[j][:, 0:D], bias[:, :], ALU.add)\
                        .then_inc(s["done"], 1)
                low(0, 0)
                low(1, 1)
                finish(0, 0)
                with dve.Fori(1, T // 2) as k:
                    low(k * 2, 0)
                    finish(k * 2 - 1, 1)
                    low(k * 2 + 1, 1)
                    finish(k * 2, 0)
                finish(T - 1, 1)
                dve.wait_ge(s["done"], T)


def attention_projections(core, w_high, w_low, bias_col, q_dram, k_dram, v_all):
    nc = core.nc
    G = 4
    NG = T // G
    with Phase(nc, "ap") as ph:
        xhat = [ph.sb(f"xhat{j}", [P, D]) for j in range(2)]
        xt_high = [ph.sb(f"xt_high{j}", [P, KD, G * P], F32R) for j in range(2)]
        xt_low = [ph.sb(f"xt_low{j}", [P, KD, G * P], F32R) for j in range(2)]
        lin = [ph.sb(f"lin{m}", [P, G * P]) for m in range(3)]
        high = [ph.sb(f"high{m}", [P, G * P], F32R) for m in range(3)]
        low = [ph.sb(f"low{m}", [P, G * P], F32R) for m in range(3)]
        bias = ph.sb("bias", [P, 3])
        turn_ps = [ph.ps() for j in range(2)]
        proj_ps = [ph.ps() for m in range(3)]
        v_ps = ph.ps()
        s = {n: ph.sem(n) for n in ("bias_in", "v_cleared", "xhat_done", "turned", "high", "low", "projected",
                                    "linear", "part_high", "part_low", "stored", "v_turned", "v_kept")}
        with ph.block() as block:
            @block.sync
            def _(sp):
                sp.dma_start(bias[:, :], bias_col).then_inc(s["bias_in"], 16)

                def store(g):
                    sp.wait_ge(s["part_low"], g * 3 + 3)
                    cols = bass.ds(g * (G * P), G * P)
                    for m in range(2):
                        sp.dma_start(q_dram[0, m * P:(m + 1) * P, cols], high[m][:, :].bitcast(F32)).then_inc(s["stored"], 16)
                        sp.dma_start(q_dram[1, m * P:(m + 1) * P, cols], low[m][:, :].bitcast(F32)).then_inc(s["stored"], 16)
                    sp.dma_start(k_dram[0, :, cols], high[2][0:64, :].bitcast(F32)).then_inc(s["stored"], 16)
                    sp.dma_start(k_dram[1, :, cols], low[2][0:64, :].bitcast(F32)).then_inc(s["stored"], 16)
                tiles(sp, NG, 2, lambda g, u: store(g))
                sp.wait_ge(s["stored"], 96 * NG)

            @block.gpsimd
            def _(pool):
                nc.gpsimd.memset(v_all[:, :, :, :], 0.0).then_inc(s["v_cleared"], 1)
                pool.wait_ge(s["v_cleared"], 1)
                nc.gpsimd.memset(v_all[:, :, :, DH:DH + 1], 1.0).then_inc(s["v_cleared"], 1)

            @block.vector
            def _(dve):
                dve.wait_ge(s["v_cleared"], 2)

                def norm(i, j):
                    ge(dve, s["turned"], i - 1)
                    nc.vector.tensor_scalar(xhat[j][:, :], core.x[:, i, :], core.mean_var[:, i, 0:1],
                                            core.rstd[:, bass.ds(i, 1)], ALU.subtract, ALU.mult)\
                        .then_inc(s["xhat_done"], 1)

                def lower(i, u, gj):
                    dve.wait_ge(s["high"], i + 1)
                    nc.vector.tensor_tensor(xt_low[gj][:, :, u * P:(u + 1) * P],
                                            turn_ps[u % 2][:, 0:D].rearrange("p (k t) -> p k t", k=KD),
                                            xt_high[gj][:, :, u * P:(u + 1) * P].bitcast(F32), ALU.subtract)\
                        .then_inc(s["low"], 1)

                def group(g, gj):
                    ge(dve, s["projected"], g * 3 - 3)
                    norm(g * G, 0)
                    for u in range(G):
                        i = g * G + u
                        if u + 1 < G:
                            norm(i + 1, (u + 1) % 2)
                        lower(i, u, gj)
                    ge(dve, s["stored"], g * 96)
                    for m in range(3):
                        dve.wait_ge(s["part_high"], g * 3 + (m + 1))
                        nc.vector.tensor_tensor(low[m][:, :], lin[m][:, :], high[m][:, :].bitcast(F32),
                                                ALU.subtract).then_inc(s["part_low"], 1)
                    dve.wait_ge(s["v_turned"], g + 1)
                    nc.vector.tensor_copy(v_all[:, bass.ds(g * G, G), :, 0:DH],
                                          v_ps[:, :].rearrange("p (t f) -> p t f", t=G)[:, :, 64:128]
                                          .rearrange("p t (h d) -> p t h d", d=DH)).then_inc(s["v_kept"], 1)
                tiles(dve, NG, 2, group)

            @block.scalar
            def _(act):
                act.wait_ge(s["bias_in"], 16)

                def group(g, gj):
                    ge(act, s["projected"], g * 3 - 3)
                    for u in range(G):
                        act.wait_ge(s["turned"], g * G + (u + 1))
                        nc.scalar.activation(xt_high[gj][:, :, u * P:(u + 1) * P],
                                             turn_ps[u % 2][:, 0:D].rearrange("p (k t) -> p k t", k=KD),
                                             ACT.Copy).then_inc(s["high"], 1)
                    ge(act, s["part_low"], g * 3)
                    ge(act, s["stored"], g * 96)
                    ge(act, s["v_turned"], g)
                    for m in range(3):
                        act.wait_ge(s["projected"], g * 3 + (m + 1))
                        nc.scalar.activation(lin[m][:, :], proj_ps[m][:, :], ACT.Identity, bias=bias[:, m:m + 1])\
                            .then_inc(s["linear"], 1)
                        act.wait_ge(s["linear"], g * 3 + (m + 1))
                        nc.scalar.activation(high[m][:, :], lin[m][:, :], ACT.Copy).then_inc(s["part_high"], 1)
                tiles(act, NG, 2, group)

            @block.tensor
            def _(pe):
                def group(g, gj):
                    for u in range(G):
                        i = g * G + u
                        pe.wait_ge(s["xhat_done"], i + 1)
                        ge(pe, s["low"], i - 1)
                        for k in range(KD):
                            last = nc.tensor.transpose(turn_ps[u % 2][:, k * P:(k + 1) * P],
                                                       xhat[u % 2][:, k * P:(k + 1) * P], core.ident[:, :])
                        last.then_inc(s["turned"], 1)
                    pe.wait_ge(s["low"], g * G + G)
                    for m in range(3):
                        ge(pe, s["linear"], g * 3 + m - 2)
                        n = 0
                        for k in range(KD):
                            for wt, xt in ((w_high, xt_high), (w_high, xt_low), (w_low, xt_high)):
                                n += 1
                                last = nc.tensor.matmul(proj_ps[m][:, :], wt[:, k, m * P:(m + 1) * P],
                                                        xt[gj][:, k, :], start=(n == 1), stop=(n == 3 * KD))
                        last.then_inc(s["projected"], 1)
                    pe.wait_ge(s["linear"], g * 3 + 3)
                    ge(pe, s["v_kept"], g)
                    for u in range(G):
                        last = nc.tensor.transpose(v_ps[:, u * P:(u + 1) * P], lin[2][:, u * P:(u + 1) * P],
                                                   core.ident[:, :])
                    last.then_inc(s["v_turned"], 1)
                tiles(pe, NG, 2, group)


def softmax_attention(core, q_dram, k_dram, v_all, negmax_dram, o_dram):
    nc = core.nc
    QU = N // 2
    QT = QU // P
    KT = N // P
    ROWS = 4 * DH
    START = 3
    STEPS = NKV * KT
    END = STEPS - 2
    MAXES = HEADS * QT
    with Phase(nc, "sa") as ph:
        q_stack = [ph.sb(f"q_stack{h}", [P, HEADS, QU], F32R) for h in range(2)]
        k_max = ph.sb("k_max", [ROWS, NKV, N], F32R)
        k_main = ph.sb("k_main", [P, NKV, N], F32R)
        v_now = ph.sb("v_now", [P, KT, NKV, 32])
        probs = [ph.sb(f"probs{j}", [P, QU]) for j in range(8)]
        negmax = [ph.sb(f"negmax{h}", [P, QT, HEADS]) for h in range(2)]
        turned_high = ph.sb("turned_high", [HEADS, QU], F32R)
        turned_low = ph.sb("turned_low", [HEADS, QU], F32R)
        o_sb = [ph.sb(f"o_sb{j}", [P, QU]) for j in range(2)]
        st_ps = [ph.ps() for j in range(3)]
        mx_ps = [ph.ps(2) for j in range(2)]
        o_ps = ph.ps()
        s = {n: ph.sem(n) for n in ("pads", "q_in0", "q_in1", "kmax_in", "kmain_in", "v_in", "max_scored",
                                    "maxed", "turned", "t_high", "t_low", "neg_out", "neg_in0", "neg_in1", "scored",
                                    "expd", "weighted", "o_kept", "o_out0", "o_out1")}

        def max_steps(step):
            def until(n):
                return min(max(0, n - START), END - START) * MAXES // (END - START)
            return range(until(step), until(step + 1))

        with ph.block() as block:
            @block.gpsimd
            def _(pool):
                for q in q_stack:
                    nc.gpsimd.memset(q[64:P, :, :].bitcast(F32), 0.0).then_inc(s["pads"], 1)
                nc.gpsimd.memset(k_main[64:P, :, :].bitcast(F32), 0.0).then_inc(s["pads"], 1)
                pool.wait_ge(s["pads"], 3)
                nc.gpsimd.memset(k_main[64:66, :, :].bitcast(F32), 1.0).then_inc(s["pads"], 1)

                def load_v(b):
                    ge(pool, s["weighted"], b * (2 * STEPS))
                    nc.gpsimd.tensor_copy(v_now[:, :, :, :], v_all[:, bass.ds(b * KT, KT), :, :]).then_inc(s["v_in"], 1)

                def store_o(b, h, kv):
                    done = b * (2 * NKV) + h * NKV + kv
                    pool.wait_ge(s["o_kept"], done + 1)
                    pool.dma_start(o_dram[b, h, kv, :, :], o_sb[kv % 2][:, :]).then_inc(s[f"o_out{kv % 2}"], 16)

                def batch(b, last):
                    for h in range(2):
                        for kv in range(NKV):
                            if h == 1 and kv == NKV - 1 and not last:
                                load_v(b + 1)
                            store_o(b, h, kv)
                pool.wait_ge(s["pads"], 4)
                load_v(0)
                with pool.Fori(0, B - 1) as b:
                    batch(b, False)
                batch(B - 1, True)
                for j in range(2):
                    pool.wait_ge(s[f"o_out{j}"], 16 * NKV * B)

            @block.sync
            def _(sp):
                def load_q(b, h):
                    ge(sp, s["scored"], (b - 1) * (2 * 4 * STEPS) + (h + 1) * (4 * STEPS))
                    for r, part in enumerate((0, 1, 0, 1)):
                        sp.dma_start(q_stack[h][r * DH:(r + 1) * DH, :, :].bitcast(F32),
                                     q_dram[part, :, bass.ds(b * N + h * QU, QU)]
                                     .rearrange("(h d) t -> d h t", d=DH)).then_inc(s[f"q_in{h}"], 16)

                def load_k(dst, sem, b):
                    for r, part in enumerate((0, 0, 1, 1)):
                        sp.dma_start(dst[r * DH:(r + 1) * DH, :, :].bitcast(F32),
                                     k_dram[part, :, bass.ds(b * N, N)].rearrange("(h d) t -> d h t", d=DH))\
                            .then_inc(s[sem], 16)

                def put_negmax(b, h):
                    unit = b * 2 + h
                    sp.wait_ge(s["t_low"], unit + 1)
                    sp.dma_start(negmax_dram[unit, 0, :, :], turned_high[:, :].bitcast(F32)).then_inc(s["neg_out"], 16)
                    sp.dma_start(negmax_dram[unit, 1, :, :], turned_low[:, :].bitcast(F32)).then_inc(s["neg_out"], 16)
                    sp.wait_ge(s["neg_out"], unit * 32 + 32)
                    sp.dma_start(q_stack[h][64:66, :, :].bitcast(F32), negmax_dram[unit, :, :, :]).then_inc(s[f"neg_in{h}"], 16)

                def batch(b, last):
                    put_negmax(b, 1)
                    if not last:
                        sp.wait_ge(s["maxed"], b * (2 * MAXES) + 2 * MAXES)
                        load_k(k_max, "kmax_in", b + 1)
                        load_q(b + 1, 0)
                        put_negmax(b + 1, 0)
                        load_q(b + 1, 1)
                        load_k(k_main, "kmain_in", b + 1)
                load_k(k_max, "kmax_in", 0)
                load_q(0, 0)
                load_k(k_main, "kmain_in", 0)
                load_q(0, 1)
                sp.wait_ge(s["pads"], 4)
                put_negmax(0, 0)
                with sp.Fori(0, B - 1) as b:
                    batch(b, False)
                batch(B - 1, True)

            @block.tensor
            def _(pe):
                def maximum(b, h, m):
                    count = b * (2 * MAXES) + h * MAXES + m
                    if m == 0:
                        pe.wait_ge(s[f"q_in{h}"], b * 64 + 64)
                        if h == 0:
                            pe.wait_ge(s["kmax_in"], b * 64 + 64)
                    ge(pe, s["maxed"], count - 1)
                    if m == 0:
                        ge(pe, s["t_low"], b * 2 + h)
                    head, qt = m // QT, m % QT
                    for half in range(2):
                        last = nc.tensor.matmul(mx_ps[m % 2][:, half * 512:(half + 1) * 512],
                                                q_stack[h][0:ROWS, head, qt * P:(qt + 1) * P],
                                                k_max[:, head // GROUPS, half * 512:(half + 1) * 512],
                                                start=True, stop=True)
                    last.then_inc(s["max_scored"], 1)

                def turn_maxima(b, h):
                    pe.wait_ge(s["maxed"], b * (2 * MAXES) + (h + 1) * MAXES)
                    for qt in range(QT):
                        last = nc.tensor.transpose(mx_ps[0][0:HEADS, qt * P:(qt + 1) * P], negmax[h][:, qt, :],
                                                   core.ident[:, :])
                    last.then_inc(s["turned"], 1)

                def weigh(b, h, step):
                    kv, kt = step // KT, step % KT
                    n0 = b * (2 * 4 * STEPS) + h * (4 * STEPS) + 4 * step
                    if step == 0 and h == 0:
                        pe.wait_ge(s["v_in"], b + 1)
                    if kt == 0:
                        ge(pe, s["o_kept"], b * (2 * NKV) + h * NKV + kv)
                    for g in range(GROUPS):
                        pe.wait_ge(s["expd"], n0 + (g + 1))
                        last = nc.tensor.matmul(o_ps[32 * g:32 * g + 32, :], v_now[:, kt, kv, :],
                                                probs[(4 * step + g) % 8][:, :], start=(kt == 0), stop=(kt == KT - 1),
                                                tile_position=(0, 32 * g))
                    last.then_inc(s["weighted"], 1)

                def unit(b, h, last_unit):
                    nb, nh = (b, 1) if h == 0 else (b + 1, 0)
                    pe.wait_ge(s[f"neg_in{h}"], b * 16 + 16)
                    if h == 0:
                        pe.wait_ge(s["kmain_in"], b * 64 + 64)
                    for step in range(STEPS):
                        kv, kt = step // KT, step % KT
                        for g in range(GROUPS):
                            n = 4 * step + g
                            count = b * (2 * 4 * STEPS) + h * (4 * STEPS) + n
                            ge(pe, s["expd"], count - (1 if n < 2 else 2))
                            nc.tensor.matmul(st_ps[n % 3][:, :],
                                             k_main[:, kv, kt * P:(kt + 1) * P],
                                             q_stack[h][:, kv * GROUPS + g, :], start=True, stop=True)\
                                .then_inc(s["scored"], 1)
                        if step >= 1:
                            weigh(b, h, step - 1)
                        if not last_unit:
                            for m in max_steps(step):
                                maximum(nb, nh, m)
                            if step == END:
                                turn_maxima(nb, nh)
                    weigh(b, h, STEPS - 1)

                pe.wait_ge(s["pads"], 4)
                for m in range(MAXES):
                    maximum(0, 0, m)
                turn_maxima(0, 0)

                def batch(b, last):
                    unit(b, 0, False)
                    unit(b, 1, last)
                batch(0, False)
                with pe.Fori(1, B - 1) as b:
                    batch(b, False)
                batch(B - 1, True)

            @block.scalar
            def _(act):
                def unit(b, h):
                    for step in range(STEPS):
                        for g in range(GROUPS):
                            n = 4 * step + g
                            count = b * (2 * 4 * STEPS) + h * (4 * STEPS) + n
                            act.wait_ge(s["scored"], count + 1)
                            if g == 0:
                                ge(act, s["weighted"], b * (2 * STEPS) + h * STEPS + step - 1)
                            nc.scalar.activation(probs[n % 8][:, :], st_ps[n % 3][:, :], ACT.Exp, scale=0.25)\
                                .then_inc(s["expd"], 1)

                def batch(b):
                    unit(b, 0)
                    unit(b, 1)
                batch(0)
                with act.Fori(1, B) as b:
                    batch(b)

            @block.vector
            def _(dve):
                def maximum(b, h, m):
                    dve.wait_ge(s["max_scored"], b * (2 * MAXES) + h * MAXES + (m + 1))
                    nc.vector.tensor_reduce(negmax[h][:, m % QT, m // QT:m // QT + 1], mx_ps[m % 2][:, :], AX.X,
                                            ALU.max, negate=True).then_inc(s["maxed"], 1)

                def maxima_parts(b, h):
                    unit = b * 2 + h
                    dve.wait_ge(s["turned"], unit + 1)
                    ge(dve, s["neg_out"], unit * 32)
                    nc.vector.tensor_copy(turned_high[:, :], mx_ps[0][0:HEADS, 0:QU]).then_inc(s["t_high"], 1)
                    dve.wait_ge(s["t_high"], unit + 1)
                    nc.vector.tensor_tensor(turned_low[:, :], mx_ps[0][0:HEADS, 0:QU],
                                            turned_high[:, :].bitcast(F32), ALU.subtract).then_inc(s["t_low"], 1)

                def keep_o(b, h, kv):
                    done = b * (2 * NKV) + h * NKV + kv
                    dve.wait_ge(s["weighted"], b * (2 * STEPS) + h * STEPS + (kv + 1) * KT)
                    ge(dve, s[f"o_out{kv % 2}"], (b * NKV + h * (NKV // 2) + kv // 2) * 16)
                    nc.vector.tensor_copy(o_sb[kv % 2][:, :], o_ps[:, :]).then_inc(s["o_kept"], 1)

                def unit(b, h, last_unit):
                    nb, nh = (b, 1) if h == 0 else (b + 1, 0)
                    for step in range(STEPS):
                        if step >= 1 and step % KT == 0:
                            keep_o(b, h, step // KT - 1)
                        if not last_unit:
                            for m in max_steps(step):
                                maximum(nb, nh, m)
                            if step == END:
                                maxima_parts(nb, nh)
                    keep_o(b, h, NKV - 1)

                for m in range(MAXES):
                    maximum(0, 0, m)
                maxima_parts(0, 0)

                def batch(b, last):
                    unit(b, 0, False)
                    unit(b, 1, last)
                batch(0, False)
                with dve.Fori(1, B - 1) as b:
                    batch(b, False)
                batch(B - 1, True)


def attention_normalised(core, o_dram):
    nc = core.nc
    U = 2 * B
    with Phase(nc, "an") as ph:
        o_in = [ph.sb(f"o_in{j}", [P, 512]) for j in range(2)]
        recip = [ph.sb(f"recip{j}", [P, 4, GROUPS]) for j in range(2)]
        turn_ps = [ph.ps() for j in range(2)]
        loaded = [ph.sem("loaded0"), ph.sem("loaded1")]
        s = {n: ph.sem(n) for n in ("turned", "recip_done", "done")}
        with ph.block() as block:
            @block.sync
            def _(sp):
                def unit(u, _):
                    for kv in range(NKV):
                        ge(sp, s["turned"], u * NKV + (kv - 1))
                        sp.dma_start(o_in[kv % 2][:, :], o_dram[u, kv, :, :]).then_inc(loaded[kv % 2], 16)
                tiles(sp, U, 1, unit)

            @block.tensor
            def _(pe):
                def unit(u, _):
                    for kv in range(NKV):
                        pe.wait_ge(loaded[kv % 2], u * 32 + (kv // 2 + 1) * 16)
                        ge(pe, s["done"], u * NKV + (kv - 1))
                        for qt in range(4):
                            last = nc.tensor.transpose(turn_ps[kv % 2][:, qt * P:(qt + 1) * P],
                                                       o_in[kv % 2][:, qt * P:(qt + 1) * P], core.ident[:, :])
                        last.then_inc(s["turned"], 1)
                tiles(pe, U, 1, unit)

            @block.vector
            def _(dve):
                def unit(u, _):
                    for kv in range(NKV):
                        dve.wait_ge(s["turned"], u * NKV + (kv + 1))
                        ps = turn_ps[kv % 2][:, :].rearrange("p (q g c) -> p q g c", q=4, g=GROUPS)
                        nc.vector.reciprocal(recip[kv % 2][:, :, :], ps[:, :, :, DH]).then_inc(s["recip_done"], 1)
                        dve.wait_ge(s["recip_done"], u * NKV + (kv + 1))
                        nc.vector.tensor_tensor(
                            core.y[:, bass.ds(u * 4, 4), kv * 64:(kv + 1) * 64]
                            .rearrange("p q (g d) -> p q g d", g=GROUPS),
                            ps[:, :, :, 0:DH], recip[kv % 2][:, :, :].unsqueeze(3).to_broadcast([P, 4, GROUPS, DH]),
                            ALU.mult).then_inc(s["done"], 1)
                tiles(dve, U, 1, unit)
                dve.wait_ge(s["done"], U * NKV)


F16 = mybir.dt.float16
E = 8
SLOT_TILES = 2 * T + E
W_SCALE = 64.0
H_SCALE = 16.0


def split_scaled(core, name, parts):
    nc = core.nc
    with Phase(nc, name) as ph:
        stage = ph.sb("stage", [P, 2, 2048])
        loaded = [ph.sem("loaded0"), ph.sem("loaded1")]
        high_done, low_done = ph.sem("high_done"), ph.sem("low_done")

        def staged(i):
            src = parts[i][0]
            flat = stage[0:src.shape[0], i % 2, 0:src.shape[1] * (src.shape[2] if len(src.shape) == 3 else 1)]
            return flat.rearrange("p (k f) -> p k f", k=src.shape[1]) if len(src.shape) == 3 else flat

        with ph.block() as block:
            @block.sync
            def _(sp):
                for i, (src, _, _) in enumerate(parts):
                    ge(sp, low_done, i - 1)
                    sp.dma_start(staged(i), src).then_inc(loaded[i % 2], 16)

            @block.scalar
            def _(act):
                for i, (_, high, _) in enumerate(parts):
                    act.wait_ge(loaded[i % 2], 16 * (i // 2 + 1))
                    nc.scalar.activation(high, staged(i), ACT.Copy, scale=W_SCALE).then_inc(high_done, 1)

            @block.vector
            def _(dve):
                for i, (_, high, low) in enumerate(parts):
                    dve.wait_ge(high_done, i + 1)
                    nc.vector.scalar_tensor_tensor(out=low, in0=staged(i), scalar=W_SCALE, in1=high,
                                                   op0=ALU.mult, op1=ALU.subtract).then_inc(low_done, 1)


class Weights:

    def __init__(self, ph, n, F):
        self.n, self.F, self.KF = n, F, -(-F // P)
        self.up = [ph.sb(f"up_{x}", [P, n, KD, 2 * F], F16) for x in ("high", "low")]
        self.down = [ph.sb(f"down_{x}", [P, n, self.KF, D], F16) for x in ("high", "low")]

    def rows(self, k):
        return min(P, self.F - k * P)

    def parts(self, up_dram, down_dram):
        F = self.F
        out = []
        for e in range(self.n):
            up = up_dram[e, :, :].rearrange("(k p) f -> p k f", p=P)
            out.append((up, self.up[0][:, e, :, :], self.up[1][:, e, :, :]))
            whole = F // P
            out.append((down_dram[e, 0:whole * P, :].rearrange("(k p) d -> p k d", p=P),
                        self.down[0][:, e, 0:whole, :], self.down[1][:, e, 0:whole, :]))
            if F % P:
                r = F % P
                out.append((down_dram[e, whole * P:F, :], self.down[0][0:r, e, whole, :],
                            self.down[1][0:r, e, whole, :]))
        return out


def feed_forward(core, name, n, w, shared, router=None, logits=None, x_rows=None, y_rows=None, expert_of=None):
    nc = core.nc
    F, KF = w.F, w.KF
    with Phase(nc, name) as ph:
        x_in = [ph.sb(f"x_in{j}", [P, D]) for j in range(2)]
        xt = [[ph.sb(f"xt_{x}{j}", [P, KD, P], F16) for x in ("high", "low")] for j in range(2)]
        gate = [ph.sb(f"gate{j}", [P, F]) for j in range(2)]
        hidden = [ph.sb(f"hidden{j}", [P, F]) for j in range(2)]
        ht = [[ph.sb(f"ht_{x}{j}", [P, KF, P], F16) for x in ("high", "low")] for j in range(2)]
        y_sb = None if shared else [ph.sb(f"y_sb{j}", [P, D]) for j in range(2)]
        xt_ps = ph.ps()
        lin_ps = [ph.ps() for j in range(2)]
        gate_ps = ph.ps()
        ht_ps = ph.ps()
        y_ps = [ph.ps() for j in range(2)]
        logit_ps = ph.ps() if shared else None
        s = {k: ph.sem(k) for k in ("x_ready", "x_turned", "xt_high", "xt_low", "gated", "lined", "silu_done",
                                    "hidden_done", "h_turned", "ht_high", "ht_low", "downed", "y_done", "logged",
                                    "kept")}
        x_loaded = [ph.sem("x_loaded0"), ph.sem("x_loaded1")]
        y_stored = [ph.sem("y_stored0"), ph.sem("y_stored1")]

        def blocks(ap):
            return ap.rearrange("p (k t) -> p k t", t=P)

        pieces = [(slice(0, F // P), P)] if F >= P else []
        if F % P:
            pieces.append((slice(F // P, KF), F % P))

        with ph.block() as block:
            @block.sync
            def _(sp):
                if shared:
                    return

                def load(i, j):
                    ge(sp, s["x_turned"], i - 1)
                    sp.dma_start(x_in[j][:, :], x_rows[i, :, :]).then_inc(x_loaded[j], 16)

                tiles(sp, n, 2, load)

            @block.gpsimd
            def _(pool):
                if shared:
                    return

                def store(i, j):
                    pool.wait_ge(s["y_done"], i + 1)
                    pool.dma_start(y_rows[i, :, :], y_sb[j][:, :]).then_inc(y_stored[j], 16)

                tiles(pool, n, 2, store)
                for j in range(2):
                    pool.wait_ge(y_stored[j], n // 2 * 16)

            @block.scalar
            def _(act):
                def high(i, j):
                    act.wait_ge(s["x_turned"], i + 1)
                    ge(act, s["lined"], i - 1)
                    nc.scalar.activation(xt[j][0][:, :, :], blocks(xt_ps[:, 0:D]), ACT.Copy).then_inc(s["xt_high"], 1)

                def silu(i, j):
                    act.wait_ge(s["gated"], i + 1)
                    ge(act, s["hidden_done"], i - 1)
                    nc.scalar.activation(gate[j][:, :], gate_ps[:, 0:F], ACT.Silu, scale=1.0 / W_SCALE)\
                        .then_inc(s["silu_done"], 1)

                def hidden_high(i, j):
                    act.wait_ge(s["h_turned"], i + 1)
                    ge(act, s["downed"], i - 1)
                    for at, rows in pieces:
                        last = nc.scalar.activation(ht[j][0][0:rows, at, :], blocks(ht_ps[0:rows, 0:KF * P])[:, at, :],
                                                    ACT.Copy)
                    last.then_inc(s["ht_high"], 1)

                def step(i, j, first=False, more=True):
                    silu(i, j)
                    if more:
                        high(i + 1, 1 - j)
                    if not first:
                        hidden_high(i - 1, 1 - j)
                high(0, 0)
                step(0, 0, first=True)
                for i in range(1, 4):
                    step(i, i % 2)
                with act.Fori(2, n // 2 - 1) as k:
                    step(k * 2, 0)
                    step(k * 2 + 1, 1)
                step(n - 2, 0)
                step(n - 1, 1, more=False)
                hidden_high(n - 1, 1)

            @block.vector
            def _(dve):
                def norm(i, j):
                    if shared:
                        ge(dve, s["x_turned"], i - 1)
                        nc.vector.tensor_scalar(x_in[j][:, :], core.x[:, i, :], core.mean_var[:, i, 0:1],
                                                core.rstd[:, bass.ds(i, 1)], ALU.subtract, ALU.mult)\
                            .then_inc(s["x_ready"], 1)

                def low(i, j):
                    dve.wait_ge(s["xt_high"], i + 1)
                    ge(dve, s["lined"], i - 1)
                    nc.vector.tensor_tensor(xt[j][1][:, :, :], blocks(xt_ps[:, 0:D]), xt[j][0][:, :, :],
                                            ALU.subtract).then_inc(s["xt_low"], 1)

                def multiply(i, j):
                    dve.wait_ge(s["lined"], i + 1)
                    dve.wait_ge(s["silu_done"], i + 1)
                    ge(dve, s["h_turned"], i - 1)
                    nc.vector.scalar_tensor_tensor(out=hidden[j][:, :], in0=lin_ps[j][:, 0:F], scalar=H_SCALE / W_SCALE,
                                                   in1=gate[j][:, :], op0=ALU.mult, op1=ALU.mult)\
                        .then_inc(s["hidden_done"], 1)

                def hidden_low(i, j):
                    dve.wait_ge(s["ht_high"], i + 1)
                    ge(dve, s["downed"], i - 1)
                    for at, rows in pieces:
                        last = nc.vector.tensor_tensor(ht[j][1][0:rows, at, :], blocks(ht_ps[0:rows, 0:KF * P])[:, at, :],
                                                       ht[j][0][0:rows, at, :], ALU.subtract)
                    last.then_inc(s["ht_low"], 1)

                def finish(i, j):
                    dve.wait_ge(s["downed"], i + 1)
                    if shared:
                        out = core.y[:, i, :]
                    else:
                        ge(dve, y_stored[j], (i // 2 if isinstance(i, int) else half_of["i"]) * 16)
                        out = y_sb[j][:, :]
                    nc.vector.tensor_scalar(out, y_ps[j][:, 0:D], 1.0 / (H_SCALE * W_SCALE), None, ALU.mult)\
                        .then_inc(s["y_done"], 1)
                half_of = {}

                def step(i, j, first=False, more=True):
                    if more:
                        norm(i + 1, 1 - j)
                    multiply(i, j)
                    if more:
                        low(i + 1, 1 - j)
                    if not first:
                        hidden_low(i - 1, 1 - j)
                        finish(i - 1, 1 - j)
                norm(0, 0)
                low(0, 0)
                step(0, 0, first=True)
                for i in range(1, 4):
                    step(i, i % 2)
                with dve.Fori(2, n // 2 - 1) as k:
                    half_of["i"] = k - 1
                    step(k * 2, 0)
                    half_of["i"] = k
                    step(k * 2 + 1, 1)
                step(n - 2, 0)
                step(n - 1, 1, more=False)
                hidden_low(n - 1, 1)
                finish(n - 1, 1)
                if shared:
                    dve.wait_ge(s["logged"], n)
                    nc.vector.tensor_copy(logits[:, :, :], logit_ps[:, 0:n * E].rearrange("p (t e) -> p t e", e=E))\
                        .then_inc(s["kept"], 1)
                dve.wait_ge(s["y_done"], n)

            @block.tensor
            def _(pe):
                def turn(i, j):
                    if shared:
                        pe.wait_ge(s["x_ready"], i + 1)
                    else:
                        pe.wait_ge(x_loaded[j], (i // 2 + 1 if isinstance(i, int) else load_of["i"]) * 16)
                    ge(pe, s["xt_low"], i)
                    for k in range(KD):
                        last = nc.tensor.transpose(xt_ps[:, k * P:(k + 1) * P], x_in[j][:, k * P:(k + 1) * P],
                                                   core.ident[:, :])
                    last.then_inc(s["x_turned"], 1)
                load_of = {}

                def three(out, left, right, stop_at):
                    m = 0
                    for k in range(stop_at):
                        for a, b in ((0, 0), (1, 0), (0, 1)):
                            m += 1
                            last = nc.tensor.matmul(out, left(a, k), right(b, k), start=(m == 1), stop=(m == 3 * stop_at))
                    return last

                def expert(i):
                    if shared:
                        return 0
                    return pe.value_load(expert_of[0:1, bass.ds(i, 1)], min_val=0, max_val=E - 1)

                def gate_up(i, j, e):
                    pe.wait_ge(s["xt_low"], i + 1)
                    ge(pe, s["silu_done"], i)
                    three(gate_ps[:, 0:F], lambda a, k: xt[j][a][:, k, :],
                          lambda b, k: w.up[b][:, e, k, F:2 * F], KD).then_inc(s["gated"], 1)

                def line_up(i, j, e):
                    ge(pe, s["hidden_done"], i - 1)
                    if shared:
                        m = 0
                        for k in range(KD):
                            for a in range(2):
                                for b in range(2):
                                    m += 1
                                    last = nc.tensor.matmul(logit_ps[:, bass.ds(i * E, E)], xt[j][a][:, k, :],
                                                            router[b][:, k, :], start=(m == 1), stop=(m == 4 * KD))
                        last.then_inc(s["logged"], 1)
                    three(lin_ps[j][:, 0:F], lambda a, k: xt[j][a][:, k, :],
                          lambda b, k: w.up[b][:, e, k, 0:F], KD).then_inc(s["lined"], 1)

                def turn_hidden(i, j):
                    pe.wait_ge(s["hidden_done"], i + 1)
                    ge(pe, s["ht_low"], i)
                    for k in range(KF):
                        last = nc.tensor.transpose(ht_ps[0:w.rows(k), k * P:(k + 1) * P],
                                                   hidden[j][:, k * P:k * P + w.rows(k)], core.ident[:, :])
                    last.then_inc(s["h_turned"], 1)

                def down(i, j, e):
                    pe.wait_ge(s["ht_low"], i + 1)
                    ge(pe, s["y_done"], i - 1)
                    three(y_ps[j][:, 0:D], lambda a, k: ht[j][a][0:w.rows(k), k, :],
                          lambda b, k: w.down[b][0:w.rows(k), e, k, :], KF).then_inc(s["downed"], 1)

                def step(i, j, first=False, more=True):
                    e = expert(i)
                    gate_up(i, j, e)
                    if not first:
                        turn_hidden(i - 1, 1 - j)
                    line_up(i, j, e)
                    if more:
                        turn(i + 1, 1 - j)
                    if not first:
                        down(i - 1, 1 - j, expert(i - 1))
                turn(0, 0)
                step(0, 0, first=True)
                for i in range(1, 4):
                    step(i, i % 2)
                with pe.Fori(2, n // 2 - 1) as k:
                    load_of["i"] = k + 1
                    step(k * 2, 0)
                    load_of["i"] = k + 2
                    step(k * 2 + 1, 1)
                step(n - 2, 0)
                step(n - 1, 1, more=False)
                turn_hidden(n - 1, 1)
                down(n - 1, 1, expert(n - 1))


class Routing:

    def __init__(self, ph):
        self.logits = ph.sb("logits", [P, T, E])
        self.slots = ph.sb("slots", [P, T, 2], I32)
        self.weights = ph.sb("weights", [P, T, 2])
        self.expert_of = ph.sb("expert_of", [P, SLOT_TILES], I32)


def zero_rows(core, rows):
    nc = core.nc
    per = SLOT_TILES
    with Phase(nc, "zr") as ph:
        zeros = ph.sb("zeros", [P, 8 * D])
        cleared, stored = ph.sem("cleared"), ph.sem("stored")
        flat = rows.rearrange("j p d -> (j p) d").rearrange("(p r) d -> p (r d)", p=P)
        with ph.block() as block:
            @block.vector
            def _(dve):
                nc.vector.memset(zeros[:, :], 0.0).then_inc(cleared, 1)

            @block.sync
            def _(sp):
                sp.wait_ge(cleared, 1)
                for r in range(0, per, 8):
                    sp.dma_start(flat[:, r * D:(r + 8) * D], zeros[:, :]).then_inc(stored, 16)
                sp.wait_ge(stored, per // 8 * 16)


def route(core, name, r, normalise, bias_row):
    nc = core.nc
    with Phase(nc, name) as ph:
        bias = ph.sb("bias", [P, E])
        top = ph.sb("top", [P, T, 8])
        index = ph.sb("index", [P, T, 8], mybir.dt.uint32)
        index_f = ph.sb("index_f", [P, T, 2])
        expert_iota = ph.sb("expert_iota", [P, E])
        tile_iota = ph.sb("tile_iota", [P, SLOT_TILES])
        chosen = [ph.sb(f"chosen{c}", [P, T, E]) for c in range(2)]
        both = ph.sb("both", [P, T, E])
        before = ph.sb("before", [P, P])
        ones = ph.sb("ones", [P, P])
        total = ph.sb("total", [P, T, E])
        running = ph.sb("running", [P, T, E])
        count_i = ph.sb("count_i", [P, E], I32)
        n_tiles = ph.sb("n_tiles", [P, E])
        ends = ph.sb("ends", [P, E])
        starts = ph.sb("starts", [P, E])
        slot = ph.sb("slot", [P, T, E])
        picked = ph.sb("picked", [P, T, E])
        slot_f = ph.sb("slot_f", [P, T, 2])
        passed = ph.sb("passed", [P, SLOT_TILES, E])
        expert_f = ph.sb("expert_f", [P, SLOT_TILES])
        shifted = ph.sb("shifted", [P, T, E])
        expd = ph.sb("expd", [P, T, E])
        denom = ph.sb("denom", [P, T, E])
        sums = ph.sb("sums", [P, T])
        rank_ps, total_ps = ph.ps(), ph.ps()
        bias_in, masks, counted = ph.sem("bias_in"), ph.sem("masks"), ph.sem("counted")
        chain, exp_ready, exp_done, both_done = ph.sem("chain"), ph.sem("exp_ready"), ph.sem("exp_done"), ph.sem("both")

        with ph.block() as block:
            @block.sync
            def _(sp):
                if bias_row is not None:
                    sp.dma_start(bias[:, :], bias_row.to_broadcast([P, E])).then_inc(bias_in, 16)

            @block.gpsimd
            def _(pool):
                nc.gpsimd.memset(ones[:, :], 1.0).then_inc(masks, 1)
                nc.gpsimd.memset(before[:, :], 1.0).then_inc(masks, 1)
                nc.gpsimd.iota(expert_iota[:, :], pattern=[[1, E]], base=0, channel_multiplier=0,
                               allow_small_or_imprecise_dtypes=True).then_inc(masks, 1)
                nc.gpsimd.iota(tile_iota[:, :], pattern=[[1, SLOT_TILES]], base=0, channel_multiplier=0,
                               allow_small_or_imprecise_dtypes=True).then_inc(masks, 1)
                pool.wait_ge(masks, 4)
                nc.gpsimd.affine_select(out=before[:, :], in_=before[:, :], compare_op=ALU.is_gt, fill=0.0, base=0,
                                        pattern=[[1, P]], channel_multiplier=-1).then_inc(masks, 1)

            @block.tensor
            def _(pe):
                pe.wait_ge(masks, 5)
                pe.wait_ge(both_done, 1)
                flat = both[:, :, :].rearrange("p t e -> p (t e)")
                nc.tensor.matmul(rank_ps[:, 0:T * E], before[:, :], flat, start=True, stop=True)
                nc.tensor.matmul(total_ps[:, 0:T * E], ones[:, :], flat, start=True, stop=True).then_inc(counted, 1)

            @block.scalar
            def _(act):
                act.wait_ge(exp_ready, 1)
                nc.scalar.activation(expd[:, :, :], shifted[:, :, :], ACT.Exp).then_inc(exp_done, 1)

            @block.vector
            def _(dve):
                steps = [0]

                def then(ins):
                    steps[0] += 1
                    ins.then_inc(chain, 1)
                    dve.wait_ge(chain, steps[0])

                dve.wait_ge(masks, 5)
                if bias_row is not None:
                    dve.wait_ge(bias_in, 16)
                    then(nc.vector.tensor_tensor(r.logits[:, :, :], r.logits[:, :, :],
                                                 bias[:, :].unsqueeze(1).to_broadcast([P, T, E]), ALU.add))
                for t in range(T):
                    last = nc.vector.max(top[:, t, :], r.logits[:, t, :])
                then(last)
                for t in range(T):
                    last = nc.vector.max_index(index[:, t, :], top[:, t, :], r.logits[:, t, :])
                then(last)
                then(nc.vector.tensor_copy(index_f[:, :, :], index[:, :, 0:2]))
                for c in range(2):
                    last = nc.vector.tensor_tensor(chosen[c][:, :, :],
                                                   expert_iota[:, :].unsqueeze(1).to_broadcast([P, T, E]),
                                                   index_f[:, :, c:c + 1].to_broadcast([P, T, E]), ALU.is_equal)
                then(last)
                nc.vector.tensor_tensor(both[:, :, :], chosen[0][:, :, :], chosen[1][:, :, :], ALU.add)\
                    .then_inc(both_done, 1)

                if normalise:
                    nc.vector.tensor_scalar(shifted[:, :, :], top[:, :, :], -1.0, None, ALU.mult).then_inc(exp_ready, 1)
                    dve.wait_ge(exp_done, 1)
                    then(nc.vector.tensor_scalar(denom[:, :, 0:2], expd[:, :, 0:2], 1.0, None, ALU.add))
                    then(nc.vector.reciprocal(r.weights[:, :, :], denom[:, :, 0:2]))
                    then(nc.vector.tensor_tensor(sums[:, :], r.weights[:, :, 0], r.weights[:, :, 1], ALU.add))
                    then(nc.vector.reciprocal(sums[:, :], sums[:, :]))
                    then(nc.vector.tensor_tensor(r.weights[:, :, :], r.weights[:, :, :],
                                                 sums[:, :].unsqueeze(2).to_broadcast([P, T, 2]), ALU.mult))
                else:
                    nc.vector.tensor_tensor(shifted[:, :, :], top[:, :, :], top[:, :, 0:1].to_broadcast([P, T, E]),
                                            ALU.subtract).then_inc(exp_ready, 1)
                    dve.wait_ge(exp_done, 1)
                    then(nc.vector.tensor_reduce(sums[:, :], expd[:, :, :], AX.X, ALU.add))
                    then(nc.vector.reciprocal(sums[:, :], sums[:, :]))
                    then(nc.vector.tensor_tensor(r.weights[:, :, :], expd[:, :, 0:2],
                                                 sums[:, :].unsqueeze(2).to_broadcast([P, T, 2]), ALU.mult))

                dve.wait_ge(counted, 1)
                then(nc.vector.tensor_copy(total[:, :, :], total_ps[:, 0:T * E].rearrange("p (t e) -> p t e", e=E)))
                for e in range(E):
                    last = nc.vector.tensor_tensor_scan(running[:, :, e], ones[:, 0:T], total[:, :, e], 0.0,
                                                        ALU.mult, ALU.add)
                then(last)
                then(nc.vector.tensor_scalar(count_i[:, :], running[:, T - 1, :], float(P - 1), None, ALU.add))
                then(nc.vector.tensor_scalar(count_i[:, :], count_i[:, :], P.bit_length() - 1, None,
                                             ALU.arith_shift_right))
                then(nc.vector.tensor_copy(n_tiles[:, :], count_i[:, :]))
                then(nc.vector.tensor_tensor_scan(ends[:, :], ones[:, 0:E], n_tiles[:, :], 0.0, ALU.mult, ALU.add))
                then(nc.vector.tensor_tensor(starts[:, :], ends[:, :], n_tiles[:, :], ALU.subtract))
                then(nc.vector.tensor_tensor(slot[:, :, :], running[:, :, :], total[:, :, :], ALU.subtract))
                then(nc.vector.tensor_tensor(slot[:, :, :], rank_ps[:, 0:T * E].rearrange("p (t e) -> p t e", e=E),
                                             slot[:, :, :], ALU.add))
                then(nc.vector.tensor_scalar(starts[:, :], starts[:, :], float(P), None, ALU.mult))
                then(nc.vector.tensor_tensor(slot[:, :, :], slot[:, :, :],
                                             starts[:, :].unsqueeze(1).to_broadcast([P, T, E]), ALU.add))
                for c in range(2):
                    then(nc.vector.tensor_tensor(picked[:, :, :], chosen[c][:, :, :], slot[:, :, :], ALU.mult))
                    then(nc.vector.tensor_reduce(slot_f[:, :, c], picked[:, :, :], AX.X, ALU.add))
                then(nc.vector.tensor_copy(r.slots[:, :, :], slot_f[:, :, :]))
                then(nc.vector.tensor_tensor(passed[:, :, :], ends[:, :].unsqueeze(1).to_broadcast([P, SLOT_TILES, E]),
                                             tile_iota[:, :].unsqueeze(2).to_broadcast([P, SLOT_TILES, E]), ALU.is_le))
                then(nc.vector.tensor_reduce(expert_f[:, :], passed[:, :, :], AX.X, ALU.add))
                then(nc.vector.tensor_scalar(r.expert_of[:, :], expert_f[:, :], float(E - 1), None, ALU.min))


def scatter_rows(core, name, r, x_rows):
    nc = core.nc
    rows = x_rows.rearrange("j p d -> (j p) d")
    with Phase(nc, name) as ph:
        xhat = [ph.sb(f"xhat{j}", [P, D]) for j in range(4)]
        ready = ph.sem("ready")
        sent = [ph.sem(f"sent{j}") for j in range(4)]
        with ph.block() as block:
            @block.vector
            def _(dve):
                def group(k):
                    for j in range(4):
                        i = k * 4 + j
                        ge(dve, sent[j], k * 32)
                        nc.vector.tensor_scalar(xhat[j][:, :], core.x[:, i, :], core.mean_var[:, i, 0:1],
                                                core.rstd[:, bass.ds(i, 1)], ALU.subtract, ALU.mult)\
                            .then_inc(ready, 1)
                tiles(dve, T // 4, 1, lambda k, _: group(k))

            @block.gpsimd
            def _(pool):
                for i in range(T):
                    pool.wait_ge(ready, i + 1)
                    for c in range(2):
                        pool.indirect_dma_start(rows, bass.IndirectOffsetOnAxis(ap=r.slots[:, i, c:c + 1], axis=0),
                                                xhat[i % 4][:, :], None).then_inc(sent[i % 4], 16)
                for j in range(4):
                    pool.wait_ge(sent[j], T // 4 * 32)


def gather_rows(core, name, r, y_rows):
    nc = core.nc
    rows = y_rows.rearrange("j p d -> (j p) d")
    with Phase(nc, name) as ph:
        got = [[ph.sb(f"got{j}{c}", [P, D]) for c in range(2)] for j in range(4)]
        first_added, added = ph.sem("first_added"), ph.sem("added")
        came = [ph.sem(f"came{j}") for j in range(4)]
        with ph.block() as block:
            @block.gpsimd
            def _(pool):
                for i in range(T):
                    ge(pool, added, i - 3)
                    for c in range(2):
                        pool.indirect_dma_start(got[i % 4][c][:, :], None, rows,
                                                bass.IndirectOffsetOnAxis(ap=r.slots[:, i, c:c + 1], axis=0))\
                            .then_inc(came[i % 4], 16)

            @block.vector
            def _(dve):
                def group(k):
                    for j in range(4):
                        i = k * 4 + j
                        dve.wait_ge(came[j], k * 32 + 32)
                        nc.vector.scalar_tensor_tensor(out=core.y[:, i, :], in0=got[j][0][:, :],
                                                       scalar=r.weights[:, i, 0:1], in1=core.y[:, i, :],
                                                       op0=ALU.mult, op1=ALU.add).then_inc(first_added, 1)
                        dve.wait_ge(first_added, i + 1)
                        nc.vector.scalar_tensor_tensor(out=core.y[:, i, :], in0=got[j][1][:, :],
                                                       scalar=r.weights[:, i, 1:2], in1=core.y[:, i, :],
                                                       op0=ALU.mult, op1=ALU.add).then_inc(added, 1)
                tiles(dve, T // 4, 1, lambda k, _: group(k))
                dve.wait_ge(added, T)


def mixture(core, nc, name, F, shared_F, normalise, router_dram, bias_row, up_s, down_s, up_r, down_r, x_rows, y_rows):
    with Phase(nc, name) as ph:
        r = Routing(ph)
        with Phase(nc, name + "s") as ps:
            w = Weights(ps, 1, shared_F)
            router = [ps.sb(f"router_{x}", [P, KD, E], F16) for x in ("high", "low")]
            split_scaled(core, name + "ws", w.parts(up_s, down_s) +
                         [(router_dram.rearrange("(k p) e -> p k e", p=P), router[0][:, :, :], router[1][:, :, :])])
            feed_forward(core, name + "fs", T, w, True, router=router, logits=r.logits)
        unscale_logits(core, name + "u", r)
        route(core, name + "r", r, normalise, bias_row)
        scatter_rows(core, name + "sc", r, x_rows)
        with Phase(nc, name + "x") as px:
            w = Weights(px, E, F)
            split_scaled(core, name + "wx", w.parts(up_r, down_r))
            feed_forward(core, name + "fx", SLOT_TILES, w, False, x_rows=x_rows, y_rows=y_rows, expert_of=r.expert_of)
        gather_rows(core, name + "g", r, y_rows)


def unscale_logits(core, name, r):
    nc = core.nc
    with Phase(nc, name) as ph:
        done = ph.sem("done")
        with ph.block() as block:
            @block.vector
            def _(dve):
                nc.vector.tensor_scalar(r.logits[:, :, :], r.logits[:, :, :], 1.0 / W_SCALE, None, ALU.mult)\
                    .then_inc(done, 1)
                dve.wait_ge(done, 1)


def build(nc, a, out):
    ctx = ExitStack()
    with ctx:
        Phase.taken_semaphores = []
        core = Core(nc, ctx)
        constants(core)
        x_dram = a["L0_attn_x"].rearrange("b (u p) d -> b p u d", p=P)
        out_dram = out.rearrange("b (u p) d -> b p u d", p=P)
        residual_and_stats(core, "in", x_dram=x_dram)
        with Phase(nc, "w0") as ph:
            qkv_high = ph.sb("qkv_high", [P, KD, 3 * D], F32R)
            qkv_low = ph.sb("qkv_low", [P, KD, 3 * D], F32R)
            wo_high = ph.sb("wo_high", [P, KD, D], F32R)
            wo_low = ph.sb("wo_low", [P, KD, D], F32R)
            parts = []
            for k in range(KD):
                parts.append((a["qkv0"][k * P:(k + 1) * P, :], qkv_high[:, k, :], qkv_low[:, k, :]))
                parts.append((a["L0_attn_wo"][k * P:(k + 1) * P, :], wo_high[:, k, :], wo_low[:, k, :]))
            split_weights(core, "w0s", parts)
            linear_attention(core, None, qkv_high, qkv_low, a["bias_qkv0"], core.y)
            output_projection(core, "wo0", wo_high, wo_low, a["bias_o0"])
        residual_and_stats(core, "r0")
        x_rows = nc.dram_tensor("x_rows", (SLOT_TILES, P, D), F32, kind="Internal").ap()
        y_rows = nc.dram_tensor("y_rows", (SLOT_TILES, P, D), F32, kind="Internal").ap()
        zero_rows(core, x_rows)
        mixture(core, nc, "m0", 512, 512, True, a["router0"], a["bias_r0"], a["up0s"], a["down0s"], a["up0"],
                a["down0"], x_rows, y_rows)
        residual_and_stats(core, "r1")
        Phase.clear_semaphores(nc)
        second_attention(core, nc, a)
        residual_and_stats(core, "r2")
        mixture(core, nc, "m1", 192, 384, False, a["router1"], None, a["up1s"], a["down1s"], a["up1"],
                a["down1"], x_rows, y_rows)
        residual_and_stats(core, "r3", out_dram=out_dram)


def second_attention(core, nc, a):
    q_dram = nc.dram_tensor("q_scratch", (2, D, B * N), F32, kind="Internal").ap()
    k_dram = nc.dram_tensor("k_scratch", (2, NKV * DH, B * N), F32, kind="Internal").ap()
    o_dram = nc.dram_tensor("o_scratch", (2 * B, NKV, P, N // 2), F32, kind="Internal").ap()
    negmax_dram = nc.dram_tensor("negmax_scratch", (2 * B, 2, HEADS, N // 2), F32, kind="Internal").ap()
    with Phase(nc, "v") as ph:
        v_all = ph.sb("v_all", [P, T, NKV, 32])
        with Phase(nc, "w2") as pw:
            high = pw.sb("high", [P, KD, 3 * P], F32R)
            low = pw.sb("low", [P, KD, 3 * P], F32R)
            split_weights(core, "w2s", [(a["qkv1"][k * P:(k + 1) * P, :], high[:, k, :], low[:, k, :])
                                        for k in range(KD)])
            attention_projections(core, high, low, a["bias_qkv1"], q_dram, k_dram, v_all)
        softmax_attention(core, q_dram, k_dram, v_all, negmax_dram,
                          o_dram.rearrange("(b h) k p t -> b h k p t", h=2))
    attention_normalised(core, o_dram)
    with Phase(nc, "w3") as pw:
        high = pw.sb("high", [P, KD, D], F32R)
        low = pw.sb("low", [P, KD, D], F32R)
        split_weights(core, "w3s", [(a["wo1"][k * P:(k + 1) * P, :], high[:, k, :], low[:, k, :])
                                    for k in range(KD)])
        output_projection(core, "wo1", high, low, a["bias_o1"])


def kernel(**inputs):
    import numpy as _np
    import concourse.bacc as _bacc
    from concourse import mybir as _mybir
    from concourse.bass_utils import run_bass_kernel_spmd as _run

    given = {k: _np.asarray(v) for k, v in inputs.items()}
    laid = {
        "L0_attn_x": given["L0_attn_x"],
        "qkv0": _np.concatenate([given["L0_attn_wq"], given["L0_attn_wk"], given["L0_attn_wv"]], axis=1),
        "bias_qkv0": _np.concatenate([given["L0_attn_bq"], given["L0_attn_bk"], given["L0_attn_bv"]])[None, :],
        "L0_attn_wo": given["L0_attn_wo"],
        "bias_o0": given["L0_attn_bo"][None, :],
        "qkv1": _np.concatenate([given["L1_attn_Wq"], given["L1_attn_Wk"], given["L1_attn_Wv"]], axis=1),
        "bias_qkv1": _np.concatenate([given["L1_attn_bq"], given["L1_attn_bk"], given["L1_attn_bv"]])
        .reshape(3, P).T,
        "wo1": given["L1_attn_Wo"].reshape(GROUPS, NKV, DH, D).transpose(1, 0, 2, 3).reshape(D, D),
        "bias_o1": given["L1_attn_bo"][None, :],
        "router0": given["L0_ffn_router_w"].T,
        "bias_r0": given["L0_ffn_routing_bias"][None, :],
        "up0s": _np.concatenate([given["L0_ffn_su_w"], given["L0_ffn_sg_w"]], axis=0).T[None],
        "down0s": given["L0_ffn_sd_w"].T[None],
        "up0": _np.concatenate([given["L0_ffn_wu"], given["L0_ffn_wg"]], axis=1).transpose(0, 2, 1),
        "down0": given["L0_ffn_wd"].transpose(0, 2, 1),
        "router1": given["L1_ffn_gate_w"].T,
        "up1s": given["L1_ffn_Ws1"].T[None],
        "down1s": given["L1_ffn_Ws2"].T[None],
        "up1": given["L1_ffn_W1"].transpose(0, 2, 1),
        "down1": given["L1_ffn_W2"].transpose(0, 2, 1),
    }
    nc = _bacc.Bacc("TRN2", target_bir_lowering=False, num_devices=1)
    arrays, args = {}, {}
    for name, v in laid.items():
        v = _np.ascontiguousarray(v)
        arrays[f"in_{name}"] = v
        args[name] = nc.dram_tensor(f"in_{name}", v.shape, _mybir.dt.from_np(v.dtype), kind="ExternalInput").ap()
    out = nc.dram_tensor("out_x", (B, N, D), _mybir.dt.float32, kind="ExternalOutput").ap()
    build(nc, args, out)
    return _run(nc, [arrays], core_ids=[0]).results[0]["out_x"]
```

```python
import concourse.bass as bass
from concourse import mybir
from contextlib import ExitStack

F32 = mybir.dt.float32
F32R = mybir.dt.float32r
BF16 = mybir.dt.bfloat16
I32 = mybir.dt.int32
ALU = mybir.AluOpType
ACT = mybir.ActivationFunctionType
AX = mybir.AxisListType

P = 128
B, N, D = 4, 1024, 256
T = B * N // P
TB = N // P
KD = D // P
EPS = 1e-5
HEADS, DH = 16, 16
HPB = P // DH
NKV, GROUPS = 4, 4


def ge(eng, sem, value):
    if not (isinstance(value, int) and value <= 0):
        eng.wait_ge(sem, value)


def tiles(eng, n, unroll, step):
    for u in range(unroll):
        step(u, u)
    if n > unroll:
        with eng.Fori(1, n // unroll) as k:
            for u in range(unroll):
                step(k * unroll + u, u)


class Core:

    def __init__(self, nc, ctx):
        self.nc = nc
        self.x = ctx.enter_context(nc.sbuf_tensor("x", [P, T, D], F32))
        self.y = ctx.enter_context(nc.sbuf_tensor("y", [P, T, D], F32))
        self.mean_var = ctx.enter_context(nc.sbuf_tensor("mean_var", [P, T, 2], F32))
        self.rstd = ctx.enter_context(nc.sbuf_tensor("rstd", [P, T], F32))
        self.minus_half = ctx.enter_context(nc.sbuf_tensor("minus_half", [P, T], F32))
        self.ident = ctx.enter_context(nc.sbuf_tensor("ident", [P, P], F32))
        Phase.psum = ctx.enter_context(nc.psum_tensor("psum", [P, 8 * 512], F32))


class Phase:

    def __init__(self, nc, name):
        self.nc, self.name, self.ctx, self.next_bank = nc, name, ExitStack(), 0

    def __enter__(self):
        return self

    def __exit__(self, *e):
        self.ctx.close()

    def sb(self, name, shape, dt=F32):
        return self.ctx.enter_context(self.nc.sbuf_tensor(f"{self.name}_{name}", shape, dt))

    def ps(self, banks=1):
        first, self.next_bank = self.next_bank, self.next_bank + banks
        return self.psum[:, first * 512:(first + banks) * 512]

    def sem(self, name):
        sem = self.nc.alloc_semaphore(f"{self.name}_{name}")
        self.taken_semaphores.append(sem)
        return sem

    taken_semaphores = []

    @classmethod
    def clear_semaphores(cls, nc):
        nc.all_engine_barrier()
        nc.clear_and_free_semaphores(cls.taken_semaphores)
        nc.all_engine_barrier()
        cls.taken_semaphores = []

    def block(self):
        return self.nc.Block()


def constants(core):
    nc = core.nc
    with Phase(nc, "const") as ph:
        zeroed = ph.sem("zeroed")
        with ph.block() as block:
            @block.gpsimd
            def _(pool):
                nc.gpsimd.memset(core.minus_half[:, :], -0.5)
                nc.gpsimd.memset(core.ident[:, :], 0.0).then_inc(zeroed, 1)
                pool.wait_ge(zeroed, 1)
                nc.gpsimd.affine_select(out=core.ident[:, :], in_=core.ident[:, :], compare_op=ALU.not_equal,
                                        fill=1.0, base=0, pattern=[[-1, P]], channel_multiplier=1).then_inc(zeroed, 1)
                pool.wait_ge(zeroed, 2)


def split_weights(core, name, parts):
    nc = core.nc
    with Phase(nc, name) as ph:
        stage = ph.sb("stage", [P, 2, 2048])
        loaded = [ph.sem("loaded0"), ph.sem("loaded1")]
        high_done, low_done = ph.sem("high_done"), ph.sem("low_done")

        def staged(i):
            src = parts[i][0]
            return stage[0:src.shape[0], i % 2, 0:src.shape[1]]

        with ph.block() as block:
            @block.sync
            def _(sp):
                for i, (src, _, _) in enumerate(parts):
                    ge(sp, low_done, i - 1)
                    sp.dma_start(staged(i), src).then_inc(loaded[i % 2], 16)

            @block.scalar
            def _(act):
                for i, (_, high, _) in enumerate(parts):
                    act.wait_ge(loaded[i % 2], 16 * (i // 2 + 1))
                    nc.scalar.activation(high, staged(i), ACT.Copy).then_inc(high_done, 1)

            @block.vector
            def _(dve):
                for i, (_, high, low) in enumerate(parts):
                    dve.wait_ge(high_done, i + 1)
                    nc.vector.tensor_tensor(low, staged(i), high.bitcast(F32), ALU.subtract).then_inc(low_done, 1)


class Stats:

    def __init__(self, ph, name):
        self.nc = ph.nc
        self.halves = ph.sb(f"{name}_halves", [P, T, 6])
        self.spread = ph.sb(f"{name}_spread", [P, T])
        self.var = ph.sb(f"{name}_var", [P, T])
        self.summed = ph.sem(f"{name}_summed")
        self.mean_done = ph.sem(f"{name}_mean_done")
        self.var_done = ph.sem(f"{name}_var_done")

    def aggregate(self, dve, at, n, times, mean, factor):
        nc = self.nc
        halves = self.halves[:, bass.ds(at, n), :]
        spread, var = self.spread[:, bass.ds(at, n)], self.var[:, bass.ds(at, n)]
        nc.vector.tensor_tensor(spread, halves[:, :, 1], halves[:, :, 4], ALU.subtract)
        nc.vector.tensor_tensor(mean, halves[:, :, 1], halves[:, :, 4], ALU.add)
        nc.vector.tensor_tensor(var, halves[:, :, 2], halves[:, :, 5], ALU.add).then_inc(self.summed, 1)
        dve.wait_ge(self.summed, times * 2 + 1)
        nc.vector.tensor_scalar(mean, mean, factor, None, ALU.mult).then_inc(self.mean_done, 1)
        nc.vector.scalar_tensor_tensor(out=spread, in0=spread, scalar=0.25, in1=spread, op0=ALU.mult,
                                       op1=ALU.mult).then_inc(self.summed, 1)
        dve.wait_ge(self.summed, times * 2 + 2)
        nc.vector.scalar_tensor_tensor(out=var, in0=var, scalar=1.0 / D, in1=spread, op0=ALU.mult, op1=ALU.add)\
            .then_inc(self.var_done, 1)

    def rstd(self, pool, out, at, n, times, minus_half, eps_added, done):
        nc = self.nc
        var = self.var[:, bass.ds(at, n)]
        pool.wait_ge(self.var_done, times + 1)
        nc.gpsimd.tensor_scalar(var, var, EPS, 1.0, ALU.add, ALU.mult).then_inc(eps_added, 1)
        pool.wait_ge(eps_added, times + 1)
        nc.gpsimd.tensor_tensor(out, var, minus_half, ALU.pow).then_inc(done, 1)


def x_statistics(core, x_dram):
    nc = core.nc
    with Phase(nc, "in") as ph:
        stats = Stats(ph, "x")
        x_in = [ph.sem(f"x_in{b}") for b in range(B)]
        x_stats, eps_added, rstd_done = ph.sem("x_stats"), ph.sem("eps_added"), ph.sem("rstd_done")
        with ph.block() as block:
            @block.sync
            def _(sp):
                for b in range(B):
                    sp.dma_start(core.x[:, b * TB:(b + 1) * TB, :], x_dram[b, :, :, :]).then_inc(x_in[b], 16)

            @block.vector
            def _(dve):
                for b in range(B):
                    dve.wait_ge(x_in[b], 16)
                    for i in range(b * TB, (b + 1) * TB):
                        nc.vector.bn_stats(stats.halves[:, i, :], core.x[:, i, :]).then_inc(x_stats, 1)
                dve.wait_ge(x_stats, T)
                stats.aggregate(dve, 0, T, 0, core.mean_var[:, :, 0], 0.5)

            @block.gpsimd
            def _(pool):
                stats.rstd(pool, core.rstd[:, :], 0, T, 0, core.minus_half[:, :], eps_added, rstd_done)


def residual(core, name, gather=None, project=None, out_dram=None):
    nc = core.nc
    G = 4
    NG = T // G
    with Phase(nc, name) as ph:
        y_stats_of, x_stats_of = Stats(ph, "y"), Stats(ph, "x")
        neg_mean = ph.sb("neg_mean", [P, T])
        rstd_y = ph.sb("rstd_y", [P, T])
        y_eps, x_eps, rstd_y_done, rstd_x_done = (ph.sem(n) for n in ("y_eps", "x_eps", "rstd_y_done", "rstd_x_done"))
        y_stats, x_stats, centred, x_ready = (ph.sem(n) for n in ("y_stats", "x_stats", "centred", "x_ready"))
        if gather is not None:
            r, y_rows = gather
            rows = y_rows.rearrange("j p d -> (j p) d")
            got = ph.sb("got", [P, 2, G, 2, D])
            came = [[ph.sem(f"came{j}{t}") for t in range(G)] for j in range(2)]
            first_added, added = ph.sem("first_added"), ph.sem("added")
        if project is not None:
            wo_high, wo_low, bias_row = project
            at_high = [ph.sb(f"at_high{j}", [P, KD, P], F32R) for j in range(G)]
            at_low = [ph.sb(f"at_low{j}", [P, KD, P], F32R) for j in range(G)]
            bias = ph.sb("bias", [1, D])
            bias_parts = [ph.sb(f"bias_{x}", [1, D], F32R) for x in ("high", "low")]
            ones = ph.sb("ones", [1, P])
            ones_r = ph.sb("ones_r", [1, P], F32R)
            turn_ps = [ph.ps() for j in range(G)]
            out_ps = [ph.ps() for j in range(G)]
            bias_in, ones_set, bias_high, bias_low, ones_kept = (
                ph.sem(n) for n in ("bias_in", "ones_set", "bias_high", "bias_low", "ones_kept"))
            turned, high, low, projected, kept = (ph.sem(n) for n in ("turned", "high", "low", "projected", "kept"))
        if out_dram is not None:
            stored = ph.sem("stored")

        with ph.block() as block:
            @block.sync
            def _(sp):
                if project is not None:
                    sp.dma_start(bias[:, :], bias_row).then_inc(bias_in, 16)
                if out_dram is not None:
                    for b in range(B):
                        sp.wait_ge(x_ready, (b + 1) * TB)
                        sp.dma_start(out_dram[b, :, :, :], core.x[:, b * TB:(b + 1) * TB, :]).then_inc(stored, 16)
                    sp.wait_ge(stored, 16 * B)

            @block.gpsimd
            def _(pool):
                if project is not None:
                    nc.gpsimd.memset(ones[:, :], 1.0).then_inc(ones_set, 1)
                for g in range(NG + 2):
                    if gather is not None and g < NG:
                        ge(pool, added, (g - 1) * G)
                        for t in range(G):
                            for c in range(2):
                                pool.indirect_dma_start(
                                    got[:, g % 2, t, c, :], None, rows,
                                    bass.IndirectOffsetOnAxis(ap=r.slots[:, g * G + t, c:c + 1], axis=0))\
                                    .then_inc(came[g % 2][t], 16)
                    if g >= 2:
                        y_stats_of.rstd(pool, rstd_y[:, (g - 2) * G:(g - 1) * G], (g - 2) * G, G, g - 2,
                                        core.minus_half[:, 0:G], y_eps, rstd_y_done)
                if out_dram is None:
                    x_stats_of.rstd(pool, core.rstd[:, :], 0, T, 0, core.minus_half[:, :], x_eps, rstd_x_done)

            @block.tensor
            def _(pe):
                if project is None:
                    return
                pe.wait_ge(bias_low, 1)
                pe.wait_ge(ones_kept, 1)

                def turn(i, j):
                    ge(pe, low, i - G + 1)
                    for k in range(KD):
                        last = nc.tensor.transpose(turn_ps[j][:, k * P:(k + 1) * P],
                                                   core.y[:, i, k * P:(k + 1) * P], core.ident[:, :])
                    last.then_inc(turned, 1)

                def project_tile(i, j):
                    pe.wait_ge(low, i + 1)
                    ge(pe, kept, i - G + 1)
                    out = out_ps[j][:, 0:D]
                    for part in range(2):
                        nc.tensor.matmul(out, ones_r[:, :], bias_parts[part][:, :], start=(part == 0), stop=False)
                    n = 0
                    for k in range(KD):
                        for at, wt in ((at_high, wo_high), (at_low, wo_high), (at_high, wo_low)):
                            n += 1
                            last = nc.tensor.matmul(out, at[j][:, k, :], wt[:, k, :], start=False, stop=(n == 3 * KD))
                    last.then_inc(projected, 1)

                for i in range(T + 2):
                    if i < T:
                        turn(i, i % G)
                    if i >= 2:
                        project_tile(i - 2, (i - 2) % G)

            @block.scalar
            def _(act):
                if project is not None:
                    act.wait_ge(bias_in, 16)
                    nc.scalar.activation(bias_parts[0][:, :], bias[:, :], ACT.Copy).then_inc(bias_high, 1)
                    act.wait_ge(ones_set, 1)
                    nc.scalar.activation(ones_r[:, :], ones[:, :], ACT.Copy).then_inc(ones_kept, 1)

                def keep(i, j):
                    act.wait_ge(projected, i + 1)
                    nc.scalar.activation(core.y[:, i, :], out_ps[j][:, 0:D], ACT.Copy).then_inc(kept, 1)

                def step(g):
                    peeled = isinstance(g, int)
                    for t in range(G):
                        if project is not None and not (peeled and g >= NG):
                            i = g * G + t
                            act.wait_ge(turned, i + 1)
                            ge(act, projected, i - G + 1)
                            nc.scalar.activation(at_high[t][:, :, :],
                                                 turn_ps[t][:, 0:D].rearrange("p (k t) -> p k t", k=KD),
                                                 ACT.Copy).then_inc(high, 1)
                            if not (peeled and i < 2):
                                keep(i - 2, (t - 2) % G)
                            if peeled and i == T - 1:
                                keep(i - 1, t - 1)
                                keep(i, t)
                        if not (peeled and g < 2):
                            act.wait_ge(y_stats_of.mean_done, g - 1)
                            i = (g - 2) * G + t
                            nc.scalar.activation(core.y[:, i, :], core.y[:, i, :], ACT.Identity,
                                                 bias=neg_mean[:, bass.ds(i, 1)]).then_inc(centred, 1)
                for g in range(2):
                    step(g)
                with act.Fori(2, NG - 1) as g:
                    step(g)
                for g in range(NG - 1, NG + 2):
                    step(g)

            @block.vector
            def _(dve):
                if project is not None:
                    dve.wait_ge(bias_high, 1)
                    nc.vector.tensor_tensor(bias_parts[1][:, :], bias[:, :], bias_parts[0][:, :].bitcast(F32),
                                            ALU.subtract).then_inc(bias_low, 1)

                def add_gathered(g, j, before):
                    for c, done in ((0, first_added), (1, added)):
                        for t in range(G):
                            i = g * G + t
                            if c == 0:
                                dve.wait_ge(came[j][t], before * 32 + 32)
                            else:
                                dve.wait_ge(first_added, i + 1)
                            nc.vector.scalar_tensor_tensor(out=core.y[:, i, :], in0=got[:, j, t, c, :],
                                                           scalar=r.weights[:, i, c:c + 1], in1=core.y[:, i, :],
                                                           op0=ALU.mult, op1=ALU.add).then_inc(done, 1)

                def lower(i, j):
                    dve.wait_ge(high, i + 1)
                    ge(dve, projected, i - G + 1)
                    nc.vector.tensor_tensor(at_low[j][:, :, :], turn_ps[j][:, 0:D].rearrange("p (k t) -> p k t", k=KD),
                                            at_high[j][:, :, :].bitcast(F32), ALU.subtract).then_inc(low, 1)

                def y_halves(i):
                    if gather is not None:
                        dve.wait_ge(added, i + 1)
                    if project is not None:
                        dve.wait_ge(kept, i + 1)
                    nc.vector.bn_stats(y_stats_of.halves[:, i, :], core.y[:, i, :]).then_inc(y_stats, 1)

                def add(i):
                    dve.wait_ge(centred, i + 1)
                    nc.vector.scalar_tensor_tensor(out=core.x[:, i, :], in0=core.y[:, i, :],
                                                   scalar=rstd_y[:, bass.ds(i, 1)], in1=core.x[:, i, :],
                                                   op0=ALU.mult, op1=ALU.add).then_inc(x_ready, 1)

                def x_halves(i):
                    if out_dram is None:
                        dve.wait_ge(x_ready, i + 1)
                        nc.vector.bn_stats(x_stats_of.halves[:, i, :], core.x[:, i, :]).then_inc(x_stats, 1)

                def step(g, j, before):
                    peeled = isinstance(g, int)
                    forming, counting, adding = (not (peeled and g >= NG), not (peeled and not 1 <= g <= NG),
                                                 not (peeled and g < 2))
                    if forming and gather is not None:
                        add_gathered(g, j, before)
                    for t in range(G):
                        if forming and project is not None:
                            lower(g * G + t, t)
                        if counting:
                            y_halves((g - 1) * G + t)
                        if adding:
                            if t == 0:
                                dve.wait_ge(rstd_y_done, g - 1)
                            add((g - 2) * G + t)
                            if t >= 1:
                                x_halves((g - 2) * G + t - 1)
                    if counting:
                        dve.wait_ge(y_stats, g * G)
                        y_stats_of.aggregate(dve, (g - 1) * G, G, g - 1, neg_mean[:, bass.ds((g - 1) * G, G)], -0.5)
                    if adding:
                        x_halves((g - 2) * G + G - 1)
                step(0, 0, 0)
                step(1, 1, 0)
                with dve.Fori(1, NG // 2) as k:
                    step(k * 2, 0, k)
                    step(k * 2 + 1, 1, k)
                step(NG, 0, NG // 2)
                step(NG + 1, 1, NG // 2)
                if out_dram is None:
                    dve.wait_ge(x_stats, T)
                    x_stats_of.aggregate(dve, 0, T, 0, core.mean_var[:, :, 0], 0.5)


def linear_attention(core, qkv_high, qkv_low, bias_q_col, bias_kv_row, zero_dram):
    nc = core.nc
    G = 4
    GROUPS_B = TB // G
    with Phase(nc, "la") as ph:
        xhat = [ph.sb(f"xhat{j}", [P, D]) for j in range(2)]
        xt_high = [ph.sb(f"xt_high{h}", [P, KD, G * P], F32R) for h in range(GROUPS_B)]
        xt_low = [ph.sb(f"xt_low{h}", [P, KD, G * P], F32R) for h in range(GROUPS_B)]
        kv_lin = [ph.sb(f"kv_lin{j}", [P, 2 * KD, P + 1]) for j in range(2)]
        k_exp = [ph.sb(f"k_exp{j}", [P, KD, P]) for j in range(2)]
        k_relu = [ph.sb(f"k_relu{j}", [P, KD, P]) for j in range(2)]
        k_map = [ph.sb(f"k_map{j}", [P, KD, P]) for j in range(2)]
        q_exp = [ph.sb(f"q_exp{m}", [P, G * P]) for m in range(KD)]
        q_relu = [ph.sb(f"q_relu{m}", [P, G * P]) for m in range(KD)]
        qT = [ph.sb(f"qT{h}", [P, KD, G * P]) for h in range(GROUPS_B)]
        kv = ph.sb("kv", [P, KD, P + HPB])
        head_mask = ph.sb("head_mask", [P, P])
        zcol_mask = ph.sb("zcol_mask", [P, HPB])
        z = [ph.sb(f"z{j}", [P, HEADS]) for j in range(2)]
        bias_q = ph.sb("bias_q", [P, KD])
        bias_kv = ph.sb("bias_kv", [P, 2 * D])
        zeros = ph.sb("zeros", [P, 8 * D])

        turn_ps = [ph.ps() for j in range(2)]
        kv_proj_ps = [ph.ps() for j in range(2)]
        q_ps = [ph.ps() for m in range(KD)]
        kv_ps = ph.ps()
        num_ps = ph.ps()
        kv_sum = kv_ps[:, 0:KD * (P + 1)].rearrange("p (k c) -> p k c", k=KD)
        num = num_ps[:, 0:KD * (P + HPB)].rearrange("p (k c) -> p k c", k=KD)

        s = {n: ph.sem(n) for n in ("bias_in", "ones_set", "zeroed", "zeros_out", "masks", "xhat_done", "turned",
                                    "high", "low", "projected", "linear", "expd", "relud", "k_done", "summed",
                                    "kv_done", "q_projected", "q_expd", "q_relud", "q_done", "numer", "z_eps",
                                    "z_done", "y_done")}

        def real(i):
            return not isinstance(i, int) or 0 <= i < T

        def queries_before(b, w):
            return b * GROUPS_B + w // G - 1, (w // G - 1) % GROUPS_B

        def slots(eng, slot):
            def turn(b):
                for w in range(TB):
                    slot(b, w)
            turn(0)
            with eng.Fori(1, B - 1) as b:
                turn(b)
            turn(B - 1)
            turn(B)

        with ph.block() as block:
            @block.sync
            def _(sp):
                sp.dma_start(bias_q[:, :], bias_q_col).then_inc(s["bias_in"], 16)
                sp.dma_start(bias_kv[:, :], bias_kv_row.to_broadcast([P, 2 * D])).then_inc(s["bias_in"], 16)
                flat = zero_dram.rearrange("j p d -> (j p) d").rearrange("(p r) d -> p (r d)", p=P)
                sp.wait_ge(s["zeroed"], 1)
                for r in range(0, SLOT_TILES, 8):
                    sp.dma_start(flat[:, r * D:(r + 8) * D], zeros[:, :]).then_inc(s["zeros_out"], 16)
                sp.wait_ge(s["zeros_out"], SLOT_TILES // 8 * 16)

            @block.gpsimd
            def _(pool):
                for j in range(2):
                    nc.gpsimd.memset(kv_lin[j][:, :, P:P + 1], 1.0).then_inc(s["ones_set"], 1)
                nc.gpsimd.memset(head_mask[:, :], 1.0).then_inc(s["masks"], 1)
                nc.gpsimd.memset(zcol_mask[:, :], 1.0).then_inc(s["masks"], 1)
                done = 2
                for m, pattern in ((head_mask, [[DH, HPB], [0, DH]]), (zcol_mask, [[DH, HPB]])):
                    view = m[:, :].rearrange("p (h c) -> p h c", c=DH) if m is head_mask else m[:, :]
                    neg = [[-st, n] for st, n in pattern]
                    pool.wait_ge(s["masks"], done)
                    nc.gpsimd.affine_select(out=view, in_=view, compare_op=ALU.is_ge, fill=0.0, base=0,
                                            pattern=neg, channel_multiplier=1).then_inc(s["masks"], 1)
                    pool.wait_ge(s["masks"], done + 1)
                    nc.gpsimd.affine_select(out=view, in_=view, compare_op=ALU.is_ge, fill=0.0, base=DH - 1,
                                            pattern=pattern, channel_multiplier=-1).then_inc(s["masks"], 1)
                    done += 2
                nc.gpsimd.memset(zeros[:, :], 0.0).then_inc(s["zeroed"], 1)

            @block.vector
            def _(dve):
                dve.wait_ge(s["bias_in"], 32)
                dve.wait_ge(s["ones_set"], 2)
                dve.wait_ge(s["masks"], 6)

                def norm(i, j):
                    ge(dve, s["turned"], i - 1)
                    nc.vector.tensor_scalar(xhat[j][:, :], core.x[:, i, :], core.mean_var[:, i, 0:1],
                                            core.rstd[:, bass.ds(i, 1)], ALU.subtract, ALU.mult)\
                        .then_inc(s["xhat_done"], 1)

                def low(i, w):
                    dve.wait_ge(s["high"], i + 1)
                    h, u = w // G % GROUPS_B, w % G
                    nc.vector.tensor_tensor(xt_low[h][:, :, u * P:(u + 1) * P],
                                            turn_ps[w % 2][:, 0:D].rearrange("p (k t) -> p k t", k=KD),
                                            xt_high[h][:, :, u * P:(u + 1) * P].bitcast(F32), ALU.subtract)\
                        .then_inc(s["low"], 1)

                def add_bias(i, j):
                    dve.wait_ge(s["projected"], i + 1)
                    ge(dve, s["expd"], i - 1)
                    ge(dve, s["relud"], i - 1)
                    ge(dve, s["summed"], i - 1)
                    nc.vector.tensor_tensor(kv_lin[j][:, :, 0:P],
                                            kv_proj_ps[j][:, :].rearrange("p (k c) -> p k c", c=P),
                                            bias_kv[:, :].rearrange("p (k c) -> p k c", c=P), ALU.add)\
                        .then_inc(s["linear"], 1)

                def map_k(i, j):
                    dve.wait_ge(s["expd"], i + 1)
                    dve.wait_ge(s["relud"], i + 1)
                    ge(dve, s["summed"], i - 1)
                    nc.vector.scalar_tensor_tensor(out=k_map[j][:, :, :], in0=k_exp[j][:, :, :], scalar=1.0,
                                                   in1=k_relu[j][:, :, :], op0=ALU.min, op1=ALU.add)\
                        .then_inc(s["k_done"], 1)

                def map_q(g, h, m):
                    dve.wait_ge(s["q_expd"], g * KD + (m + 1))
                    dve.wait_ge(s["q_relud"], g * KD + (m + 1))
                    ge(dve, s["numer"], g * G - G)
                    nc.vector.scalar_tensor_tensor(out=qT[h][:, m, :], in0=q_exp[m][:, :], scalar=1.0,
                                                   in1=q_relu[m][:, :], op0=ALU.min, op1=ALU.add)\
                        .then_inc(s["q_done"], 1)

                def keep_kv(b):
                    dve.wait_ge(s["summed"], b * TB + TB)
                    ge(dve, s["numer"], b * TB)
                    for k in range(KD):
                        nc.vector.tensor_tensor(kv[:, k, 0:P], kv_sum[:, k, 0:P], head_mask[:, :], ALU.mult)
                        nc.vector.tensor_scalar(kv[:, k, P:P + HPB], zcol_mask[:, :], kv_sum[:, k, P:P + 1], None,
                                                ALU.mult).then_inc(s["kv_done"], 1)

                def scores(i, j):
                    dve.wait_ge(s["numer"], i + 1)
                    zj = z[j][:, :].rearrange("p (k h) -> p k h", k=KD)
                    nc.vector.tensor_scalar(zj, num[:, :, P:P + HPB], 1e-6, None, ALU.add).then_inc(s["z_eps"], 1)
                    dve.wait_ge(s["z_eps"], i + 1)
                    nc.vector.reciprocal(z[j][:, :], z[j][:, :]).then_inc(s["z_done"], 1)
                    dve.wait_ge(s["z_done"], i + 1)
                    for k in range(KD):
                        last = nc.vector.tensor_tensor(
                            core.y[:, i, k * P:(k + 1) * P].rearrange("p (h c) -> p h c", c=DH),
                            num[:, k, 0:P].rearrange("p (h c) -> p h c", c=DH),
                            z[j][:, k * HPB:(k + 1) * HPB].unsqueeze(2).to_broadcast([P, HPB, DH]), ALU.mult)
                    last.then_inc(s["y_done"], 1)

                def slot(b, w):
                    i, j = b * TB + w, w % 2
                    if real(i - 1):
                        map_k(i - 1, 1 - j)
                    if real(i + 2):
                        low(i + 2, w + 2)
                    if real(i + 3):
                        norm(i + 3, 1 - j)
                    if real(i):
                        add_bias(i, j)
                    g, h = queries_before(b, w)
                    if w % G >= 2 and real(g * G):
                        map_q(g, h, w % G - 2)
                    if w == 0 and real(i - 1):
                        keep_kv(b - 1)
                    if real(i - TB):
                        scores(i - TB, j)

                norm(0, 0)
                norm(1, 1)
                low(0, 0)
                norm(2, 0)
                low(1, 1)
                slots(dve, slot)

            @block.scalar
            def _(act):
                act.wait_ge(s["bias_in"], 32)

                def high(i, w):
                    act.wait_ge(s["turned"], i + 1)
                    h, u = w // G % GROUPS_B, w % G
                    if u == 0:
                        group = i // G if isinstance(i, int) else queries_of["group"]
                        ge(act, s["q_projected"], group * KD - KD)
                    nc.scalar.activation(xt_high[h][:, :, u * P:(u + 1) * P],
                                         turn_ps[w % 2][:, 0:D].rearrange("p (k t) -> p k t", k=KD), ACT.Copy)\
                        .then_inc(s["high"], 1)
                queries_of = {}

                def parts_k(i, j):
                    act.wait_ge(s["linear"], i + 1)
                    ge(act, s["k_done"], i - 1)
                    nc.scalar.activation(k_exp[j][:, :, :], kv_lin[j][:, 0:KD, 0:P], ACT.Exp).then_inc(s["expd"], 1)
                    nc.scalar.activation(k_relu[j][:, :, :], kv_lin[j][:, 0:KD, 0:P], ACT.Relu)\
                        .then_inc(s["relud"], 1)

                def parts_q(g, m):
                    act.wait_ge(s["q_projected"], g * KD + (m + 1))
                    ge(act, s["q_done"], g * KD + (m - 1))
                    nc.scalar.activation(q_exp[m][:, :], q_ps[m][:, :], ACT.Exp, bias=bias_q[:, m:m + 1])\
                        .then_inc(s["q_expd"], 1)
                    nc.scalar.activation(q_relu[m][:, :], q_ps[m][:, :], ACT.Relu, bias=bias_q[:, m:m + 1])\
                        .then_inc(s["q_relud"], 1)

                def slot(b, w):
                    i, j = b * TB + w, w % 2
                    queries_of["group"] = b * GROUPS_B + (w + 2) // G
                    if real(i + 2):
                        high(i + 2, w + 2)
                    if real(i):
                        parts_k(i, j)
                    g, h = queries_before(b, w)
                    if w % G in (1, 2) and real(g * G):
                        parts_q(g, w % G - 1)
                high(0, 0)
                high(1, 1)
                slots(act, slot)

            @block.tensor
            def _(pe):
                def turn(i, j):
                    pe.wait_ge(s["xhat_done"], i + 1)
                    ge(pe, s["low"], i - 1)
                    for k in range(KD):
                        last = nc.tensor.transpose(turn_ps[j][:, k * P:(k + 1) * P], xhat[j][:, k * P:(k + 1) * P],
                                                   core.ident[:, :])
                    last.then_inc(s["turned"], 1)

                def project_kv(i, w):
                    pe.wait_ge(s["low"], i + 1)
                    ge(pe, s["linear"], i - 1)
                    n = 0
                    h, u = w // G, w % G
                    for k in range(KD):
                        for xt, wt in ((xt_high, qkv_high), (xt_low, qkv_high), (xt_high, qkv_low)):
                            n += 1
                            last = nc.tensor.matmul(kv_proj_ps[w % 2][:, :], xt[h][:, k, u * P:(u + 1) * P],
                                                    wt[:, k, D:3 * D], start=(n == 1), stop=(n == 3 * KD))
                    last.then_inc(s["projected"], 1)

                def project_q(g, h, m):
                    pe.wait_ge(s["low"], g * G + G)
                    ge(pe, s["q_relud"], g * KD + (m - 1))
                    n = 0
                    for k in range(KD):
                        for wt, xt in ((qkv_high, xt_high), (qkv_high, xt_low), (qkv_low, xt_high)):
                            n += 1
                            last = nc.tensor.matmul(q_ps[m][:, :], wt[:, k, m * P:(m + 1) * P], xt[h][:, k, :],
                                                    start=(n == 1), stop=(n == 3 * KD))
                    last.then_inc(s["q_projected"], 1)

                def sum_kv(i, j, first, last_of_batch, batches_before):
                    pe.wait_ge(s["k_done"], i + 1)
                    if first:
                        ge(pe, s["kv_done"], batches_before * KD)
                    for k in range(KD):
                        last = nc.tensor.matmul(kv_sum[:, k, :], k_map[j][:, k, :], kv_lin[j][:, KD + k, :],
                                                start=(first and k == 0),
                                                stop=(last_of_batch and k == KD - 1))
                    last.then_inc(s["summed"], 1)

                def score(b, w):
                    i = b * TB + w
                    pe.wait_ge(s["kv_done"], b * KD + KD)
                    pe.wait_ge(s["q_done"], b * (GROUPS_B * KD) + (w // G + 1) * KD)
                    ge(pe, s["y_done"], i)
                    h, u = w // G, w % G
                    for k in range(KD):
                        last = nc.tensor.matmul(num[:, k, :], qT[h][:, k, u * P:(u + 1) * P], kv[:, k, :],
                                                start=True, stop=True)
                    last.then_inc(s["numer"], 1)

                def slot(b, w):
                    i, j = b * TB + w, w % 2
                    if real(i + 2):
                        turn(i + 2, j)
                    if real(i):
                        project_kv(i, w)
                    if real(i - 1):
                        sum_kv(i - 1, 1 - j, w == 1, w == 0, b)
                    if real(i - TB):
                        score(b - 1, w)
                    g, h = queries_before(b, w)
                    if w % G < KD and real(g * G):
                        project_q(g, h, w % G)
                turn(0, 0)
                turn(1, 1)
                slots(pe, slot)


def attention_projections(core, w_high, w_low, bias_col, q_dram, k_dram, v_all):
    nc = core.nc
    G = 4
    NG = T // G
    with Phase(nc, "ap") as ph:
        xhat = [ph.sb(f"xhat{j}", [P, D]) for j in range(2)]
        xt_high = [ph.sb(f"xt_high{j}", [P, KD, G * P], F32R) for j in range(2)]
        xt_low = [ph.sb(f"xt_low{j}", [P, KD, G * P], F32R) for j in range(2)]
        lin = [ph.sb(f"lin{m}", [P, G * P]) for m in range(3)]
        high = [ph.sb(f"high{m}", [P, G * P], F32R) for m in range(3)]
        low = [ph.sb(f"low{m}", [P, G * P], F32R) for m in range(3)]
        bias = ph.sb("bias", [P, 3])
        turn_ps = [ph.ps() for j in range(2)]
        proj_ps = [ph.ps() for m in range(3)]
        v_ps = ph.ps()
        s = {n: ph.sem(n) for n in ("bias_in", "v_cleared", "xhat_done", "turned", "high", "low", "projected",
                                    "linear", "part_high", "part_low", "stored", "v_turned", "v_kept")}
        with ph.block() as block:
            @block.sync
            def _(sp):
                sp.dma_start(bias[:, :], bias_col).then_inc(s["bias_in"], 16)

                def store(g):
                    sp.wait_ge(s["part_low"], g * 3 + 3)
                    cols = bass.ds(g * (G * P), G * P)
                    for m in range(2):
                        sp.dma_start(q_dram[0, m * P:(m + 1) * P, cols], high[m][:, :].bitcast(F32)).then_inc(s["stored"], 16)
                        sp.dma_start(q_dram[1, m * P:(m + 1) * P, cols], low[m][:, :].bitcast(F32)).then_inc(s["stored"], 16)
                    sp.dma_start(k_dram[0, :, cols], high[2][0:64, :].bitcast(F32)).then_inc(s["stored"], 16)
                    sp.dma_start(k_dram[1, :, cols], low[2][0:64, :].bitcast(F32)).then_inc(s["stored"], 16)
                tiles(sp, NG, 2, lambda g, u: store(g))
                sp.wait_ge(s["stored"], 96 * NG)

            @block.gpsimd
            def _(pool):
                nc.gpsimd.memset(v_all[:, :, :, :], 0.0).then_inc(s["v_cleared"], 1)
                pool.wait_ge(s["v_cleared"], 1)
                nc.gpsimd.memset(v_all[:, :, :, DH:DH + 1], 1.0).then_inc(s["v_cleared"], 1)

            @block.vector
            def _(dve):
                dve.wait_ge(s["v_cleared"], 2)

                def norm(i, j):
                    ge(dve, s["turned"], i - 1)
                    nc.vector.tensor_scalar(xhat[j][:, :], core.x[:, i, :], core.mean_var[:, i, 0:1],
                                            core.rstd[:, bass.ds(i, 1)], ALU.subtract, ALU.mult)\
                        .then_inc(s["xhat_done"], 1)

                def lower(i, u, gj):
                    dve.wait_ge(s["high"], i + 1)
                    nc.vector.tensor_tensor(xt_low[gj][:, :, u * P:(u + 1) * P],
                                            turn_ps[u % 2][:, 0:D].rearrange("p (k t) -> p k t", k=KD),
                                            xt_high[gj][:, :, u * P:(u + 1) * P].bitcast(F32), ALU.subtract)\
                        .then_inc(s["low"], 1)

                def group(g, gj):
                    ge(dve, s["projected"], g * 3 - 3)
                    norm(g * G, 0)
                    for u in range(G):
                        i = g * G + u
                        if u + 1 < G:
                            norm(i + 1, (u + 1) % 2)
                        lower(i, u, gj)
                    ge(dve, s["stored"], g * 96)
                    for m in range(3):
                        dve.wait_ge(s["part_high"], g * 3 + (m + 1))
                        nc.vector.tensor_tensor(low[m][:, :], lin[m][:, :], high[m][:, :].bitcast(F32),
                                                ALU.subtract).then_inc(s["part_low"], 1)
                    dve.wait_ge(s["v_turned"], g + 1)
                    nc.vector.tensor_copy(v_all[:, bass.ds(g * G, G), :, 0:DH],
                                          v_ps[:, :].rearrange("p (t f) -> p t f", t=G)[:, :, 64:128]
                                          .rearrange("p t (h d) -> p t h d", d=DH)).then_inc(s["v_kept"], 1)
                tiles(dve, NG, 2, group)

            @block.scalar
            def _(act):
                act.wait_ge(s["bias_in"], 16)

                def group(g, gj):
                    ge(act, s["projected"], g * 3 - 3)
                    for u in range(G):
                        act.wait_ge(s["turned"], g * G + (u + 1))
                        nc.scalar.activation(xt_high[gj][:, :, u * P:(u + 1) * P],
                                             turn_ps[u % 2][:, 0:D].rearrange("p (k t) -> p k t", k=KD),
                                             ACT.Copy).then_inc(s["high"], 1)
                    ge(act, s["part_low"], g * 3)
                    ge(act, s["stored"], g * 96)
                    ge(act, s["v_turned"], g)
                    for m in range(3):
                        act.wait_ge(s["projected"], g * 3 + (m + 1))
                        nc.scalar.activation(lin[m][:, :], proj_ps[m][:, :], ACT.Identity, bias=bias[:, m:m + 1])\
                            .then_inc(s["linear"], 1)
                        act.wait_ge(s["linear"], g * 3 + (m + 1))
                        nc.scalar.activation(high[m][:, :], lin[m][:, :], ACT.Copy).then_inc(s["part_high"], 1)
                tiles(act, NG, 2, group)

            @block.tensor
            def _(pe):
                def group(g, gj):
                    for u in range(G):
                        i = g * G + u
                        pe.wait_ge(s["xhat_done"], i + 1)
                        ge(pe, s["low"], i - 1)
                        for k in range(KD):
                            last = nc.tensor.transpose(turn_ps[u % 2][:, k * P:(k + 1) * P],
                                                       xhat[u % 2][:, k * P:(k + 1) * P], core.ident[:, :])
                        last.then_inc(s["turned"], 1)
                    pe.wait_ge(s["low"], g * G + G)
                    for m in range(3):
                        ge(pe, s["linear"], g * 3 + m - 2)
                        n = 0
                        for k in range(KD):
                            for wt, xt in ((w_high, xt_high), (w_high, xt_low), (w_low, xt_high)):
                                n += 1
                                last = nc.tensor.matmul(proj_ps[m][:, :], wt[:, k, m * P:(m + 1) * P],
                                                        xt[gj][:, k, :], start=(n == 1), stop=(n == 3 * KD))
                        last.then_inc(s["projected"], 1)
                    pe.wait_ge(s["linear"], g * 3 + 3)
                    ge(pe, s["v_kept"], g)
                    for u in range(G):
                        last = nc.tensor.transpose(v_ps[:, u * P:(u + 1) * P], lin[2][:, u * P:(u + 1) * P],
                                                   core.ident[:, :])
                    last.then_inc(s["v_turned"], 1)
                tiles(pe, NG, 2, group)


def softmax_attention(core, q_dram, k_dram, v_all, negmax_dram, o_dram):
    nc = core.nc
    QU = N // 2
    QT = QU // P
    KT = N // P
    ROWS = 4 * DH
    STEPS = NKV * KT
    END = STEPS - 4
    MAXES = HEADS * QT
    KV_MAXES = GROUPS * QT
    with Phase(nc, "sa") as ph:
        q_stack = [ph.sb(f"q_stack{h}", [P, HEADS, QU], F32R) for h in range(2)]
        k_max = ph.sb("k_max", [ROWS, NKV, N], F32R)
        k_main = ph.sb("k_main", [P, NKV, N], F32R)
        v_now = ph.sb("v_now", [P, KT, NKV, 32])
        probs = [ph.sb(f"probs{j}", [P, QU]) for j in range(8)]
        negmax = [ph.sb(f"negmax{h}", [P, QT, HEADS]) for h in range(2)]
        turned_high = ph.sb("turned_high", [HEADS, QU], F32R)
        turned_low = ph.sb("turned_low", [HEADS, QU], F32R)
        o_sb = [ph.sb(f"o_sb{j}", [P, QU]) for j in range(2)]
        st_ps = [ph.ps() for j in range(3)]
        mx_ps = [ph.ps(2) for j in range(2)]
        o_ps = ph.ps()
        q_in = [[ph.sem(f"q_in{h}{kv}") for kv in range(NKV)] for h in range(2)]
        kmax_in = [ph.sem(f"kmax_in{kv}") for kv in range(NKV)]
        kmain_in = [ph.sem(f"kmain_in{kv}") for kv in range(NKV)]
        s = {n: ph.sem(n) for n in ("pads", "v_in", "max_scored",
                                    "maxed", "turned", "t_high", "t_low", "neg_out", "neg_in0", "neg_in1", "scored",
                                    "expd", "weighted", "o_kept", "o_out0", "o_out1")}

        def max_steps(step):
            def until(n):
                return min(n, END) * MAXES // END
            return range(until(step), until(step + 1))

        with ph.block() as block:
            @block.gpsimd
            def _(pool):
                for q in q_stack:
                    nc.gpsimd.memset(q[64:P, :, :].bitcast(F32), 0.0).then_inc(s["pads"], 1)
                nc.gpsimd.memset(k_main[64:P, :, :].bitcast(F32), 0.0).then_inc(s["pads"], 1)
                pool.wait_ge(s["pads"], 3)
                nc.gpsimd.memset(k_main[64:66, :, :].bitcast(F32), 1.0).then_inc(s["pads"], 1)

                def load_v(b, kv):
                    nc.gpsimd.tensor_copy(v_now[:, :, kv, :], v_all[:, bass.ds(b * KT, KT), kv, :]).then_inc(s["v_in"], 1)

                def store_o(b, h, kv):
                    done = b * (2 * NKV) + h * NKV + kv
                    pool.wait_ge(s["o_kept"], done + 1)
                    pool.dma_start(o_dram[b, h, kv, :, :], o_sb[kv % 2][:, :]).then_inc(s[f"o_out{kv % 2}"], 16)

                def batch(b, last):
                    for h in range(2):
                        for kv in range(NKV):
                            store_o(b, h, kv)
                            if h == 1 and not last:
                                load_v(b + 1, kv)
                pool.wait_ge(s["pads"], 4)
                for kv in range(NKV):
                    load_v(0, kv)
                with pool.Fori(0, B - 1) as b:
                    batch(b, False)
                batch(B - 1, True)
                for j in range(2):
                    pool.wait_ge(s[f"o_out{j}"], 16 * NKV * B)

            @block.sync
            def _(sp):
                def load_q(b, h, kv):
                    heads = slice(kv * GROUPS, (kv + 1) * GROUPS)
                    for r, part in enumerate((0, 1, 0, 1)):
                        sp.dma_start(q_stack[h][r * DH:(r + 1) * DH, heads, :].bitcast(F32),
                                     q_dram[part, kv * GROUPS * DH:(kv + 1) * GROUPS * DH,
                                            bass.ds(b * N + h * QU, QU)]
                                     .rearrange("(h d) t -> d h t", d=DH)).then_inc(q_in[h][kv], 16)

                def load_k(dst, sems, b, kv):
                    for r, part in enumerate((0, 0, 1, 1)):
                        sp.dma_start(dst[r * DH:(r + 1) * DH, kv, :].bitcast(F32),
                                     k_dram[part, kv * DH:(kv + 1) * DH, bass.ds(b * N, N)]).then_inc(sems[kv], 16)

                def put_negmax(b, h):
                    unit = b * 2 + h
                    sp.wait_ge(s["t_low"], unit + 1)
                    sp.dma_start(negmax_dram[unit, 0, :, :], turned_high[:, :].bitcast(F32)).then_inc(s["neg_out"], 16)
                    sp.dma_start(negmax_dram[unit, 1, :, :], turned_low[:, :].bitcast(F32)).then_inc(s["neg_out"], 16)
                    sp.wait_ge(s["neg_out"], unit * 32 + 32)
                    sp.dma_start(q_stack[h][64:66, :, :].bitcast(F32), negmax_dram[unit, :, :, :]).then_inc(s[f"neg_in{h}"], 16)

                def after_main(b, h, kv):
                    sp.wait_ge(s["scored"], b * (2 * 4 * STEPS) + h * (4 * STEPS) + (kv + 1) * (4 * KT))

                def batch(b, last):
                    for kv in range(NKV):
                        if not last:
                            sp.wait_ge(s["maxed"], b * (2 * MAXES) + MAXES + (kv + 1) * KV_MAXES)
                            load_k(k_max, kmax_in, b + 1, kv)
                        if kv == NKV - 1:
                            put_negmax(b, 1)
                        if not last:
                            after_main(b, 0, kv)
                            load_q(b + 1, 0, kv)
                    if not last:
                        for kv in range(NKV):
                            if kv == NKV - 1:
                                put_negmax(b + 1, 0)
                            after_main(b, 1, kv)
                            load_k(k_main, kmain_in, b + 1, kv)
                            load_q(b + 1, 1, kv)
                for kv in range(NKV):
                    load_k(k_max, kmax_in, 0, kv)
                    load_q(0, 0, kv)
                for kv in range(NKV):
                    load_k(k_main, kmain_in, 0, kv)
                    load_q(0, 1, kv)
                sp.wait_ge(s["pads"], 4)
                put_negmax(0, 0)
                with sp.Fori(0, B - 1) as b:
                    batch(b, False)
                batch(B - 1, True)

            @block.tensor
            def _(pe):
                def maximum(b, h, m):
                    count = b * (2 * MAXES) + h * MAXES + m
                    if m % KV_MAXES == 0:
                        pe.wait_ge(q_in[h][m // KV_MAXES], b * 64 + 64)
                        if h == 0:
                            pe.wait_ge(kmax_in[m // KV_MAXES], b * 64 + 64)
                    ge(pe, s["maxed"], count - 1)
                    if m == 0:
                        ge(pe, s["t_low"], b * 2 + h)
                    head, qt = m // QT, m % QT
                    for half in range(2):
                        last = nc.tensor.matmul(mx_ps[m % 2][:, half * 512:(half + 1) * 512],
                                                q_stack[h][0:ROWS, head, qt * P:(qt + 1) * P],
                                                k_max[:, head // GROUPS, half * 512:(half + 1) * 512],
                                                start=True, stop=True)
                    last.then_inc(s["max_scored"], 1)

                def turn_maxima(b, h):
                    pe.wait_ge(s["maxed"], b * (2 * MAXES) + (h + 1) * MAXES)
                    for qt in range(QT):
                        last = nc.tensor.transpose(mx_ps[0][0:HEADS, qt * P:(qt + 1) * P], negmax[h][:, qt, :],
                                                   core.ident[:, :])
                    last.then_inc(s["turned"], 1)

                def weigh(b, h, step):
                    kv, kt = step // KT, step % KT
                    n0 = b * (2 * 4 * STEPS) + h * (4 * STEPS) + 4 * step
                    if kt == 0 and h == 0:
                        pe.wait_ge(s["v_in"], b * NKV + (kv + 1))
                    if kt == 0:
                        ge(pe, s["o_kept"], b * (2 * NKV) + h * NKV + kv)
                    for g in range(GROUPS):
                        pe.wait_ge(s["expd"], n0 + (g + 1))
                        last = nc.tensor.matmul(o_ps[32 * g:32 * g + 32, :], v_now[:, kt, kv, :],
                                                probs[(4 * step + g) % 8][:, :], start=(kt == 0), stop=(kt == KT - 1),
                                                tile_position=(0, 32 * g))
                    last.then_inc(s["weighted"], 1)

                def unit(b, h, last_unit):
                    nb, nh = (b, 1) if h == 0 else (b + 1, 0)
                    pe.wait_ge(s[f"neg_in{h}"], b * 16 + 16)
                    for step in range(STEPS):
                        kv, kt = step // KT, step % KT
                        maxes = [] if last_unit else list(max_steps(step))
                        if kt == 0 and h == 0:
                            pe.wait_ge(kmain_in[kv], b * 64 + 64)
                        for g in range(GROUPS):
                            if g == 2 and maxes:
                                maximum(nb, nh, maxes.pop(0))
                            n = 4 * step + g
                            count = b * (2 * 4 * STEPS) + h * (4 * STEPS) + n
                            ge(pe, s["expd"], count - (1 if n < 2 else 2))
                            nc.tensor.matmul(st_ps[n % 3][:, :],
                                             k_main[:, kv, kt * P:(kt + 1) * P],
                                             q_stack[h][:, kv * GROUPS + g, :], start=True, stop=True)\
                                .then_inc(s["scored"], 1)
                        if maxes:
                            maximum(nb, nh, maxes.pop(0))
                        if step >= 1:
                            weigh(b, h, step - 1)
                        for m in maxes:
                            maximum(nb, nh, m)
                        if step == END and not last_unit:
                            turn_maxima(nb, nh)
                    weigh(b, h, STEPS - 1)

                pe.wait_ge(s["pads"], 4)
                for m in range(MAXES):
                    maximum(0, 0, m)
                turn_maxima(0, 0)

                def batch(b, last):
                    unit(b, 0, False)
                    unit(b, 1, last)
                batch(0, False)
                with pe.Fori(1, B - 1) as b:
                    batch(b, False)
                batch(B - 1, True)

            @block.scalar
            def _(act):
                def unit(b, h):
                    for step in range(STEPS):
                        for g in range(GROUPS):
                            n = 4 * step + g
                            count = b * (2 * 4 * STEPS) + h * (4 * STEPS) + n
                            act.wait_ge(s["scored"], count + 1)
                            if g == 0:
                                ge(act, s["weighted"], b * (2 * STEPS) + h * STEPS + step - 1)
                            nc.scalar.activation(probs[n % 8][:, :], st_ps[n % 3][:, :], ACT.Exp, scale=0.25)\
                                .then_inc(s["expd"], 1)

                def batch(b):
                    unit(b, 0)
                    unit(b, 1)
                batch(0)
                with act.Fori(1, B) as b:
                    batch(b)

            @block.vector
            def _(dve):
                def maximum(b, h, m):
                    dve.wait_ge(s["max_scored"], b * (2 * MAXES) + h * MAXES + (m + 1))
                    nc.vector.tensor_reduce(negmax[h][:, m % QT, m // QT:m // QT + 1], mx_ps[m % 2][:, :], AX.X,
                                            ALU.max, negate=True).then_inc(s["maxed"], 1)

                def maxima_parts(b, h):
                    unit = b * 2 + h
                    dve.wait_ge(s["turned"], unit + 1)
                    ge(dve, s["neg_out"], unit * 32)
                    nc.vector.tensor_copy(turned_high[:, :], mx_ps[0][0:HEADS, 0:QU]).then_inc(s["t_high"], 1)
                    dve.wait_ge(s["t_high"], unit + 1)
                    nc.vector.tensor_tensor(turned_low[:, :], mx_ps[0][0:HEADS, 0:QU],
                                            turned_high[:, :].bitcast(F32), ALU.subtract).then_inc(s["t_low"], 1)

                def keep_o(b, h, kv):
                    done = b * (2 * NKV) + h * NKV + kv
                    dve.wait_ge(s["weighted"], b * (2 * STEPS) + h * STEPS + (kv + 1) * KT)
                    ge(dve, s[f"o_out{kv % 2}"], (b * NKV + h * (NKV // 2) + kv // 2) * 16)
                    nc.vector.tensor_copy(o_sb[kv % 2][:, :], o_ps[:, :]).then_inc(s["o_kept"], 1)

                def unit(b, h, last_unit):
                    nb, nh = (b, 1) if h == 0 else (b + 1, 0)
                    for step in range(STEPS):
                        if step >= 1 and step % KT == 0:
                            keep_o(b, h, step // KT - 1)
                        if not last_unit:
                            for m in max_steps(step):
                                maximum(nb, nh, m)
                            if step == END:
                                maxima_parts(nb, nh)
                    keep_o(b, h, NKV - 1)

                for m in range(MAXES):
                    maximum(0, 0, m)
                maxima_parts(0, 0)

                def batch(b, last):
                    unit(b, 0, False)
                    unit(b, 1, last)
                batch(0, False)
                with dve.Fori(1, B - 1) as b:
                    batch(b, False)
                batch(B - 1, True)


def attention_normalised(core, o_dram):
    nc = core.nc
    U = 2 * B
    with Phase(nc, "an") as ph:
        o_in = [ph.sb(f"o_in{j}", [P, 512]) for j in range(NKV)]
        recip = [ph.sb(f"recip{j}", [P, 4, GROUPS]) for j in range(NKV)]
        turn_ps = [ph.ps() for j in range(NKV)]
        loaded = [ph.sem(f"loaded{j}") for j in range(NKV)]
        s = {n: ph.sem(n) for n in ("turned", "recip_done", "done")}
        with ph.block() as block:
            @block.sync
            def _(sp):
                def unit(u, _):
                    for kv in range(NKV):
                        ge(sp, s["turned"], u * NKV + (kv - NKV + 1))
                        sp.dma_start(o_in[kv][:, :], o_dram[u, kv, :, :]).then_inc(loaded[kv], 16)
                tiles(sp, U, 1, unit)

            @block.tensor
            def _(pe):
                def unit(u, _):
                    for kv in range(NKV):
                        pe.wait_ge(loaded[kv], u * 16 + 16)
                        ge(pe, s["done"], u * NKV + (kv - NKV + 1))
                        for qt in range(4):
                            last = nc.tensor.transpose(turn_ps[kv][:, qt * P:(qt + 1) * P],
                                                       o_in[kv][:, qt * P:(qt + 1) * P], core.ident[:, :])
                        last.then_inc(s["turned"], 1)
                tiles(pe, U, 1, unit)

            @block.vector
            def _(dve):
                def unit(u, _):
                    for kv in range(NKV):
                        dve.wait_ge(s["turned"], u * NKV + (kv + 1))
                        ps = turn_ps[kv][:, :].rearrange("p (q g c) -> p q g c", q=4, g=GROUPS)
                        nc.vector.reciprocal(recip[kv][:, :, :], ps[:, :, :, DH]).then_inc(s["recip_done"], 1)
                        dve.wait_ge(s["recip_done"], u * NKV + (kv + 1))
                        nc.vector.tensor_tensor(
                            core.y[:, bass.ds(u * 4, 4), kv * 64:(kv + 1) * 64]
                            .rearrange("p q (g d) -> p q g d", g=GROUPS),
                            ps[:, :, :, 0:DH], recip[kv][:, :, :].unsqueeze(3).to_broadcast([P, 4, GROUPS, DH]),
                            ALU.mult).then_inc(s["done"], 1)
                tiles(dve, U, 1, unit)
                dve.wait_ge(s["done"], U * NKV)


F16 = mybir.dt.float16
E = 8
SLOT_TILES = 2 * T + E
W_SCALE = 64.0
H_SCALE = 16.0


def split_scaled(core, name, parts):
    nc = core.nc
    with Phase(nc, name) as ph:
        stage = ph.sb("stage", [P, 2, 2048])
        loaded = [ph.sem("loaded0"), ph.sem("loaded1")]
        high_done, low_done = ph.sem("high_done"), ph.sem("low_done")

        def staged(i):
            src = parts[i][0]
            flat = stage[0:src.shape[0], i % 2, 0:src.shape[1] * (src.shape[2] if len(src.shape) == 3 else 1)]
            return flat.rearrange("p (k f) -> p k f", k=src.shape[1]) if len(src.shape) == 3 else flat

        with ph.block() as block:
            @block.sync
            def _(sp):
                for i, (src, _, _) in enumerate(parts):
                    ge(sp, low_done, i - 1)
                    sp.dma_start(staged(i), src).then_inc(loaded[i % 2], 16)

            @block.scalar
            def _(act):
                for i, (_, high, _) in enumerate(parts):
                    act.wait_ge(loaded[i % 2], 16 * (i // 2 + 1))
                    nc.scalar.activation(high, staged(i), ACT.Copy, scale=W_SCALE).then_inc(high_done, 1)

            @block.vector
            def _(dve):
                for i, (_, high, low) in enumerate(parts):
                    dve.wait_ge(high_done, i + 1)
                    nc.vector.scalar_tensor_tensor(out=low, in0=staged(i), scalar=W_SCALE, in1=high,
                                                   op0=ALU.mult, op1=ALU.subtract).then_inc(low_done, 1)


class Weights:

    def __init__(self, ph, n, F):
        self.n, self.F, self.KF = n, F, -(-F // P)
        self.up = [ph.sb(f"up_{x}", [P, n, KD, 2 * F], F16) for x in ("high", "low")]
        self.down = [ph.sb(f"down_{x}", [P, n, self.KF, D], F16) for x in ("high", "low")]

    def rows(self, k):
        return min(P, self.F - k * P)

    PARTS = 4
    PART = 1024

    def part_shape(self, u):
        if u < 2:
            return P, 2 * self.F
        whole = self.KF // 2
        return (P, whole * D) if u == 2 or self.F % P == 0 else (self.F % P, (self.KF - whole) * D)

    def part_source(self, up_dram, down_dram, e, u):
        if u < 2:
            return up_dram[e, u * P:(u + 1) * P, :].unsqueeze(1)
        rows = self.KF // 2 * P
        source = down_dram[e, 0:rows, :] if u == 2 else down_dram[e, rows:self.F, :]
        return source.rearrange("(k p) d -> p k d", p=self.part_shape(u)[0])

    def part(self, half, e, u):
        if u < 2:
            return self.up[half][:, bass.ds(e, 1), u, :].rearrange("p e f -> p (e f)")
        at = slice(0, self.KF // 2) if u == 2 else slice(self.KF // 2, self.KF)
        return self.down[half][0:self.part_shape(u)[0], bass.ds(e, 1), at, :].rearrange("p e k d -> p (e k d)")

    def parts(self, up_dram, down_dram):
        F = self.F
        out = []
        for e in range(self.n):
            up = up_dram[e, :, :].rearrange("(k p) f -> p k f", p=P)
            out.append((up, self.up[0][:, e, :, :], self.up[1][:, e, :, :]))
            whole = F // P
            out.append((down_dram[e, 0:whole * P, :].rearrange("(k p) d -> p k d", p=P),
                        self.down[0][:, e, 0:whole, :], self.down[1][:, e, 0:whole, :]))
            if F % P:
                r = F % P
                out.append((down_dram[e, whole * P:F, :], self.down[0][0:r, e, whole, :],
                            self.down[1][0:r, e, whole, :]))
        return out


def feed_forward(core, name, n, w, x_rows, y_rows=None, expert_of=None, slots=None, w_next=None, next_dram=None):
    nc = core.nc
    F, KF = w.F, w.KF
    shared = expert_of is None
    UNROLL = T // E if shared else 2
    TURNS = n // UNROLL
    PEELED = 1 if shared else 2
    flat_rows = x_rows.rearrange("j p d -> (j p) d")
    with Phase(nc, name) as ph:
        x_in = [ph.sb(f"x_in{j}", [P, D]) for j in range(2)]
        xt = [[ph.sb(f"xt_{x}{j}", [P, KD, P], F16) for x in ("high", "low")] for j in range(2)]
        gate = [ph.sb(f"gate{j}", [P, F]) for j in range(2)]
        hidden = [ph.sb(f"hidden{j}", [P, F]) for j in range(2)]
        ht = [[ph.sb(f"ht_{x}{j}", [P, KF, P], F16) for x in ("high", "low")] for j in range(2)]
        y_sb = None if shared else [ph.sb(f"y_sb{j}", [P, D]) for j in range(2)]
        xt_ps = ph.ps()
        lin_ps = [ph.ps() for j in range(2)]
        gate_ps = ph.ps()
        ht_ps = ph.ps()
        y_ps = [ph.ps() for j in range(2)]
        s = {k: ph.sem(k) for k in ("x_ready", "x_turned", "xt_high", "xt_low", "gated", "lined", "silu_done",
                                    "hidden_done", "h_turned", "ht_high", "ht_low", "downed", "y_done")}
        if shared:
            stage = ph.sb("stage", [P, 2, Weights.PART])
            sent = [ph.sem("sent0"), ph.sem("sent1")]
            staged = [ph.sem("staged0"), ph.sem("staged1")]
            next_high, next_low = ph.sem("next_high"), ph.sem("next_low")
        else:
            x_loaded = [ph.sem("x_loaded0"), ph.sem("x_loaded1")]
            y_stored = [ph.sem("y_stored0"), ph.sem("y_stored1")]

        def staged_part(u):
            rows, cols = w_next.part_shape(u)
            return stage[0:rows, u % 2, 0:cols]

        def turns(eng, step):
            for k in range(PEELED):
                step(k)
            with eng.Fori(PEELED, TURNS - 1) as k:
                step(k)
            step(TURNS - 1)

        def blocks(ap):
            return ap.rearrange("p (k t) -> p k t", t=P)

        pieces = [(slice(0, F // P), P)] if F >= P else []
        if F % P:
            pieces.append((slice(F // P, KF), F % P))

        with ph.block() as block:
            @block.sync
            def _(sp):
                if shared:
                    for e in range(E):
                        for u in range(UNROLL):
                            ge(sp, next_low, e * UNROLL + u - 1)
                            source = w_next.part_source(*next_dram, e, u)
                            sp.dma_start(staged_part(u).rearrange("p (k f) -> p k f", k=source.shape[1]), source)\
                                .then_inc(staged[u % 2], 16)
                    return

                def load(i, j):
                    ge(sp, s["x_turned"], i - 1)
                    sp.dma_start(x_in[j][:, :], x_rows[i, :, :]).then_inc(x_loaded[j], 16)

                tiles(sp, n, 2, load)

            @block.gpsimd
            def _(pool):
                if shared:
                    for i in range(n):
                        pool.wait_ge(s["x_ready"], i + 1)
                        for c in range(2):
                            pool.indirect_dma_start(flat_rows,
                                                    bass.IndirectOffsetOnAxis(ap=slots[:, i, c:c + 1], axis=0),
                                                    x_in[i % 2][:, :], None).then_inc(sent[i % 2], 16)
                    for j in range(2):
                        pool.wait_ge(sent[j], n // 2 * 32)
                    return

                def store(i, j):
                    pool.wait_ge(s["y_done"], i + 1)
                    pool.dma_start(y_rows[i, :, :], y_sb[j][:, :]).then_inc(y_stored[j], 16)

                tiles(pool, n, 2, store)
                for j in range(2):
                    pool.wait_ge(y_stored[j], n // 2 * 16)

            @block.scalar
            def _(act):
                def high(i, j):
                    act.wait_ge(s["x_turned"], i + 1)
                    ge(act, s["lined"], i - 1)
                    nc.scalar.activation(xt[j][0][:, :, :], blocks(xt_ps[:, 0:D]), ACT.Copy).then_inc(s["xt_high"], 1)

                def silu(i, j):
                    act.wait_ge(s["gated"], i + 1)
                    ge(act, s["hidden_done"], i - 1)
                    nc.scalar.activation(gate[j][:, :], gate_ps[:, 0:F], ACT.Silu, scale=1.0 / W_SCALE)\
                        .then_inc(s["silu_done"], 1)

                def hidden_high(i, j):
                    act.wait_ge(s["h_turned"], i + 1)
                    ge(act, s["downed"], i - 1)
                    for at, rows in pieces:
                        last = nc.scalar.activation(ht[j][0][0:rows, at, :], blocks(ht_ps[0:rows, 0:KF * P])[:, at, :],
                                                    ACT.Copy)
                    last.then_inc(s["ht_high"], 1)

                def cut_high(k, u):
                    act.wait_ge(staged[u % 2], (k * 2 + (u // 2 + 1)) * 16)
                    nc.scalar.activation(w_next.part(0, k, u), staged_part(u), ACT.Copy, scale=W_SCALE)\
                        .then_inc(next_high, 1)

                def turn(k):
                    for u in range(UNROLL):
                        i, j = k * UNROLL + u, u % 2
                        silu(i, j)
                        if not (isinstance(i, int) and i == 0):
                            hidden_high(i - 1, 1 - j)
                        if not (isinstance(i, int) and i == n - 1):
                            high(i + 1, 1 - j)
                        if shared:
                            cut_high(k, u)
                high(0, 0)
                turns(act, turn)
                hidden_high(n - 1, 1)

            @block.vector
            def _(dve):
                def norm(i, j, before=0):
                    if shared:
                        ge(dve, s["x_turned"], i - 1)
                        ge(dve, sent[j], before * 32)
                        nc.vector.tensor_scalar(x_in[j][:, :], core.x[:, i, :], core.mean_var[:, i, 0:1],
                                                core.rstd[:, bass.ds(i, 1)], ALU.subtract, ALU.mult)\
                            .then_inc(s["x_ready"], 1)

                def low(i, j):
                    dve.wait_ge(s["xt_high"], i + 1)
                    ge(dve, s["lined"], i - 1)
                    nc.vector.tensor_tensor(xt[j][1][:, :, :], blocks(xt_ps[:, 0:D]), xt[j][0][:, :, :],
                                            ALU.subtract).then_inc(s["xt_low"], 1)

                def multiply(i, j):
                    dve.wait_ge(s["lined"], i + 1)
                    dve.wait_ge(s["silu_done"], i + 1)
                    ge(dve, s["h_turned"], i - 1)
                    nc.vector.scalar_tensor_tensor(out=hidden[j][:, :], in0=lin_ps[j][:, 0:F], scalar=H_SCALE / W_SCALE,
                                                   in1=gate[j][:, :], op0=ALU.mult, op1=ALU.mult)\
                        .then_inc(s["hidden_done"], 1)

                def hidden_low(i, j):
                    dve.wait_ge(s["ht_high"], i + 1)
                    ge(dve, s["downed"], i - 1)
                    for at, rows in pieces:
                        last = nc.vector.tensor_tensor(ht[j][1][0:rows, at, :], blocks(ht_ps[0:rows, 0:KF * P])[:, at, :],
                                                       ht[j][0][0:rows, at, :], ALU.subtract)
                    last.then_inc(s["ht_low"], 1)

                def finish(i, j, before):
                    dve.wait_ge(s["downed"], i + 1)
                    if shared:
                        out = core.y[:, i, :]
                    else:
                        ge(dve, y_stored[j], before * 16)
                        out = y_sb[j][:, :]
                    nc.vector.tensor_scalar(out, y_ps[j][:, 0:D], 1.0 / (H_SCALE * W_SCALE), None, ALU.mult)\
                        .then_inc(s["y_done"], 1)

                def cut_low(k, u):
                    dve.wait_ge(next_high, k * UNROLL + (u + 1))
                    nc.vector.scalar_tensor_tensor(out=w_next.part(1, k, u), in0=staged_part(u), scalar=W_SCALE,
                                                   in1=w_next.part(0, k, u), op0=ALU.mult, op1=ALU.subtract)\
                        .then_inc(next_low, 1)

                def turn(k):
                    for u in range(UNROLL):
                        i, j = k * UNROLL + u, u % 2
                        peeled = isinstance(i, int)
                        if not (peeled and i == 0):
                            hidden_low(i - 1, 1 - j)
                        if not (peeled and i == n - 1):
                            low(i + 1, 1 - j)
                        if not (peeled and i >= n - 2):
                            norm(i + 2, j, k * (UNROLL // 2) + (u // 2 + 1))
                        multiply(i, j)
                        if shared:
                            cut_low(k, u)
                        if not (peeled and i == 0):
                            finish(i - 1, 1 - j, k * (UNROLL // 2) + (u - 1) // 2)
                norm(0, 0)
                norm(1, 1)
                low(0, 0)
                turns(dve, turn)
                hidden_low(n - 1, 1)
                finish(n - 1, 1, n // 2 - 1)
                dve.wait_ge(s["y_done"], n)

            @block.tensor
            def _(pe):
                def turn(i, j, before):
                    if shared:
                        pe.wait_ge(s["x_ready"], i + 1)
                    else:
                        pe.wait_ge(x_loaded[j], before * 16 + 16)
                    ge(pe, s["xt_low"], i)
                    for k in range(KD):
                        last = nc.tensor.transpose(xt_ps[:, k * P:(k + 1) * P], x_in[j][:, k * P:(k + 1) * P],
                                                   core.ident[:, :])
                    last.then_inc(s["x_turned"], 1)
                def three(out, left, right, stop_at):
                    m = 0
                    for k in range(stop_at):
                        for a, b in ((0, 0), (1, 0), (0, 1)):
                            m += 1
                            last = nc.tensor.matmul(out, left(a, k), right(b, k), start=(m == 1), stop=(m == 3 * stop_at))
                    return last

                def experts(k):
                    if shared:
                        return [0] * (UNROLL + 1)
                    _, values = nc.values_load_multi_w_load_instructions(
                        expert_of[0:1, bass.ds(k, 1), 0:3].rearrange("p k c -> p (k c)"),
                        engines=(mybir.EngineType.PE,), min_val=0, max_val=E - 1)
                    return values

                def gate_up(i, j, e):
                    pe.wait_ge(s["xt_low"], i + 1)
                    ge(pe, s["silu_done"], i)
                    three(gate_ps[:, 0:F], lambda a, k: xt[j][a][:, k, :],
                          lambda b, k: w.up[b][:, e, k, F:2 * F], KD).then_inc(s["gated"], 1)

                def line_up(i, j, e):
                    ge(pe, s["hidden_done"], i - 1)
                    three(lin_ps[j][:, 0:F], lambda a, k: xt[j][a][:, k, :],
                          lambda b, k: w.up[b][:, e, k, 0:F], KD).then_inc(s["lined"], 1)

                def turn_hidden(i, j):
                    pe.wait_ge(s["hidden_done"], i + 1)
                    ge(pe, s["ht_low"], i)
                    for k in range(KF):
                        last = nc.tensor.transpose(ht_ps[0:w.rows(k), k * P:(k + 1) * P],
                                                   hidden[j][:, k * P:k * P + w.rows(k)], core.ident[:, :])
                    last.then_inc(s["h_turned"], 1)

                def down(i, j, e):
                    pe.wait_ge(s["ht_low"], i + 1)
                    ge(pe, s["y_done"], i - 1)
                    three(y_ps[j][:, 0:D], lambda a, k: ht[j][a][0:w.rows(k), k, :],
                          lambda b, k: w.down[b][0:w.rows(k), e, k, :], KF).then_inc(s["downed"], 1)

                def turn_of(k):
                    e = experts(k)
                    for u in range(UNROLL):
                        i, j = k * UNROLL + u, u % 2
                        peeled = isinstance(i, int)
                        gate_up(i, j, e[u + 1])
                        if not (peeled and i == 0):
                            turn_hidden(i - 1, 1 - j)
                        if not (peeled and i == n - 1):
                            turn(i + 1, 1 - j, k * (UNROLL // 2) + (u + 1) // 2)
                        line_up(i, j, e[u + 1])
                        if not (peeled and i == 0):
                            down(i - 1, 1 - j, e[u])
                        if peeled and i == n - 1:
                            turn_hidden(i, j)
                            down(i, j, e[u + 1])
                turn(0, 0, 0)
                turns(pe, turn_of)


class Routing:

    def __init__(self, ph):
        self.logits = ph.sb("logits", [P, T, E])
        self.slots = ph.sb("slots", [P, T, 2], I32)
        self.weights = ph.sb("weights", [P, T, 2])
        self.expert_of = ph.sb("expert_of", [P, SLOT_TILES // 2, 4], I32)


def route(core, name, r, normalise, bias_row):
    nc = core.nc
    with Phase(nc, name) as ph:
        bias = ph.sb("bias", [P, E])
        top = ph.sb("top", [P, T, 8])
        index = ph.sb("index", [P, T, 8], mybir.dt.uint32)
        index_f = ph.sb("index_f", [P, T, 2])
        expert_iota = ph.sb("expert_iota", [P, E])
        tile_iota = ph.sb("tile_iota", [P, SLOT_TILES])
        chosen = [ph.sb(f"chosen{c}", [P, T, E]) for c in range(2)]
        both = ph.sb("both", [P, T, E])
        before = ph.sb("before", [P, P])
        ones = ph.sb("ones", [P, P])
        total = ph.sb("total", [P, T, E])
        running = ph.sb("running", [P, T, E])
        count_i = ph.sb("count_i", [P, E], I32)
        n_tiles = ph.sb("n_tiles", [P, E])
        ends = ph.sb("ends", [P, E])
        starts = ph.sb("starts", [P, E])
        slot = ph.sb("slot", [P, T, E])
        picked = ph.sb("picked", [P, T, E])
        slot_f = ph.sb("slot_f", [P, T, 2])
        passed = ph.sb("passed", [P, SLOT_TILES, E])
        expert_f = ph.sb("expert_f", [P, SLOT_TILES])
        shifted = ph.sb("shifted", [P, T, E])
        expd = ph.sb("expd", [P, T, E])
        denom = ph.sb("denom", [P, T, E])
        sums = ph.sb("sums", [P, T])
        rank_ps, total_ps = ph.ps(), ph.ps()
        bias_in, masks, counted = ph.sem("bias_in"), ph.sem("masks"), ph.sem("counted")
        chain, exp_ready, exp_done, both_done = ph.sem("chain"), ph.sem("exp_ready"), ph.sem("exp_done"), ph.sem("both")

        with ph.block() as block:
            @block.sync
            def _(sp):
                if bias_row is not None:
                    sp.dma_start(bias[:, :], bias_row.to_broadcast([P, E])).then_inc(bias_in, 16)

            @block.gpsimd
            def _(pool):
                nc.gpsimd.memset(ones[:, :], 1.0).then_inc(masks, 1)
                nc.gpsimd.memset(before[:, :], 1.0).then_inc(masks, 1)
                nc.gpsimd.iota(expert_iota[:, :], pattern=[[1, E]], base=0, channel_multiplier=0,
                               allow_small_or_imprecise_dtypes=True).then_inc(masks, 1)
                nc.gpsimd.iota(tile_iota[:, :], pattern=[[1, SLOT_TILES]], base=0, channel_multiplier=0,
                               allow_small_or_imprecise_dtypes=True).then_inc(masks, 1)
                pool.wait_ge(masks, 4)
                nc.gpsimd.affine_select(out=before[:, :], in_=before[:, :], compare_op=ALU.is_gt, fill=0.0, base=0,
                                        pattern=[[1, P]], channel_multiplier=-1).then_inc(masks, 1)

            @block.tensor
            def _(pe):
                pe.wait_ge(masks, 5)
                pe.wait_ge(both_done, 1)
                flat = both[:, :, :].rearrange("p t e -> p (t e)")
                nc.tensor.matmul(rank_ps[:, 0:T * E], before[:, :], flat, start=True, stop=True)
                nc.tensor.matmul(total_ps[:, 0:T * E], ones[:, :], flat, start=True, stop=True).then_inc(counted, 1)

            @block.scalar
            def _(act):
                act.wait_ge(exp_ready, 1)
                nc.scalar.activation(expd[:, :, :], shifted[:, :, :], ACT.Exp).then_inc(exp_done, 1)

            @block.vector
            def _(dve):
                steps = [0]

                def then(ins):
                    steps[0] += 1
                    ins.then_inc(chain, 1)
                    dve.wait_ge(chain, steps[0])

                dve.wait_ge(masks, 5)
                if bias_row is not None:
                    dve.wait_ge(bias_in, 16)
                    then(nc.vector.tensor_tensor(r.logits[:, :, :], r.logits[:, :, :],
                                                 bias[:, :].unsqueeze(1).to_broadcast([P, T, E]), ALU.add))
                for t in range(T):
                    last = nc.vector.max(top[:, t, :], r.logits[:, t, :])
                then(last)
                for t in range(T):
                    last = nc.vector.max_index(index[:, t, :], top[:, t, :], r.logits[:, t, :])
                then(last)
                then(nc.vector.tensor_copy(index_f[:, :, :], index[:, :, 0:2]))
                for c in range(2):
                    last = nc.vector.tensor_tensor(chosen[c][:, :, :],
                                                   expert_iota[:, :].unsqueeze(1).to_broadcast([P, T, E]),
                                                   index_f[:, :, c:c + 1].to_broadcast([P, T, E]), ALU.is_equal)
                then(last)
                nc.vector.tensor_tensor(both[:, :, :], chosen[0][:, :, :], chosen[1][:, :, :], ALU.add)\
                    .then_inc(both_done, 1)

                if normalise:
                    nc.vector.tensor_scalar(shifted[:, :, :], top[:, :, :], -1.0, None, ALU.mult).then_inc(exp_ready, 1)
                    dve.wait_ge(exp_done, 1)
                    then(nc.vector.tensor_scalar(denom[:, :, 0:2], expd[:, :, 0:2], 1.0, None, ALU.add))
                    then(nc.vector.reciprocal(r.weights[:, :, :], denom[:, :, 0:2]))
                    then(nc.vector.tensor_tensor(sums[:, :], r.weights[:, :, 0], r.weights[:, :, 1], ALU.add))
                    then(nc.vector.reciprocal(sums[:, :], sums[:, :]))
                    then(nc.vector.tensor_tensor(r.weights[:, :, :], r.weights[:, :, :],
                                                 sums[:, :].unsqueeze(2).to_broadcast([P, T, 2]), ALU.mult))
                else:
                    nc.vector.tensor_tensor(shifted[:, :, :], top[:, :, :], top[:, :, 0:1].to_broadcast([P, T, E]),
                                            ALU.subtract).then_inc(exp_ready, 1)
                    dve.wait_ge(exp_done, 1)
                    then(nc.vector.tensor_reduce(sums[:, :], expd[:, :, :], AX.X, ALU.add))
                    then(nc.vector.reciprocal(sums[:, :], sums[:, :]))
                    then(nc.vector.tensor_tensor(r.weights[:, :, :], expd[:, :, 0:2],
                                                 sums[:, :].unsqueeze(2).to_broadcast([P, T, 2]), ALU.mult))

                dve.wait_ge(counted, 1)
                then(nc.vector.tensor_copy(total[:, :, :], total_ps[:, 0:T * E].rearrange("p (t e) -> p t e", e=E)))
                for e in range(E):
                    last = nc.vector.tensor_tensor_scan(running[:, :, e], ones[:, 0:T], total[:, :, e], 0.0,
                                                        ALU.mult, ALU.add)
                then(last)
                then(nc.vector.tensor_scalar(count_i[:, :], running[:, T - 1, :], float(P - 1), None, ALU.add))
                then(nc.vector.tensor_scalar(count_i[:, :], count_i[:, :], P.bit_length() - 1, None,
                                             ALU.arith_shift_right))
                then(nc.vector.tensor_copy(n_tiles[:, :], count_i[:, :]))
                then(nc.vector.tensor_tensor_scan(ends[:, :], ones[:, 0:E], n_tiles[:, :], 0.0, ALU.mult, ALU.add))
                then(nc.vector.tensor_tensor(starts[:, :], ends[:, :], n_tiles[:, :], ALU.subtract))
                then(nc.vector.tensor_tensor(slot[:, :, :], running[:, :, :], total[:, :, :], ALU.subtract))
                then(nc.vector.tensor_tensor(slot[:, :, :], rank_ps[:, 0:T * E].rearrange("p (t e) -> p t e", e=E),
                                             slot[:, :, :], ALU.add))
                then(nc.vector.tensor_scalar(starts[:, :], starts[:, :], float(P), None, ALU.mult))
                then(nc.vector.tensor_tensor(slot[:, :, :], slot[:, :, :],
                                             starts[:, :].unsqueeze(1).to_broadcast([P, T, E]), ALU.add))
                for c in range(2):
                    then(nc.vector.tensor_tensor(picked[:, :, :], chosen[c][:, :, :], slot[:, :, :], ALU.mult))
                    then(nc.vector.tensor_reduce(slot_f[:, :, c], picked[:, :, :], AX.X, ALU.add))
                then(nc.vector.tensor_copy(r.slots[:, :, :], slot_f[:, :, :]))
                then(nc.vector.tensor_tensor(passed[:, :, :], ends[:, :].unsqueeze(1).to_broadcast([P, SLOT_TILES, E]),
                                             tile_iota[:, :].unsqueeze(2).to_broadcast([P, SLOT_TILES, E]), ALU.is_le))
                then(nc.vector.tensor_reduce(expert_f[:, :], passed[:, :, :], AX.X, ALU.add))
                pairs = expert_f[:, :].rearrange("p (k c) -> p k c", c=2)
                nc.vector.tensor_scalar(r.expert_of[:, :, 1:3], pairs, float(E - 1), None, ALU.min)
                nc.vector.tensor_scalar(r.expert_of[:, 1:, 0], pairs[:, 0:SLOT_TILES // 2 - 1, 1], float(E - 1), None,
                                        ALU.min)
                then(nc.vector.tensor_scalar(r.expert_of[:, 0:1, 0], pairs[:, 0:1, 1], float(E - 1), None, ALU.min))


def router_logits(core, name, router, logits):
    nc = core.nc
    G = 2
    NG = T // G
    with Phase(nc, name) as ph:
        xhat = [ph.sb(f"xhat{j}", [P, G, D]) for j in range(2)]
        xt = [[ph.sb(f"xt_{x}{j}", [P, G * KD, P], F16) for x in ("high", "low")] for j in range(2)]
        turn_ps = [ph.ps() for j in range(2)]
        logit_ps = ph.ps()
        s = {n: ph.sem(n) for n in ("xhat_done", "turned", "high", "low", "logged", "kept")}
        with ph.block() as block:
            @block.tensor
            def _(pe):
                def turn(g, j):
                    pe.wait_ge(s["xhat_done"], g * G + G)
                    ge(pe, s["low"], g - 1)
                    for u in range(G):
                        for k in range(KD):
                            at = u * KD + k
                            last = nc.tensor.transpose(turn_ps[j][:, at * P:(at + 1) * P],
                                                       xhat[j][:, u, k * P:(k + 1) * P], core.ident[:, :])
                    last.then_inc(s["turned"], 1)

                def multiply(g, j):
                    pe.wait_ge(s["low"], g + 1)
                    for u in range(G):
                        n = 0
                        for k in range(KD):
                            for a in range(2):
                                for b in range(2):
                                    n += 1
                                    last = nc.tensor.matmul(logit_ps[:, bass.ds(g * (G * E) + u * E, E)],
                                                            xt[j][a][:, u * KD + k, :], router[b][:, k, :],
                                                            start=(n == 1), stop=(n == 4 * KD))
                    last.then_inc(s["logged"], 1)

                def pair(k, more=True):
                    turn(k * 2 + 1, 1)
                    multiply(k * 2, 0)
                    if more:
                        turn(k * 2 + 2, 0)
                    multiply(k * 2 + 1, 1)
                turn(0, 0)
                pair(0)
                with pe.Fori(1, NG // 2 - 1) as k:
                    pair(k)
                pair(NG // 2 - 1, more=False)

            @block.scalar
            def _(act):
                def high(g, j):
                    act.wait_ge(s["turned"], g + 1)
                    ge(act, s["logged"], g - 1)
                    nc.scalar.activation(xt[j][0][:, :, :], turn_ps[j][:, :].rearrange("p (k t) -> p k t", t=P),
                                         ACT.Copy).then_inc(s["high"], 1)
                tiles(act, NG, 2, high)

            @block.vector
            def _(dve):
                def norm(g, j):
                    ge(dve, s["turned"], g - 1)
                    for u in range(G):
                        nc.vector.tensor_scalar(xhat[j][:, u, :], core.x[:, g * G + u, :],
                                                core.mean_var[:, g * G + u, 0:1],
                                                core.rstd[:, bass.ds(g * G + u, 1)], ALU.subtract, ALU.mult)\
                            .then_inc(s["xhat_done"], 1)

                def low(g, j):
                    dve.wait_ge(s["high"], g + 1)
                    ge(dve, s["logged"], g - 1)
                    nc.vector.tensor_tensor(xt[j][1][:, :, :], turn_ps[j][:, :].rearrange("p (k t) -> p k t", t=P),
                                            xt[j][0][:, :, :], ALU.subtract).then_inc(s["low"], 1)
                norm(0, 0)
                norm(1, 1)
                low(0, 0)
                norm(2, 0)
                low(1, 1)
                with dve.Fori(1, NG // 2 - 1) as k:
                    norm(k * 2 + 1, 1)
                    low(k * 2, 0)
                    norm(k * 2 + 2, 0)
                    low(k * 2 + 1, 1)
                norm(NG - 1, 1)
                low(NG - 2, 0)
                low(NG - 1, 1)
                dve.wait_ge(s["logged"], NG)
                nc.vector.tensor_scalar(logits[:, :, :], logit_ps[:, 0:T * E].rearrange("p (t e) -> p t e", e=E),
                                        1.0 / W_SCALE, None, ALU.mult).then_inc(s["kept"], 1)
                dve.wait_ge(s["kept"], 1)


def mixture(core, nc, name, F, shared_F, normalise, router_dram, bias_row, up_s, down_s, up_r, down_r, x_rows, y_rows,
            out_dram=None):
    with Phase(nc, name) as ph:
        r = Routing(ph)
        w = Weights(ph, E, F)
        with Phase(nc, name + "s") as ps:
            w_shared = Weights(ps, 1, shared_F)
            with Phase(nc, name + "l") as pl:
                router = [pl.sb(f"router_{x}", [P, KD, E], F16) for x in ("high", "low")]
                split_scaled(core, name + "ws", w_shared.parts(up_s, down_s) +
                             [(router_dram.rearrange("(k p) e -> p k e", p=P), router[0][:, :, :], router[1][:, :, :])])
                router_logits(core, name + "rl", router, r.logits)
                route(core, name + "r", r, normalise, bias_row)
            feed_forward(core, name + "fs", T, w_shared, x_rows, slots=r.slots, w_next=w, next_dram=(up_r, down_r))
        feed_forward(core, name + "fx", SLOT_TILES, w, x_rows, y_rows=y_rows, expert_of=r.expert_of)
        residual(core, name + "g", gather=(r, y_rows), out_dram=out_dram)


def build(nc, a, out):
    ctx = ExitStack()
    with ctx:
        Phase.taken_semaphores = []
        core = Core(nc, ctx)
        constants(core)
        x_dram = a["L0_attn_x"].rearrange("b (u p) d -> b p u d", p=P)
        out_dram = out.rearrange("b (u p) d -> b p u d", p=P)
        x_rows = nc.dram_tensor("x_rows", (SLOT_TILES, P, D), F32, kind="Internal").ap()
        y_rows = nc.dram_tensor("y_rows", (SLOT_TILES, P, D), F32, kind="Internal").ap()
        x_statistics(core, x_dram)
        with Phase(nc, "w0") as ph:
            qkv_high = ph.sb("qkv_high", [P, KD, 3 * D], F32R)
            qkv_low = ph.sb("qkv_low", [P, KD, 3 * D], F32R)
            wo_high = ph.sb("wo_high", [P, KD, D], F32R)
            wo_low = ph.sb("wo_low", [P, KD, D], F32R)
            parts = []
            for k in range(KD):
                parts.append((a["qkv0"][k * P:(k + 1) * P, :], qkv_high[:, k, :], qkv_low[:, k, :]))
                parts.append((a["L0_attn_wo"][k * P:(k + 1) * P, :], wo_high[:, k, :], wo_low[:, k, :]))
            split_weights(core, "w0s", parts)
            linear_attention(core, qkv_high, qkv_low, a["bias_q0"], a["bias_kv0"], x_rows)
            residual(core, "wo0", project=(wo_high, wo_low, a["bias_o0"]))
        mixture(core, nc, "m0", 512, 512, True, a["router0"], a["bias_r0"], a["up0s"], a["down0s"], a["up0"],
                a["down0"], x_rows, y_rows)
        Phase.clear_semaphores(nc)
        second_attention(core, nc, a)
        Phase.clear_semaphores(nc)
        mixture(core, nc, "m1", 192, 384, False, a["router1"], None, a["up1s"], a["down1s"], a["up1"],
                a["down1"], x_rows, y_rows, out_dram=out_dram)


def second_attention(core, nc, a, out_dram=None):
    q_dram = nc.dram_tensor("q_scratch", (2, D, B * N), F32, kind="Internal").ap()
    k_dram = nc.dram_tensor("k_scratch", (2, NKV * DH, B * N), F32, kind="Internal").ap()
    o_dram = nc.dram_tensor("o_scratch", (2 * B, NKV, P, N // 2), F32, kind="Internal").ap()
    negmax_dram = nc.dram_tensor("negmax_scratch", (2 * B, 2, HEADS, N // 2), F32, kind="Internal").ap()
    with Phase(nc, "v") as ph:
        v_all = ph.sb("v_all", [P, T, NKV, 32])
        with Phase(nc, "w2") as pw:
            high = pw.sb("high", [P, KD, 3 * P], F32R)
            low = pw.sb("low", [P, KD, 3 * P], F32R)
            split_weights(core, "w2s", [(a["qkv1"][k * P:(k + 1) * P, :], high[:, k, :], low[:, k, :])
                                        for k in range(KD)])
            attention_projections(core, high, low, a["bias_qkv1"], q_dram, k_dram, v_all)
        softmax_attention(core, q_dram, k_dram, v_all, negmax_dram,
                          o_dram.rearrange("(b h) k p t -> b h k p t", h=2))
    attention_normalised(core, o_dram)
    with Phase(nc, "w3") as pw:
        high = pw.sb("high", [P, KD, D], F32R)
        low = pw.sb("low", [P, KD, D], F32R)
        split_weights(core, "w3s", [(a["wo1"][k * P:(k + 1) * P, :], high[:, k, :], low[:, k, :])
                                    for k in range(KD)])
        residual(core, "wo1", project=(high, low, a["bias_o1"]), out_dram=out_dram)


def kernel(**inputs):
    import numpy as _np
    import concourse.bacc as _bacc
    from concourse import mybir as _mybir
    from concourse.bass_utils import run_bass_kernel_spmd as _run

    given = {k: _np.asarray(v) for k, v in inputs.items()}
    laid = {
        "L0_attn_x": given["L0_attn_x"],
        "qkv0": _np.concatenate([given["L0_attn_wq"], given["L0_attn_wk"], given["L0_attn_wv"]], axis=1),
        "bias_q0": given["L0_attn_bq"].reshape(KD, P).T,
        "bias_kv0": _np.concatenate([given["L0_attn_bk"], given["L0_attn_bv"]])[None, :],
        "L0_attn_wo": given["L0_attn_wo"],
        "bias_o0": given["L0_attn_bo"][None, :],
        "qkv1": _np.concatenate([given["L1_attn_Wq"], given["L1_attn_Wk"], given["L1_attn_Wv"]], axis=1),
        "bias_qkv1": _np.concatenate([given["L1_attn_bq"], given["L1_attn_bk"], given["L1_attn_bv"]])
        .reshape(3, P).T,
        "wo1": given["L1_attn_Wo"].reshape(GROUPS, NKV, DH, D).transpose(1, 0, 2, 3).reshape(D, D),
        "bias_o1": given["L1_attn_bo"][None, :],
        "router0": given["L0_ffn_router_w"].T,
        "bias_r0": given["L0_ffn_routing_bias"][None, :],
        "up0s": _np.concatenate([given["L0_ffn_su_w"], given["L0_ffn_sg_w"]], axis=0).T[None],
        "down0s": given["L0_ffn_sd_w"].T[None],
        "up0": _np.concatenate([given["L0_ffn_wu"], given["L0_ffn_wg"]], axis=1).transpose(0, 2, 1),
        "down0": given["L0_ffn_wd"].transpose(0, 2, 1),
        "router1": given["L1_ffn_gate_w"].T,
        "up1s": given["L1_ffn_Ws1"].T[None],
        "down1s": given["L1_ffn_Ws2"].T[None],
        "up1": given["L1_ffn_W1"].transpose(0, 2, 1),
        "down1": given["L1_ffn_W2"].transpose(0, 2, 1),
    }
    nc = _bacc.Bacc("TRN2", target_bir_lowering=False, num_devices=1)
    arrays, args = {}, {}
    for name, v in laid.items():
        v = _np.ascontiguousarray(v)
        arrays[f"in_{name}"] = v
        args[name] = nc.dram_tensor(f"in_{name}", v.shape, _mybir.dt.from_np(v.dtype), kind="ExternalInput").ap()
    out = nc.dram_tensor("out_x", (B, N, D), _mybir.dt.float32, kind="ExternalOutput").ap()
    build(nc, args, out)
    return _run(nc, [arrays], core_ids=[0]).results[0]["out_x"]
```

```python
import concourse.bass as bass
from concourse import mybir
from contextlib import ExitStack, contextmanager

F32 = mybir.dt.float32
F32R = mybir.dt.float32r
BF16 = mybir.dt.bfloat16
I32 = mybir.dt.int32
ALU = mybir.AluOpType
ACT = mybir.ActivationFunctionType
AX = mybir.AxisListType

P = 128
B, N, D = 4, 1024, 256
T = B * N // P
TB = N // P
KD = D // P
EPS = 1e-5
HEADS, DH = 16, 16
HPB = P // DH
NKV, GROUPS = 4, 4


def ge(eng, sem, value):
    if not (isinstance(value, int) and value <= 0):
        eng.wait_ge(sem, value)


def tiles(eng, n, unroll, step):
    for u in range(unroll):
        step(u, u)
    if n > unroll:
        with eng.Fori(1, n // unroll) as k:
            for u in range(unroll):
                step(k * unroll + u, u)


class Core:

    def __init__(self, nc, ctx):
        self.nc = nc
        self.x = ctx.enter_context(nc.sbuf_tensor("x", [P, T, D], F32))
        self.y = ctx.enter_context(nc.sbuf_tensor("y", [P, T, D], F32))
        self.mean_var = ctx.enter_context(nc.sbuf_tensor("mean_var", [P, T, 2], F32))
        self.rstd = ctx.enter_context(nc.sbuf_tensor("rstd", [P, T], F32))
        self.minus_half = ctx.enter_context(nc.sbuf_tensor("minus_half", [P, T], F32))
        self.ident = ctx.enter_context(nc.sbuf_tensor("ident", [P, P], F32))
        Phase.psum = ctx.enter_context(nc.psum_tensor("psum", [P, 8 * 512], F32))


class Phase:

    def __init__(self, nc, name):
        self.nc, self.name, self.ctx, self.next_bank = nc, name, ExitStack(), 0

    def __enter__(self):
        return self

    def __exit__(self, *e):
        self.ctx.close()

    def sb(self, name, shape, dt=F32):
        return self.ctx.enter_context(self.nc.sbuf_tensor(f"{self.name}_{name}", shape, dt))

    def ps(self, banks=1):
        first, self.next_bank = self.next_bank, self.next_bank + banks
        return self.psum[:, first * 512:(first + banks) * 512]

    def sem(self, name):
        sem = self.nc.alloc_semaphore(f"{self.name}_{name}")
        self.taken_semaphores.append(sem)
        return sem

    taken_semaphores = []

    @classmethod
    def clear_semaphores(cls, nc):
        nc.all_engine_barrier()
        nc.clear_and_free_semaphores(cls.taken_semaphores)
        nc.all_engine_barrier()
        cls.taken_semaphores = []

    def block(self):
        return self.nc.Block()


def constants(core):
    nc = core.nc
    with Phase(nc, "const") as ph:
        zeroed = ph.sem("zeroed")
        with ph.block() as block:
            @block.gpsimd
            def _(pool):
                nc.gpsimd.memset(core.minus_half[:, :], -0.5)
                nc.gpsimd.memset(core.ident[:, :], 0.0).then_inc(zeroed, 1)
                pool.wait_ge(zeroed, 1)
                nc.gpsimd.affine_select(out=core.ident[:, :], in_=core.ident[:, :], compare_op=ALU.not_equal,
                                        fill=1.0, base=0, pattern=[[-1, P]], channel_multiplier=1).then_inc(zeroed, 1)
                pool.wait_ge(zeroed, 2)


def split_weights(core, name, parts):
    nc = core.nc
    with Phase(nc, name) as ph:
        stage = ph.sb("stage", [P, 2, 2048])
        loaded = [ph.sem("loaded0"), ph.sem("loaded1")]
        high_done, low_done = ph.sem("high_done"), ph.sem("low_done")

        def staged(i):
            src = parts[i][0]
            return stage[0:src.shape[0], i % 2, 0:src.shape[1]]

        with ph.block() as block:
            @block.sync
            def _(sp):
                for i, (src, _, _) in enumerate(parts):
                    ge(sp, low_done, i - 1)
                    sp.dma_start(staged(i), src).then_inc(loaded[i % 2], 16)

            @block.scalar
            def _(act):
                for i, (_, high, _) in enumerate(parts):
                    act.wait_ge(loaded[i % 2], 16 * (i // 2 + 1))
                    nc.scalar.activation(high, staged(i), ACT.Copy).then_inc(high_done, 1)

            @block.vector
            def _(dve):
                for i, (_, high, low) in enumerate(parts):
                    dve.wait_ge(high_done, i + 1)
                    nc.vector.tensor_tensor(low, staged(i), high.bitcast(F32), ALU.subtract).then_inc(low_done, 1)


class Stats:

    def __init__(self, ph, name):
        self.nc = ph.nc
        self.halves = ph.sb(f"{name}_halves", [P, T, 6])
        self.spread = ph.sb(f"{name}_spread", [P, T])
        self.var = ph.sb(f"{name}_var", [P, T])
        self.summed = ph.sem(f"{name}_summed")
        self.mean_done = ph.sem(f"{name}_mean_done")
        self.var_done = ph.sem(f"{name}_var_done")

    def aggregate(self, dve, at, n, times, mean, factor):
        nc = self.nc
        halves = self.halves[:, bass.ds(at, n), :]
        spread, var = self.spread[:, bass.ds(at, n)], self.var[:, bass.ds(at, n)]
        nc.vector.tensor_tensor(spread, halves[:, :, 1], halves[:, :, 4], ALU.subtract)
        nc.vector.tensor_tensor(mean, halves[:, :, 1], halves[:, :, 4], ALU.add)
        nc.vector.tensor_tensor(var, halves[:, :, 2], halves[:, :, 5], ALU.add).then_inc(self.summed, 1)
        dve.wait_ge(self.summed, times * 2 + 1)
        nc.vector.tensor_scalar(mean, mean, factor, None, ALU.mult).then_inc(self.mean_done, 1)
        nc.vector.scalar_tensor_tensor(out=spread, in0=spread, scalar=0.25, in1=spread, op0=ALU.mult,
                                       op1=ALU.mult).then_inc(self.summed, 1)
        dve.wait_ge(self.summed, times * 2 + 2)
        nc.vector.scalar_tensor_tensor(out=var, in0=var, scalar=1.0 / D, in1=spread, op0=ALU.mult, op1=ALU.add)\
            .then_inc(self.var_done, 1)

    def rstd(self, pool, out, at, n, times, minus_half, eps_added, done):
        nc = self.nc
        var = self.var[:, bass.ds(at, n)]
        pool.wait_ge(self.var_done, times + 1)
        nc.gpsimd.tensor_scalar(var, var, EPS, 1.0, ALU.add, ALU.mult).then_inc(eps_added, 1)
        pool.wait_ge(eps_added, times + 1)
        nc.gpsimd.tensor_tensor(out, var, minus_half, ALU.pow).then_inc(done, 1)


def x_statistics(core, x_dram):
    nc = core.nc
    with Phase(nc, "in") as ph:
        stats = Stats(ph, "x")
        x_in = [ph.sem(f"x_in{b}") for b in range(B)]
        x_stats, eps_added, rstd_done = ph.sem("x_stats"), ph.sem("eps_added"), ph.sem("rstd_done")
        with ph.block() as block:
            @block.sync
            def _(sp):
                for b in range(B):
                    sp.dma_start(core.x[:, b * TB:(b + 1) * TB, :], x_dram[b, :, :, :]).then_inc(x_in[b], 16)

            @block.vector
            def _(dve):
                for b in range(B):
                    dve.wait_ge(x_in[b], 16)
                    for i in range(b * TB, (b + 1) * TB):
                        nc.vector.bn_stats(stats.halves[:, i, :], core.x[:, i, :]).then_inc(x_stats, 1)
                dve.wait_ge(x_stats, T)
                stats.aggregate(dve, 0, T, 0, core.mean_var[:, :, 0], 0.5)

            @block.gpsimd
            def _(pool):
                stats.rstd(pool, core.rstd[:, :], 0, T, 0, core.minus_half[:, :], eps_added, rstd_done)


def residual(core, name, gather=None, project=None, out_dram=None, follow=None):
    nc = core.nc
    G = 4
    NG = T // G
    LAG = 3
    with Phase(nc, name) as ph:
        y_stats_of, x_stats_of = Stats(ph, "y"), Stats(ph, "x")
        neg_mean = ph.sb("neg_mean", [P, T])
        rstd_y = ph.sb("rstd_y", [P, T])
        y_eps, x_eps, rstd_y_done, rstd_x_done = (ph.sem(n) for n in ("y_eps", "x_eps", "rstd_y_done", "rstd_x_done"))
        y_stats, x_stats, centred, x_ready = (ph.sem(n) for n in ("y_stats", "x_stats", "centred", "x_ready"))
        if gather is not None:
            r, y_rows = gather
            rows = y_rows.rearrange("j p d -> (j p) d")
            got = ph.sb("got", [P, 2, G, 2, D])
            came = [[ph.sem(f"came{j}{t}") for t in range(G)] for j in range(2)]
            first_added, added = ph.sem("first_added"), ph.sem("added")
        if project is not None:
            wo_high, wo_low, bias_row = project
            at_high = [ph.sb(f"at_high{j}", [P, KD, P], F32R) for j in range(G)]
            at_low = [ph.sb(f"at_low{j}", [P, KD, P], F32R) for j in range(G)]
            bias = ph.sb("bias", [1, D])
            bias_parts = [ph.sb(f"bias_{x}", [1, D], F32R) for x in ("high", "low")]
            ones = ph.sb("ones", [1, P])
            ones_r = ph.sb("ones_r", [1, P], F32R)
            turn_ps = [ph.ps() for j in range(G)]
            out_ps = [ph.ps() for j in range(G)]
            bias_in, ones_set, bias_high, bias_low, ones_kept = (
                ph.sem(n) for n in ("bias_in", "ones_set", "bias_high", "bias_low", "ones_kept"))
            turned, high, low, projected, kept = (ph.sem(n) for n in ("turned", "high", "low", "projected", "kept"))
        if out_dram is not None:
            stored = ph.sem("stored")
        follower = follow(ph) if follow is not None else None
        STEPS = NG + 2 if follower is None else NG + LAG + 1
        WHOLE = 2

        before_of = {}

        def steps(eng, step):
            if follower is not None:
                for g in range(STEPS):
                    step(g, g % 2)
                return
            for g in range(WHOLE):
                step(g, g % 2)
            with eng.Fori(WHOLE // 2, NG // 2 - (1 if project is not None else 0)) as k:
                before_of["k"] = k
                for j in range(2):
                    step(k * 2 + j, j)
            for g in range(NG - (2 if project is not None else 0), STEPS):
                step(g, g % 2)

        with ph.block() as block:
            @block.sync
            def _(sp):
                if project is not None:
                    sp.dma_start(bias[:, :], bias_row).then_inc(bias_in, 16)
                if follower is not None:
                    follower.sync_begin(sp)
                    follower.sync_all(sp)
                if out_dram is not None:
                    for b in range(B):
                        sp.wait_ge(x_ready, (b + 1) * TB)
                        sp.dma_start(out_dram[b, :, :, :], core.x[:, b * TB:(b + 1) * TB, :]).then_inc(stored, 16)
                    sp.wait_ge(stored, 16 * B)

            @block.gpsimd
            def _(pool):
                if project is not None:
                    nc.gpsimd.memset(ones[:, :], 1.0).then_inc(ones_set, 1)
                if follower is not None:
                    follower.gpsimd_begin(pool)
                for g in range(NG + 2 if follower is None else NG + 3):
                    if gather is not None and g < NG:
                        ge(pool, added, (g - 1) * G)
                        for t in range(G):
                            for c in range(2):
                                pool.indirect_dma_start(
                                    got[:, g % 2, t, c, :], None, rows,
                                    bass.IndirectOffsetOnAxis(ap=r.slots[:, g * G + t, c:c + 1], axis=0))\
                                    .then_inc(came[g % 2][t], 16)
                    if follower is not None and g >= 3:
                        x_stats_of.rstd(pool, core.rstd[:, (g - 3) * G:(g - 2) * G], (g - 3) * G, G, g - 3,
                                        core.minus_half[:, 0:G], x_eps, rstd_x_done)
                    if 2 <= g < NG + 2:
                        y_stats_of.rstd(pool, rstd_y[:, (g - 2) * G:(g - 1) * G], (g - 2) * G, G, g - 2,
                                        core.minus_half[:, 0:G], y_eps, rstd_y_done)
                if out_dram is None and follower is None:
                    x_stats_of.rstd(pool, core.rstd[:, :], 0, T, 0, core.minus_half[:, :], x_eps, rstd_x_done)

            @block.tensor
            def _(pe):
                if follower is not None:
                    follower.tensor_all(pe)
                if project is None:
                    return
                pe.wait_ge(bias_low, 1)
                pe.wait_ge(ones_kept, 1)

                def turn(i, j):
                    ge(pe, low, i - G + 1)
                    for k in range(KD):
                        last = nc.tensor.transpose(turn_ps[j][:, k * P:(k + 1) * P],
                                                   core.y[:, i, k * P:(k + 1) * P], core.ident[:, :])
                    last.then_inc(turned, 1)

                def project_tile(i, j):
                    pe.wait_ge(low, i + 1)
                    ge(pe, kept, i - G + 1)
                    out = out_ps[j][:, 0:D]
                    for part in range(2):
                        nc.tensor.matmul(out, ones_r[:, :], bias_parts[part][:, :], start=(part == 0), stop=False)
                    n = 0
                    for k in range(KD):
                        for at, wt in ((at_high, wo_high), (at_low, wo_high), (at_high, wo_low)):
                            n += 1
                            last = nc.tensor.matmul(out, at[j][:, k, :], wt[:, k, :], start=False, stop=(n == 3 * KD))
                    last.then_inc(projected, 1)

                for i in range(T + 2):
                    if i < T:
                        turn(i, i % G)
                    if i >= 2:
                        project_tile(i - 2, (i - 2) % G)

            @block.scalar
            def _(act):
                if project is not None:
                    act.wait_ge(bias_in, 16)
                    nc.scalar.activation(bias_parts[0][:, :], bias[:, :], ACT.Copy).then_inc(bias_high, 1)
                    act.wait_ge(ones_set, 1)
                    nc.scalar.activation(ones_r[:, :], ones[:, :], ACT.Copy).then_inc(ones_kept, 1)

                def keep(i, j):
                    act.wait_ge(projected, i + 1)
                    nc.scalar.activation(core.y[:, i, :], out_ps[j][:, 0:D], ACT.Copy).then_inc(kept, 1)

                def step(g, j):
                    peeled = isinstance(g, int)
                    following = follower is not None and not (peeled and not LAG <= g < NG + LAG)
                    for t in range(G):
                        if project is not None and not (peeled and g >= NG):
                            i = g * G + t
                            act.wait_ge(turned, i + 1)
                            ge(act, projected, i - G + 1)
                            nc.scalar.activation(at_high[t][:, :, :],
                                                 turn_ps[t][:, 0:D].rearrange("p (k t) -> p k t", k=KD),
                                                 ACT.Copy).then_inc(high, 1)
                            if not (peeled and i < 2):
                                keep(i - 2, (t - 2) % G)
                            if peeled and i == T - 1:
                                keep(i - 1, t - 1)
                                keep(i, t)
                        if not (peeled and not 2 <= g < NG + 2):
                            act.wait_ge(y_stats_of.mean_done, g - 1)
                            i = (g - 2) * G + t
                            nc.scalar.activation(core.y[:, i, :], core.y[:, i, :], ACT.Identity,
                                                 bias=neg_mean[:, bass.ds(i, 1)]).then_inc(centred, 1)
                        if following:
                            follower.scalar_tile(act, g - LAG, (j - LAG) % 2, t)
                    if following:
                        follower.scalar_rest(act, g - LAG)
                steps(act, step)

            @block.vector
            def _(dve):
                if project is not None:
                    dve.wait_ge(bias_high, 1)
                    nc.vector.tensor_tensor(bias_parts[1][:, :], bias[:, :], bias_parts[0][:, :].bitcast(F32),
                                            ALU.subtract).then_inc(bias_low, 1)

                def add_gathered(g, j, before):
                    for c, done in ((0, first_added), (1, added)):
                        for t in range(G):
                            i = g * G + t
                            if c == 0:
                                dve.wait_ge(came[j][t], before * 32 + 32)
                            else:
                                dve.wait_ge(first_added, i + 1)
                            nc.vector.scalar_tensor_tensor(out=core.y[:, i, :], in0=got[:, j, t, c, :],
                                                           scalar=r.weights[:, i, c:c + 1], in1=core.y[:, i, :],
                                                           op0=ALU.mult, op1=ALU.add).then_inc(done, 1)

                def lower(i, j):
                    dve.wait_ge(high, i + 1)
                    ge(dve, projected, i - G + 1)
                    nc.vector.tensor_tensor(at_low[j][:, :, :], turn_ps[j][:, 0:D].rearrange("p (k t) -> p k t", k=KD),
                                            at_high[j][:, :, :].bitcast(F32), ALU.subtract).then_inc(low, 1)

                def y_halves(i):
                    if gather is not None:
                        dve.wait_ge(added, i + 1)
                    if project is not None:
                        dve.wait_ge(kept, i + 1)
                    nc.vector.bn_stats(y_stats_of.halves[:, i, :], core.y[:, i, :]).then_inc(y_stats, 1)

                def add(i):
                    dve.wait_ge(centred, i + 1)
                    nc.vector.scalar_tensor_tensor(out=core.x[:, i, :], in0=core.y[:, i, :],
                                                   scalar=rstd_y[:, bass.ds(i, 1)], in1=core.x[:, i, :],
                                                   op0=ALU.mult, op1=ALU.add).then_inc(x_ready, 1)

                def x_halves(i):
                    if out_dram is None:
                        dve.wait_ge(x_ready, i + 1)
                        nc.vector.bn_stats(x_stats_of.halves[:, i, :], core.x[:, i, :]).then_inc(x_stats, 1)

                def step(g, j):
                    peeled = isinstance(g, int)
                    before = before_of["k"] if not peeled else g // 2
                    following = follower is not None and not (peeled and not LAG <= g < NG + LAG)
                    forming, counting, adding = (not (peeled and g >= NG), not (peeled and not 1 <= g <= NG),
                                                 not (peeled and not 2 <= g < NG + 2))
                    if forming and gather is not None:
                        add_gathered(g, j, before)
                    if follower is not None and not (peeled and g < LAG + 1):
                        follower.vector_rest(dve, g - LAG - 1)
                    if following:
                        dve.wait_ge(rstd_x_done, g - LAG + 1)
                        dve.wait_ge(x_stats_of.mean_done, g - LAG + 1)
                    for t in range(G):
                        if forming and project is not None:
                            lower(g * G + t, t)
                        if counting:
                            y_halves((g - 1) * G + t)
                        if adding:
                            if t == 0:
                                dve.wait_ge(rstd_y_done, g - 1)
                            add((g - 2) * G + t)
                            if t >= 1:
                                x_halves((g - 2) * G + t - 1)
                        if following:
                            follower.vector_tile(dve, g - LAG, (j - LAG) % 2, t)
                    if counting:
                        dve.wait_ge(y_stats, g * G)
                        y_stats_of.aggregate(dve, (g - 1) * G, G, g - 1, neg_mean[:, bass.ds((g - 1) * G, G)], -0.5)
                    if adding:
                        x_halves((g - 2) * G + G - 1)
                        if follower is not None:
                            dve.wait_ge(x_stats, (g - 1) * G)
                            x_stats_of.aggregate(dve, (g - 2) * G, G, g - 2,
                                                 core.mean_var[:, bass.ds((g - 2) * G, G), 0], 0.5)
                steps(dve, step)
                if out_dram is None and follower is None:
                    dve.wait_ge(x_stats, T)
                    x_stats_of.aggregate(dve, 0, T, 0, core.mean_var[:, :, 0], 0.5)


def linear_attention(core, qkv_high, qkv_low, bias_q_col, bias_kv_row, zero_dram):
    nc = core.nc
    G = 4
    GROUPS_B = TB // G
    with Phase(nc, "la") as ph:
        xhat = [ph.sb(f"xhat{j}", [P, D]) for j in range(2)]
        xt_high = [ph.sb(f"xt_high{h}", [P, KD, G * P], F32R) for h in range(GROUPS_B)]
        xt_low = [ph.sb(f"xt_low{h}", [P, KD, G * P], F32R) for h in range(GROUPS_B)]
        kv_lin = [ph.sb(f"kv_lin{j}", [P, 2 * KD, P + 1]) for j in range(2)]
        k_exp = [ph.sb(f"k_exp{j}", [P, KD, P]) for j in range(2)]
        k_relu = [ph.sb(f"k_relu{j}", [P, KD, P]) for j in range(2)]
        k_map = [ph.sb(f"k_map{j}", [P, KD, P]) for j in range(2)]
        q_exp = [ph.sb(f"q_exp{m}", [P, G * P]) for m in range(KD)]
        q_relu = [ph.sb(f"q_relu{m}", [P, G * P]) for m in range(KD)]
        qT = [ph.sb(f"qT{h}", [P, KD, G * P]) for h in range(GROUPS_B)]
        kv = ph.sb("kv", [P, KD, P + HPB])
        head_mask = ph.sb("head_mask", [P, P])
        zcol_mask = ph.sb("zcol_mask", [P, HPB])
        z = [ph.sb(f"z{j}", [P, HEADS]) for j in range(2)]
        bias_q = ph.sb("bias_q", [P, KD])
        bias_kv = ph.sb("bias_kv", [P, 2 * D])
        zeros = ph.sb("zeros", [P, 8 * D])

        turn_ps = [ph.ps() for j in range(2)]
        kv_proj_ps = [ph.ps() for j in range(2)]
        q_ps = [ph.ps() for m in range(KD)]
        kv_ps = ph.ps()
        num_ps = ph.ps()
        kv_sum = kv_ps[:, 0:KD * (P + 1)].rearrange("p (k c) -> p k c", k=KD)
        num = num_ps[:, 0:KD * (P + HPB)].rearrange("p (k c) -> p k c", k=KD)

        s = {n: ph.sem(n) for n in ("bias_in", "ones_set", "zeroed", "zeros_out", "masks", "xhat_done", "turned",
                                    "high", "low", "projected", "linear", "expd", "relud", "k_done", "summed",
                                    "kv_done", "q_projected", "q_expd", "q_relud", "q_done", "numer", "z_eps",
                                    "z_done", "y_done")}

        def real(i):
            return not isinstance(i, int) or 0 <= i < T

        def queries_before(b, w):
            return b * GROUPS_B + w // G - 1, (w // G - 1) % GROUPS_B

        def slots(eng, slot):
            def turn(b):
                for w in range(TB):
                    slot(b, w)
            turn(0)
            with eng.Fori(1, B - 1) as b:
                turn(b)
            turn(B - 1)
            turn(B)

        with ph.block() as block:
            @block.sync
            def _(sp):
                sp.dma_start(bias_q[:, :], bias_q_col).then_inc(s["bias_in"], 16)
                sp.dma_start(bias_kv[:, :], bias_kv_row.to_broadcast([P, 2 * D])).then_inc(s["bias_in"], 16)
                flat = zero_dram.rearrange("j p d -> (j p) d").rearrange("(p r) d -> p (r d)", p=P)
                sp.wait_ge(s["zeroed"], 1)
                for r in range(0, SLOT_TILES, 8):
                    sp.dma_start(flat[:, r * D:(r + 8) * D], zeros[:, :]).then_inc(s["zeros_out"], 16)
                sp.wait_ge(s["zeros_out"], SLOT_TILES // 8 * 16)

            @block.gpsimd
            def _(pool):
                for j in range(2):
                    nc.gpsimd.memset(kv_lin[j][:, :, P:P + 1], 1.0).then_inc(s["ones_set"], 1)
                nc.gpsimd.memset(head_mask[:, :], 1.0).then_inc(s["masks"], 1)
                nc.gpsimd.memset(zcol_mask[:, :], 1.0).then_inc(s["masks"], 1)
                done = 2
                for m, pattern in ((head_mask, [[DH, HPB], [0, DH]]), (zcol_mask, [[DH, HPB]])):
                    view = m[:, :].rearrange("p (h c) -> p h c", c=DH) if m is head_mask else m[:, :]
                    neg = [[-st, n] for st, n in pattern]
                    pool.wait_ge(s["masks"], done)
                    nc.gpsimd.affine_select(out=view, in_=view, compare_op=ALU.is_ge, fill=0.0, base=0,
                                            pattern=neg, channel_multiplier=1).then_inc(s["masks"], 1)
                    pool.wait_ge(s["masks"], done + 1)
                    nc.gpsimd.affine_select(out=view, in_=view, compare_op=ALU.is_ge, fill=0.0, base=DH - 1,
                                            pattern=pattern, channel_multiplier=-1).then_inc(s["masks"], 1)
                    done += 2
                nc.gpsimd.memset(zeros[:, :], 0.0).then_inc(s["zeroed"], 1)

            @block.vector
            def _(dve):
                dve.wait_ge(s["bias_in"], 32)
                dve.wait_ge(s["ones_set"], 2)
                dve.wait_ge(s["masks"], 6)

                def norm(i, j):
                    ge(dve, s["turned"], i - 1)
                    nc.vector.tensor_scalar(xhat[j][:, :], core.x[:, i, :], core.mean_var[:, i, 0:1],
                                            core.rstd[:, bass.ds(i, 1)], ALU.subtract, ALU.mult)\
                        .then_inc(s["xhat_done"], 1)

                def low(i, w):
                    dve.wait_ge(s["high"], i + 1)
                    h, u = w // G % GROUPS_B, w % G
                    nc.vector.tensor_tensor(xt_low[h][:, :, u * P:(u + 1) * P],
                                            turn_ps[w % 2][:, 0:D].rearrange("p (k t) -> p k t", k=KD),
                                            xt_high[h][:, :, u * P:(u + 1) * P].bitcast(F32), ALU.subtract)\
                        .then_inc(s["low"], 1)

                def add_bias(i, j):
                    dve.wait_ge(s["projected"], i + 1)
                    ge(dve, s["expd"], i - 1)
                    ge(dve, s["relud"], i - 1)
                    ge(dve, s["summed"], i - 1)
                    nc.vector.tensor_tensor(kv_lin[j][:, :, 0:P],
                                            kv_proj_ps[j][:, :].rearrange("p (k c) -> p k c", c=P),
                                            bias_kv[:, :].rearrange("p (k c) -> p k c", c=P), ALU.add)\
                        .then_inc(s["linear"], 1)

                def map_k(i, j):
                    dve.wait_ge(s["expd"], i + 1)
                    dve.wait_ge(s["relud"], i + 1)
                    ge(dve, s["summed"], i - 1)
                    nc.vector.scalar_tensor_tensor(out=k_map[j][:, :, :], in0=k_exp[j][:, :, :], scalar=1.0,
                                                   in1=k_relu[j][:, :, :], op0=ALU.min, op1=ALU.add)\
                        .then_inc(s["k_done"], 1)

                def map_q(g, h, m):
                    dve.wait_ge(s["q_expd"], g * KD + (m + 1))
                    dve.wait_ge(s["q_relud"], g * KD + (m + 1))
                    ge(dve, s["numer"], g * G - G)
                    nc.vector.scalar_tensor_tensor(out=qT[h][:, m, :], in0=q_exp[m][:, :], scalar=1.0,
                                                   in1=q_relu[m][:, :], op0=ALU.min, op1=ALU.add)\
                        .then_inc(s["q_done"], 1)

                def keep_kv(b):
                    dve.wait_ge(s["summed"], b * TB + TB)
                    ge(dve, s["numer"], b * TB)
                    for k in range(KD):
                        nc.vector.tensor_tensor(kv[:, k, 0:P], kv_sum[:, k, 0:P], head_mask[:, :], ALU.mult)
                        nc.vector.tensor_scalar(kv[:, k, P:P + HPB], zcol_mask[:, :], kv_sum[:, k, P:P + 1], None,
                                                ALU.mult).then_inc(s["kv_done"], 1)

                def scores(i, j):
                    dve.wait_ge(s["numer"], i + 1)
                    zj = z[j][:, :].rearrange("p (k h) -> p k h", k=KD)
                    nc.vector.tensor_scalar(zj, num[:, :, P:P + HPB], 1e-6, None, ALU.add).then_inc(s["z_eps"], 1)
                    dve.wait_ge(s["z_eps"], i + 1)
                    nc.vector.reciprocal(z[j][:, :], z[j][:, :]).then_inc(s["z_done"], 1)
                    dve.wait_ge(s["z_done"], i + 1)
                    for k in range(KD):
                        last = nc.vector.tensor_tensor(
                            core.y[:, i, k * P:(k + 1) * P].rearrange("p (h c) -> p h c", c=DH),
                            num[:, k, 0:P].rearrange("p (h c) -> p h c", c=DH),
                            z[j][:, k * HPB:(k + 1) * HPB].unsqueeze(2).to_broadcast([P, HPB, DH]), ALU.mult)
                    last.then_inc(s["y_done"], 1)

                def slot(b, w):
                    i, j = b * TB + w, w % 2
                    if real(i - 1):
                        map_k(i - 1, 1 - j)
                    if real(i + 2):
                        low(i + 2, w + 2)
                    if real(i + 3):
                        norm(i + 3, 1 - j)
                    if real(i):
                        add_bias(i, j)
                    g, h = queries_before(b, w)
                    if w % G >= 2 and real(g * G):
                        map_q(g, h, w % G - 2)
                    if w == 0 and real(i - 1):
                        keep_kv(b - 1)
                    if real(i - TB):
                        scores(i - TB, j)

                norm(0, 0)
                norm(1, 1)
                low(0, 0)
                norm(2, 0)
                low(1, 1)
                slots(dve, slot)

            @block.scalar
            def _(act):
                act.wait_ge(s["bias_in"], 32)

                def high(i, w):
                    act.wait_ge(s["turned"], i + 1)
                    h, u = w // G % GROUPS_B, w % G
                    if u == 0:
                        group = i // G if isinstance(i, int) else queries_of["group"]
                        ge(act, s["q_projected"], group * KD - KD)
                    nc.scalar.activation(xt_high[h][:, :, u * P:(u + 1) * P],
                                         turn_ps[w % 2][:, 0:D].rearrange("p (k t) -> p k t", k=KD), ACT.Copy)\
                        .then_inc(s["high"], 1)
                queries_of = {}

                def parts_k(i, j):
                    act.wait_ge(s["linear"], i + 1)
                    ge(act, s["k_done"], i - 1)
                    nc.scalar.activation(k_exp[j][:, :, :], kv_lin[j][:, 0:KD, 0:P], ACT.Exp).then_inc(s["expd"], 1)
                    nc.scalar.activation(k_relu[j][:, :, :], kv_lin[j][:, 0:KD, 0:P], ACT.Relu)\
                        .then_inc(s["relud"], 1)

                def parts_q(g, m):
                    act.wait_ge(s["q_projected"], g * KD + (m + 1))
                    ge(act, s["q_done"], g * KD + (m - 1))
                    nc.scalar.activation(q_exp[m][:, :], q_ps[m][:, :], ACT.Exp, bias=bias_q[:, m:m + 1])\
                        .then_inc(s["q_expd"], 1)
                    nc.scalar.activation(q_relu[m][:, :], q_ps[m][:, :], ACT.Relu, bias=bias_q[:, m:m + 1])\
                        .then_inc(s["q_relud"], 1)

                def slot(b, w):
                    i, j = b * TB + w, w % 2
                    queries_of["group"] = b * GROUPS_B + (w + 2) // G
                    if real(i + 2):
                        high(i + 2, w + 2)
                    if real(i):
                        parts_k(i, j)
                    g, h = queries_before(b, w)
                    if w % G in (1, 2) and real(g * G):
                        parts_q(g, w % G - 1)
                high(0, 0)
                high(1, 1)
                slots(act, slot)

            @block.tensor
            def _(pe):
                def turn(i, j):
                    pe.wait_ge(s["xhat_done"], i + 1)
                    ge(pe, s["low"], i - 1)
                    for k in range(KD):
                        last = nc.tensor.transpose(turn_ps[j][:, k * P:(k + 1) * P], xhat[j][:, k * P:(k + 1) * P],
                                                   core.ident[:, :])
                    last.then_inc(s["turned"], 1)

                def project_kv(i, w):
                    pe.wait_ge(s["low"], i + 1)
                    ge(pe, s["linear"], i - 1)
                    n = 0
                    h, u = w // G, w % G
                    for k in range(KD):
                        for xt, wt in ((xt_high, qkv_high), (xt_low, qkv_high), (xt_high, qkv_low)):
                            n += 1
                            last = nc.tensor.matmul(kv_proj_ps[w % 2][:, :], xt[h][:, k, u * P:(u + 1) * P],
                                                    wt[:, k, D:3 * D], start=(n == 1), stop=(n == 3 * KD))
                    last.then_inc(s["projected"], 1)

                def project_q(g, h, m):
                    pe.wait_ge(s["low"], g * G + G)
                    ge(pe, s["q_relud"], g * KD + (m - 1))
                    n = 0
                    for k in range(KD):
                        for wt, xt in ((qkv_high, xt_high), (qkv_high, xt_low), (qkv_low, xt_high)):
                            n += 1
                            last = nc.tensor.matmul(q_ps[m][:, :], wt[:, k, m * P:(m + 1) * P], xt[h][:, k, :],
                                                    start=(n == 1), stop=(n == 3 * KD))
                    last.then_inc(s["q_projected"], 1)

                def sum_kv(i, j, first, last_of_batch, batches_before):
                    pe.wait_ge(s["k_done"], i + 1)
                    if first:
                        ge(pe, s["kv_done"], batches_before * KD)
                    for k in range(KD):
                        last = nc.tensor.matmul(kv_sum[:, k, :], k_map[j][:, k, :], kv_lin[j][:, KD + k, :],
                                                start=(first and k == 0),
                                                stop=(last_of_batch and k == KD - 1))
                    last.then_inc(s["summed"], 1)

                def score(b, w):
                    i = b * TB + w
                    pe.wait_ge(s["kv_done"], b * KD + KD)
                    pe.wait_ge(s["q_done"], b * (GROUPS_B * KD) + (w // G + 1) * KD)
                    ge(pe, s["y_done"], i)
                    h, u = w // G, w % G
                    for k in range(KD):
                        last = nc.tensor.matmul(num[:, k, :], qT[h][:, k, u * P:(u + 1) * P], kv[:, k, :],
                                                start=True, stop=True)
                    last.then_inc(s["numer"], 1)

                def slot(b, w):
                    i, j = b * TB + w, w % 2
                    if real(i + 2):
                        turn(i + 2, j)
                    if real(i):
                        project_kv(i, w)
                    if real(i - 1):
                        sum_kv(i - 1, 1 - j, w == 1, w == 0, b)
                    if real(i - TB):
                        score(b - 1, w)
                    g, h = queries_before(b, w)
                    if w % G < KD and real(g * G):
                        project_q(g, h, w % G)
                turn(0, 0)
                turn(1, 1)
                slots(pe, slot)


class AttentionProjections:

    G = 4
    NG = T // G

    def __init__(self, core, ph, w_high, w_low, bias_col, q_dram, k_dram, v_all):
        self.core, self.nc = core, core.nc
        self.w_high, self.w_low, self.bias_col = w_high, w_low, bias_col
        self.q_dram, self.k_dram, self.v_all = q_dram, k_dram, v_all
        G = self.G
        self.xhat = [ph.sb(f"xhat{j}", [P, D]) for j in range(2)]
        self.xt_high = [ph.sb(f"xt_high{j}", [P, KD, G * P], F32R) for j in range(2)]
        self.xt_low = [ph.sb(f"xt_low{j}", [P, KD, G * P], F32R) for j in range(2)]
        self.lin = [ph.sb(f"lin{m}", [P, G * P]) for m in range(3)]
        self.high = [ph.sb(f"high{m}", [P, G * P], F32R) for m in range(3)]
        self.low = [ph.sb(f"low{m}", [P, G * P], F32R) for m in range(3)]
        self.bias = ph.sb("bias", [P, 3])
        self.turn_ps = [ph.ps() for j in range(2)]
        self.proj_ps = [ph.ps() for m in range(3)]
        self.v_ps = ph.ps()
        self.s = {n: ph.sem(n) for n in ("bias_in", "v_cleared", "xhat_done", "turned", "xt_high", "xt_low",
                                         "projected", "linear", "part_high", "part_low", "stored", "v_turned",
                                         "v_kept")}

    def turned_tile(self, u):
        return self.turn_ps[u % 2][:, 0:D].rearrange("p (k t) -> p k t", k=KD)

    def sync_begin(self, sp):
        sp.dma_start(self.bias[:, :], self.bias_col).then_inc(self.s["bias_in"], 16)

    def sync_all(self, sp):
        s, G, q_dram, k_dram = self.s, self.G, self.q_dram, self.k_dram

        def store(g):
            sp.wait_ge(s["part_low"], g * 3 + 3)
            cols = bass.ds(g * (G * P), G * P)
            for part, source in ((0, self.high), (1, self.low)):
                for m in range(2):
                    sp.dma_start(q_dram[part, m * P:(m + 1) * P, cols], source[m][:, :].bitcast(F32))\
                        .then_inc(s["stored"], 16)
                sp.dma_start(k_dram[part, :, cols], source[2][0:64, :].bitcast(F32)).then_inc(s["stored"], 16)
        tiles(sp, self.NG, 2, lambda g, u: store(g))
        sp.wait_ge(s["stored"], 96 * self.NG)

    def gpsimd_begin(self, pool):
        s, v_all = self.s, self.v_all
        self.nc.gpsimd.memset(v_all[:, :, :, :], 0.0).then_inc(s["v_cleared"], 1)
        pool.wait_ge(s["v_cleared"], 1)
        self.nc.gpsimd.memset(v_all[:, :, :, DH:DH + 1], 1.0).then_inc(s["v_cleared"], 1)

    def vector_norm(self, dve, i, j):
        core, s = self.core, self.s
        ge(dve, s["turned"], i - 1)
        self.nc.vector.tensor_scalar(self.xhat[j][:, :], core.x[:, i, :], core.mean_var[:, i, 0:1],
                                     core.rstd[:, bass.ds(i, 1)], ALU.subtract, ALU.mult).then_inc(s["xhat_done"], 1)

    def vector_tile(self, dve, g, j, u):
        s, i = self.s, g * self.G + u
        if u == 0:
            ge(dve, s["projected"], g * 3 - 3)
            self.vector_norm(dve, i, 0)
        if u + 1 < self.G:
            self.vector_norm(dve, i + 1, (u + 1) % 2)
        dve.wait_ge(s["xt_high"], i + 1)
        part = slice(u * P, (u + 1) * P)
        self.nc.vector.tensor_tensor(self.xt_low[j][:, :, part], self.turned_tile(u),
                                     self.xt_high[j][:, :, part].bitcast(F32), ALU.subtract).then_inc(s["xt_low"], 1)

    def vector_rest(self, dve, g):
        s, G, nc = self.s, self.G, self.nc
        ge(dve, s["stored"], g * 96)
        if isinstance(g, int) and g == 0:
            dve.wait_ge(s["v_cleared"], 2)
        for m in range(3):
            dve.wait_ge(s["part_high"], g * 3 + (m + 1))
            nc.vector.tensor_tensor(self.low[m][:, :], self.lin[m][:, :], self.high[m][:, :].bitcast(F32),
                                    ALU.subtract).then_inc(s["part_low"], 1)
        dve.wait_ge(s["v_turned"], g + 1)
        nc.vector.tensor_copy(self.v_all[:, bass.ds(g * G, G), :, 0:DH],
                              self.v_ps[:, :].rearrange("p (t f) -> p t f", t=G)[:, :, 64:128]
                              .rearrange("p t (h d) -> p t h d", d=DH)).then_inc(s["v_kept"], 1)

    def scalar_tile(self, act, g, j, u):
        s, i = self.s, g * self.G + u
        if u == 0:
            ge(act, s["projected"], g * 3 - 3)
        act.wait_ge(s["turned"], i + 1)
        self.nc.scalar.activation(self.xt_high[j][:, :, u * P:(u + 1) * P], self.turned_tile(u), ACT.Copy)\
            .then_inc(s["xt_high"], 1)

    def scalar_rest(self, act, g):
        s, nc = self.s, self.nc
        if isinstance(g, int) and g == 0:
            act.wait_ge(s["bias_in"], 16)
        ge(act, s["part_low"], g * 3)
        ge(act, s["stored"], g * 96)
        ge(act, s["v_turned"], g)
        for m in range(3):
            act.wait_ge(s["projected"], g * 3 + (m + 1))
            nc.scalar.activation(self.lin[m][:, :], self.proj_ps[m][:, :], ACT.Identity, bias=self.bias[:, m:m + 1])\
                .then_inc(s["linear"], 1)
            act.wait_ge(s["linear"], g * 3 + (m + 1))
            nc.scalar.activation(self.high[m][:, :], self.lin[m][:, :], ACT.Copy).then_inc(s["part_high"], 1)

    def tensor_all(self, pe):
        core, nc, s, G = self.core, self.nc, self.s, self.G

        def group(g, j):
            for u in range(G):
                i = g * G + u
                pe.wait_ge(s["xhat_done"], i + 1)
                ge(pe, s["xt_low"], i - 1)
                for k in range(KD):
                    last = nc.tensor.transpose(self.turn_ps[u % 2][:, k * P:(k + 1) * P],
                                               self.xhat[u % 2][:, k * P:(k + 1) * P], core.ident[:, :])
                last.then_inc(s["turned"], 1)
            pe.wait_ge(s["xt_low"], g * G + G)
            for m in range(3):
                ge(pe, s["linear"], g * 3 + m - 2)
                n = 0
                for k in range(KD):
                    for wt, xt in ((self.w_high, self.xt_high), (self.w_high, self.xt_low),
                                   (self.w_low, self.xt_high)):
                        n += 1
                        last = nc.tensor.matmul(self.proj_ps[m][:, :], wt[:, k, m * P:(m + 1) * P], xt[j][:, k, :],
                                                start=(n == 1), stop=(n == 3 * KD))
                last.then_inc(s["projected"], 1)
            pe.wait_ge(s["linear"], g * 3 + 3)
            ge(pe, s["v_kept"], g)
            for u in range(G):
                last = nc.tensor.transpose(self.v_ps[:, u * P:(u + 1) * P], self.lin[2][:, u * P:(u + 1) * P],
                                           core.ident[:, :])
            last.then_inc(s["v_turned"], 1)
        tiles(pe, self.NG, 2, group)


def softmax_attention(core, q_dram, k_dram, v_all, negmax_dram, o_dram):
    nc = core.nc
    QU = N // 2
    QT = QU // P
    KT = N // P
    ROWS = 4 * DH
    STEPS = NKV * KT
    MAXES = HEADS * QT
    KV_MAXES = GROUPS * QT
    AHEAD = 4
    HALF = HEADS // 2
    with Phase(nc, "sa") as ph:
        q_stack = [ph.sb(f"q_stack{h}", [P, HEADS, QU], F32R) for h in range(2)]
        k_max = ph.sb("k_max", [ROWS, NKV, N], F32R)
        k_main = ph.sb("k_main", [P, NKV, N], F32R)
        v_now = ph.sb("v_now", [P, KT, NKV, 32])
        probs = [ph.sb(f"probs{j}", [P, QU]) for j in range(8)]
        negmax = [ph.sb(f"negmax{h}", [P, QT, HEADS]) for h in range(2)]
        turned_high = ph.sb("turned_high", [HALF, QU], F32R)
        turned_low = ph.sb("turned_low", [HALF, QU], F32R)
        o_sb = [ph.sb(f"o_sb{j}", [P, QU]) for j in range(2)]
        st_ps = [ph.ps() for j in range(3)]
        mx_ps = [ph.ps(2) for j in range(2)]
        o_ps = ph.ps()
        q_in = [[ph.sem(f"q_in{h}{kv}") for kv in range(NKV)] for h in range(2)]
        kmax_in = [ph.sem(f"kmax_in{kv}") for kv in range(NKV)]
        kmain_in = [ph.sem(f"kmain_in{kv}") for kv in range(NKV)]
        neg_in = [[ph.sem(f"neg_in{h}{half}") for half in range(2)] for h in range(2)]
        s = {n: ph.sem(n) for n in ("pads", "v_in", "max_scored",
                                    "maxed", "turned", "t_high", "t_low", "neg_out", "scored",
                                    "expd", "weighted", "o_kept", "o_out0", "o_out1")}

        def unit_before(b, h):
            return (b, 0) if h == 1 else (b - 1, 1)

        def unit_after(b, h):
            return (b, 1) if h == 0 else (b + 1, 0)

        def maxima_beside(step):
            at = (step + AHEAD) % (STEPS // 2)
            half = (step + AHEAD) // (STEPS // 2) + 1
            each = MAXES // STEPS
            counts = [0] + [each + 1 if x in (1, 3) else each for x in range(1, STEPS // 2)]
            start = half % 2 * (MAXES // 2) + sum(counts[:at])
            return half >= 2, list(range(start, start + counts[at]))

        EARLY = maxima_beside(0)[1][0]

        with ph.block() as block:
            @block.gpsimd
            def _(pool):
                for q in q_stack:
                    nc.gpsimd.memset(q[64:P, :, :].bitcast(F32), 0.0).then_inc(s["pads"], 1)
                nc.gpsimd.memset(k_main[64:P, :, :].bitcast(F32), 0.0).then_inc(s["pads"], 1)
                pool.wait_ge(s["pads"], 3)
                nc.gpsimd.memset(k_main[64:66, :, :].bitcast(F32), 1.0).then_inc(s["pads"], 1)

                def load_v(b, kv):
                    nc.gpsimd.tensor_copy(v_now[:, :, kv, :], v_all[:, bass.ds(b * KT, KT), kv, :]).then_inc(s["v_in"], 1)

                def store_o(b, h, kv):
                    done = b * (2 * NKV) + h * NKV + kv
                    pool.wait_ge(s["o_kept"], done + 1)
                    pool.dma_start(o_dram[b, h, kv, :, :], o_sb[kv % 2][:, :]).then_inc(s[f"o_out{kv % 2}"], 16)

                def batch(b, last):
                    for h in range(2):
                        for kv in range(NKV):
                            store_o(b, h, kv)
                            if h == 1 and not last:
                                load_v(b + 1, kv)
                pool.wait_ge(s["pads"], 4)
                for kv in range(NKV):
                    load_v(0, kv)
                with pool.Fori(0, B - 1) as b:
                    batch(b, False)
                batch(B - 1, True)
                for j in range(2):
                    pool.wait_ge(s[f"o_out{j}"], 16 * NKV * B)

            @block.sync
            def _(sp):
                def load_q(b, h, kv):
                    heads = slice(kv * GROUPS, (kv + 1) * GROUPS)
                    for r, part in enumerate((0, 1, 0, 1)):
                        sp.dma_start(q_stack[h][r * DH:(r + 1) * DH, heads, :].bitcast(F32),
                                     q_dram[part, kv * GROUPS * DH:(kv + 1) * GROUPS * DH,
                                            bass.ds(b * N + h * QU, QU)]
                                     .rearrange("(h d) t -> d h t", d=DH)).then_inc(q_in[h][kv], 16)

                def load_k(dst, sems, b, kv):
                    for r, part in enumerate((0, 0, 1, 1)):
                        sp.dma_start(dst[r * DH:(r + 1) * DH, kv, :].bitcast(F32),
                                     k_dram[part, kv * DH:(kv + 1) * DH, bass.ds(b * N, N)]).then_inc(sems[kv], 16)

                def put_negmax(b, h, half):
                    unit = b * 2 + h
                    heads = slice(half * HALF, (half + 1) * HALF)
                    sp.wait_ge(s["t_low"], unit * 2 + (half + 1))
                    sp.dma_start(negmax_dram[unit, 0, heads, :], turned_high[:, :].bitcast(F32)).then_inc(s["neg_out"], 16)
                    sp.dma_start(negmax_dram[unit, 1, heads, :], turned_low[:, :].bitcast(F32)).then_inc(s["neg_out"], 16)
                    sp.wait_ge(s["neg_out"], unit * 64 + (half + 1) * 32)
                    sp.dma_start(q_stack[h][64:66, heads, :].bitcast(F32), negmax_dram[unit, :, heads, :])\
                        .then_inc(neg_in[h][half], 16)

                def after_main(b, h, kv):
                    sp.wait_ge(s["scored"], b * (2 * 4 * STEPS) + h * (4 * STEPS) + (kv + 1) * (4 * KT))

                def after_maxima(b, kv):
                    sp.wait_ge(s["maxed"], b * (2 * MAXES) + MAXES + (kv + 1) * KV_MAXES)

                def batch(b, last):
                    def queries(h, kv):
                        if not last:
                            after_main(b, h, kv)
                            load_q(b + 1, h, kv)

                    def keys(kv):
                        if not last:
                            load_k(k_main, kmain_in, b + 1, kv)

                    def max_keys(kv):
                        if not last:
                            after_maxima(b, kv)
                            load_k(k_max, kmax_in, b + 1, kv)
                    queries(0, 0)
                    put_negmax(b, 0, 1)
                    queries(0, 1)
                    max_keys(0)
                    queries(0, 2)
                    max_keys(1)
                    put_negmax(b, 1, 0)
                    queries(0, 3)
                    max_keys(2)
                    queries(1, 0)
                    keys(0)
                    max_keys(3)
                    put_negmax(b, 1, 1)
                    queries(1, 1)
                    keys(1)
                    queries(1, 2)
                    keys(2)
                    if not last:
                        put_negmax(b + 1, 0, 0)
                    queries(1, 3)
                    keys(3)
                for kv in range(NKV):
                    load_k(k_max, kmax_in, 0, kv)
                    load_q(0, 0, kv)
                for kv in range(NKV):
                    load_k(k_main, kmain_in, 0, kv)
                    load_q(0, 1, kv)
                sp.wait_ge(s["pads"], 4)
                put_negmax(0, 0, 0)
                with sp.Fori(0, B - 1) as b:
                    batch(b, False)
                batch(B - 1, True)

            @block.tensor
            def _(pe):
                def maximum(b, h, m):
                    count = b * (2 * MAXES) + h * MAXES + m
                    if m % KV_MAXES == 0:
                        pe.wait_ge(q_in[h][m // KV_MAXES], b * 64 + 64)
                        if h == 0:
                            pe.wait_ge(kmax_in[m // KV_MAXES], b * 64 + 64)
                    ge(pe, s["maxed"], count - 1)
                    if m % (MAXES // 2) == 0:
                        ge(pe, s["t_low"], b * 4 + h * 2 + m // (MAXES // 2))
                    head, qt = m // QT, m % QT
                    for half in range(2):
                        last = nc.tensor.matmul(mx_ps[m % 2][:, half * 512:(half + 1) * 512],
                                                q_stack[h][0:ROWS, head, qt * P:(qt + 1) * P],
                                                k_max[:, head // GROUPS, half * 512:(half + 1) * 512],
                                                start=True, stop=True)
                    last.then_inc(s["max_scored"], 1)

                def turn_maxima(b, h, half):
                    pe.wait_ge(s["maxed"], b * (2 * MAXES) + h * MAXES + (half + 1) * (MAXES // 2))
                    for qt in range(QT):
                        last = nc.tensor.transpose(mx_ps[0][0:HALF, qt * P:(qt + 1) * P],
                                                   negmax[h][:, qt, half * HALF:(half + 1) * HALF],
                                                   core.ident[:, :])
                    last.then_inc(s["turned"], 1)

                def weigh(b, h, step):
                    kv, kt = step // KT, step % KT
                    n0 = b * (2 * 4 * STEPS) + h * (4 * STEPS) + 4 * step
                    if kt == 0 and h == 0:
                        pe.wait_ge(s["v_in"], b * NKV + (kv + 1))
                    if kt == 0:
                        ge(pe, s["o_kept"], b * (2 * NKV) + h * NKV + kv)
                    for g in range(GROUPS):
                        pe.wait_ge(s["expd"], n0 + (g + 1))
                        last = nc.tensor.matmul(o_ps[32 * g:32 * g + 32, :], v_now[:, kt, kv, :],
                                                probs[(4 * step + g) % 8][:, :], start=(kt == 0), stop=(kt == KT - 1),
                                                tile_position=(0, 32 * g))
                    last.then_inc(s["weighted"], 1)

                def unit(b, h, first=False, last=False):
                    for step in range(STEPS):
                        kv, kt = step // KT, step % KT
                        ahead, maxes = maxima_beside(step)
                        owner = unit_after(b, h) if ahead else (b, h)
                        if last and ahead:
                            maxes = []
                        if step % (STEPS // 2) == 0:
                            pe.wait_ge(neg_in[h][step // (STEPS // 2)], b * 16 + 16)
                        if kt == 0 and h == 0:
                            pe.wait_ge(kmain_in[kv], b * 64 + 64)
                        for g in range(GROUPS):
                            if g == 2 and maxes:
                                maximum(*owner, maxes.pop(0))
                            if g == 3:
                                if step >= 1:
                                    weigh(b, h, step - 1)
                                elif not first:
                                    weigh(*unit_before(b, h), STEPS - 1)
                            n = 4 * step + g
                            count = b * (2 * 4 * STEPS) + h * (4 * STEPS) + n
                            ge(pe, s["expd"], count - (1 if n < 2 else 2))
                            nc.tensor.matmul(st_ps[n % 3][:, :],
                                             k_main[:, kv, kt * P:(kt + 1) * P],
                                             q_stack[h][:, kv * GROUPS + g, :], start=True, stop=True)\
                                .then_inc(s["scored"], 1)
                        if step == STEPS // 2 - AHEAD:
                            turn_maxima(b, h, 1)
                        if step == STEPS - AHEAD and not last:
                            turn_maxima(*owner, 0)
                        for m in maxes:
                            maximum(*owner, m)
                    if last:
                        weigh(b, h, STEPS - 1)

                for m in range(MAXES // 2):
                    maximum(0, 0, m)
                turn_maxima(0, 0, 0)
                for m in range(MAXES // 2, EARLY):
                    maximum(0, 0, m)
                pe.wait_ge(s["pads"], 4)

                def batch(b, first=False, last=False):
                    unit(b, 0, first=first)
                    unit(b, 1, last=last)
                batch(0, first=True)
                with pe.Fori(1, B - 1) as b:
                    batch(b)
                batch(B - 1, last=True)

            @block.scalar
            def _(act):
                def unit(b, h):
                    for step in range(STEPS):
                        for g in range(GROUPS):
                            n = 4 * step + g
                            count = b * (2 * 4 * STEPS) + h * (4 * STEPS) + n
                            act.wait_ge(s["scored"], count + 1)
                            if g == 0:
                                ge(act, s["weighted"], b * (2 * STEPS) + h * STEPS + step - 1)
                            nc.scalar.activation(probs[n % 8][:, :], st_ps[n % 3][:, :], ACT.Exp, scale=0.25)\
                                .then_inc(s["expd"], 1)

                def batch(b):
                    unit(b, 0)
                    unit(b, 1)
                batch(0)
                with act.Fori(1, B) as b:
                    batch(b)

            @block.vector
            def _(dve):
                def maximum(b, h, m):
                    dve.wait_ge(s["max_scored"], b * (2 * MAXES) + h * MAXES + (m + 1))
                    nc.vector.tensor_reduce(negmax[h][:, m % QT, m // QT:m // QT + 1], mx_ps[m % 2][:, :], AX.X,
                                            ALU.max, negate=True).then_inc(s["maxed"], 1)

                def maxima_parts(b, h, half):
                    before = b * 4 + (h * 2 + half)
                    dve.wait_ge(s["turned"], before + 1)
                    ge(dve, s["neg_out"], before * 32)
                    nc.vector.tensor_copy(turned_high[:, :], mx_ps[0][0:HALF, 0:QU]).then_inc(s["t_high"], 1)
                    dve.wait_ge(s["t_high"], before + 1)
                    nc.vector.tensor_tensor(turned_low[:, :], mx_ps[0][0:HALF, 0:QU],
                                            turned_high[:, :].bitcast(F32), ALU.subtract).then_inc(s["t_low"], 1)

                def keep_o(b, h, kv):
                    done = b * (2 * NKV) + h * NKV + kv
                    dve.wait_ge(s["weighted"], b * (2 * STEPS) + h * STEPS + (kv + 1) * KT)
                    ge(dve, s[f"o_out{kv % 2}"], (b * NKV + h * (NKV // 2) + kv // 2) * 16)
                    nc.vector.tensor_copy(o_sb[kv % 2][:, :], o_ps[:, :]).then_inc(s["o_kept"], 1)

                def unit(b, h, first=False, last=False):
                    for step in range(STEPS):
                        ahead, maxes = maxima_beside(step)
                        owner = unit_after(b, h) if ahead else (b, h)
                        if last and ahead:
                            maxes = []
                        if maxes:
                            maximum(*owner, maxes.pop(0))
                        if step == 0:
                            if not first:
                                keep_o(*unit_before(b, h), NKV - 1)
                        elif step % KT == 0:
                            keep_o(b, h, step // KT - 1)
                        if step == STEPS // 2 - AHEAD:
                            maxima_parts(b, h, 1)
                        if step == STEPS - AHEAD and not last:
                            maxima_parts(*owner, 0)
                        for m in maxes:
                            maximum(*owner, m)
                    if last:
                        keep_o(b, h, NKV - 1)

                for m in range(MAXES // 2):
                    maximum(0, 0, m)
                maxima_parts(0, 0, 0)
                for m in range(MAXES // 2, EARLY):
                    maximum(0, 0, m)

                def batch(b, first=False, last=False):
                    unit(b, 0, first=first)
                    unit(b, 1, last=last)
                batch(0, first=True)
                with dve.Fori(1, B - 1) as b:
                    batch(b)
                batch(B - 1, last=True)


def attention_normalised(core, o_dram):
    nc = core.nc
    U = 2 * B
    with Phase(nc, "an") as ph:
        o_in = [ph.sb(f"o_in{j}", [P, 512]) for j in range(NKV)]
        recip = [ph.sb(f"recip{j}", [P, 4, GROUPS]) for j in range(NKV)]
        turn_ps = [ph.ps() for j in range(NKV)]
        loaded = [ph.sem(f"loaded{j}") for j in range(NKV)]
        s = {n: ph.sem(n) for n in ("turned", "recip_done", "done")}
        with ph.block() as block:
            @block.sync
            def _(sp):
                def unit(u, _):
                    for kv in range(NKV):
                        ge(sp, s["turned"], u * NKV + (kv - NKV + 1))
                        sp.dma_start(o_in[kv][:, :], o_dram[u, kv, :, :]).then_inc(loaded[kv], 16)
                tiles(sp, U, 1, unit)

            @block.tensor
            def _(pe):
                def unit(u, _):
                    for kv in range(NKV):
                        pe.wait_ge(loaded[kv], u * 16 + 16)
                        ge(pe, s["done"], u * NKV + (kv - NKV + 1))
                        for qt in range(4):
                            last = nc.tensor.transpose(turn_ps[kv][:, qt * P:(qt + 1) * P],
                                                       o_in[kv][:, qt * P:(qt + 1) * P], core.ident[:, :])
                        last.then_inc(s["turned"], 1)
                tiles(pe, U, 1, unit)

            @block.vector
            def _(dve):
                def unit(u, _):
                    for kv in range(NKV):
                        dve.wait_ge(s["turned"], u * NKV + (kv + 1))
                        ps = turn_ps[kv][:, :].rearrange("p (q g c) -> p q g c", q=4, g=GROUPS)
                        nc.vector.reciprocal(recip[kv][:, :, :], ps[:, :, :, DH]).then_inc(s["recip_done"], 1)
                        dve.wait_ge(s["recip_done"], u * NKV + (kv + 1))
                        nc.vector.tensor_tensor(
                            core.y[:, bass.ds(u * 4, 4), kv * 64:(kv + 1) * 64]
                            .rearrange("p q (g d) -> p q g d", g=GROUPS),
                            ps[:, :, :, 0:DH], recip[kv][:, :, :].unsqueeze(3).to_broadcast([P, 4, GROUPS, DH]),
                            ALU.mult).then_inc(s["done"], 1)
                tiles(dve, U, 1, unit)
                dve.wait_ge(s["done"], U * NKV)


F16 = mybir.dt.float16
E = 8
SLOT_TILES = 2 * T + E
W_SCALE = 64.0
H_SCALE = 16.0


def split_scaled(core, name, parts):
    nc = core.nc
    with Phase(nc, name) as ph:
        stage = ph.sb("stage", [P, 2, 2048])
        loaded = [ph.sem("loaded0"), ph.sem("loaded1")]
        high_done, low_done = ph.sem("high_done"), ph.sem("low_done")

        def staged(i):
            src = parts[i][0]
            flat = stage[0:src.shape[0], i % 2, 0:src.shape[1] * (src.shape[2] if len(src.shape) == 3 else 1)]
            return flat.rearrange("p (k f) -> p k f", k=src.shape[1]) if len(src.shape) == 3 else flat

        with ph.block() as block:
            @block.sync
            def _(sp):
                for i, (src, _, _) in enumerate(parts):
                    ge(sp, low_done, i - 1)
                    sp.dma_start(staged(i), src).then_inc(loaded[i % 2], 16)

            @block.scalar
            def _(act):
                for i, (_, high, _) in enumerate(parts):
                    act.wait_ge(loaded[i % 2], 16 * (i // 2 + 1))
                    nc.scalar.activation(high, staged(i), ACT.Copy, scale=W_SCALE).then_inc(high_done, 1)

            @block.vector
            def _(dve):
                for i, (_, high, low) in enumerate(parts):
                    dve.wait_ge(high_done, i + 1)
                    nc.vector.scalar_tensor_tensor(out=low, in0=staged(i), scalar=W_SCALE, in1=high,
                                                   op0=ALU.mult, op1=ALU.subtract).then_inc(low_done, 1)


class Weights:

    def __init__(self, ph, n, F):
        self.n, self.F, self.KF = n, F, -(-F // P)
        self.up = [ph.sb(f"up_{x}", [P, n, KD, 2 * F], F16) for x in ("high", "low")]
        self.down = [ph.sb(f"down_{x}", [P, n, self.KF, D], F16) for x in ("high", "low")]

    def rows(self, k):
        return min(P, self.F - k * P)

    PARTS = 4
    PART = 1024

    def part_shape(self, u):
        if u < 2:
            return P, 2 * self.F
        whole = self.KF // 2
        return (P, whole * D) if u == 2 or self.F % P == 0 else (self.F % P, (self.KF - whole) * D)

    def part_source(self, up_dram, down_dram, e, u):
        if u < 2:
            return up_dram[e, u * P:(u + 1) * P, :].unsqueeze(1)
        rows = self.KF // 2 * P
        source = down_dram[e, 0:rows, :] if u == 2 else down_dram[e, rows:self.F, :]
        return source.rearrange("(k p) d -> p k d", p=self.part_shape(u)[0])

    def part(self, half, e, u):
        if u < 2:
            return self.up[half][:, bass.ds(e, 1), u, :].rearrange("p e f -> p (e f)")
        at = slice(0, self.KF // 2) if u == 2 else slice(self.KF // 2, self.KF)
        return self.down[half][0:self.part_shape(u)[0], bass.ds(e, 1), at, :].rearrange("p e k d -> p (e k d)")

    def parts(self, up_dram, down_dram):
        F = self.F
        out = []
        for e in range(self.n):
            up = up_dram[e, :, :].rearrange("(k p) f -> p k f", p=P)
            out.append((up, self.up[0][:, e, :, :], self.up[1][:, e, :, :]))
            whole = F // P
            out.append((down_dram[e, 0:whole * P, :].rearrange("(k p) d -> p k d", p=P),
                        self.down[0][:, e, 0:whole, :], self.down[1][:, e, 0:whole, :]))
            if F % P:
                r = F % P
                out.append((down_dram[e, whole * P:F, :], self.down[0][0:r, e, whole, :],
                            self.down[1][0:r, e, whole, :]))
        return out


def shared_expert(core, name, w, x_rows, slots_of, w_next, next_dram):
    nc = core.nc
    F, KF = w.F, w.KF
    n = T
    UNROLL = T // E
    TURNS = n // UNROLL
    PEELED = 1
    flat_rows = x_rows.rearrange("j p d -> (j p) d")
    with Phase(nc, name) as ph:
        x_in = [ph.sb(f"x_in{j}", [P, D]) for j in range(2)]
        xt = [[ph.sb(f"xt_{x}{j}", [P, KD, P], F16) for x in ("high", "low")] for j in range(2)]
        gate = [ph.sb(f"gate{j}", [P, KF * P]) for j in range(2)]
        hidden = [ph.sb(f"hidden{j}", [P, KF * P]) for j in range(2)]
        ht = [[ph.sb(f"ht_{x}{j}", [P, KF * P], F16) for x in ("high", "low")] for j in range(2)]
        xt_ps = [ph.ps() for j in range(2)]
        lin_ps = [ph.ps() for j in range(2)]
        gate_ps = [ph.ps() for j in range(2)]
        y_ps = [ph.ps() for j in range(2)]
        s = {k: ph.sem(k) for k in ("x_ready", "x_turned", "xt_high", "xt_low", "gated", "lined", "silu_done",
                                    "hidden_done", "h_high", "h_low", "downed", "y_done")}
        stage = ph.sb("stage", [P, 2, Weights.PART])
        sent = [ph.sem("sent0"), ph.sem("sent1")]
        staged = [ph.sem("staged0"), ph.sem("staged1")]
        next_high, next_low = ph.sem("next_high"), ph.sem("next_low")

        def staged_part(u):
            rows, cols = w_next.part_shape(u)
            return stage[0:rows, u % 2, 0:cols]

        def real(i):
            return not isinstance(i, int) or 0 <= i < n

        def slots(eng, slot):
            def turn(k):
                for u in range(UNROLL):
                    slot(k, u)
            for k in range(PEELED):
                turn(k)
            with eng.Fori(PEELED, TURNS - PEELED) as k:
                turn(k)
            for k in range(TURNS - PEELED, TURNS):
                turn(k)
            slot(TURNS, 0)
            slot(TURNS, 1)

        with ph.block() as block:
            @block.sync
            def _(sp):
                for e in range(E):
                    for u in range(UNROLL):
                        ge(sp, next_low, e * UNROLL + u - 1)
                        source = w_next.part_source(*next_dram, e, u)
                        sp.dma_start(staged_part(u).rearrange("p (k f) -> p k f", k=source.shape[1]), source)\
                            .then_inc(staged[u % 2], 16)

            @block.gpsimd
            def _(pool):
                for i in range(n):
                    pool.wait_ge(s["x_ready"], i + 1)
                    for c in range(2):
                        pool.indirect_dma_start(flat_rows,
                                                bass.IndirectOffsetOnAxis(ap=slots_of[:, i, c:c + 1], axis=0),
                                                x_in[i % 2][:, :], None).then_inc(sent[i % 2], 16)
                for j in range(2):
                    pool.wait_ge(sent[j], n // 2 * 32)

            @block.scalar
            def _(act):
                def high(i, j):
                    act.wait_ge(s["x_turned"], i + 1)
                    ge(act, s["lined"], i - 1)
                    nc.scalar.activation(xt[j][0][:, :, :], xt_ps[j][:, 0:D].rearrange("p (k t) -> p k t", k=KD),
                                         ACT.Copy).then_inc(s["xt_high"], 1)

                def silu(i, j):
                    act.wait_ge(s["gated"], i + 1)
                    ge(act, s["hidden_done"], i - 1)
                    nc.scalar.activation(gate[j][:, :], gate_ps[j][:, 0:KF * P], ACT.Silu, scale=1.0 / W_SCALE)\
                        .then_inc(s["silu_done"], 1)

                def hidden_high(i, j):
                    act.wait_ge(s["hidden_done"], i + 1)
                    ge(act, s["downed"], i - 1)
                    nc.scalar.activation(ht[j][0][:, :], hidden[j][:, :], ACT.Copy).then_inc(s["h_high"], 1)

                def cut_high(k, u):
                    act.wait_ge(staged[u % 2], (k * 2 + (u // 2 + 1)) * 16)
                    nc.scalar.activation(w_next.part(0, k, u), staged_part(u), ACT.Copy, scale=W_SCALE)\
                        .then_inc(next_high, 1)

                def slot(k, u):
                    i, j = k * UNROLL + u, u % 2
                    if real(i):
                        silu(i, j)
                        cut_high(k, u)
                    if real(i + 2):
                        high(i + 2, j)
                    if real(i):
                        hidden_high(i, j)
                high(0, 0)
                high(1, 1)
                slots(act, slot)

            @block.vector
            def _(dve):
                def norm(i, j, before):
                    ge(dve, s["x_turned"], i - 1)
                    ge(dve, sent[j], before * 32)
                    nc.vector.tensor_scalar(x_in[j][:, :], core.x[:, i, :], core.mean_var[:, i, 0:1],
                                            core.rstd[:, bass.ds(i, 1)], ALU.subtract, ALU.mult)\
                        .then_inc(s["x_ready"], 1)

                def low(i, j):
                    dve.wait_ge(s["xt_high"], i + 1)
                    ge(dve, s["lined"], i - 1)
                    nc.vector.tensor_tensor(xt[j][1][:, :, :], xt_ps[j][:, 0:D].rearrange("p (k t) -> p k t", k=KD),
                                            xt[j][0][:, :, :], ALU.subtract).then_inc(s["xt_low"], 1)

                def multiply(i, j):
                    dve.wait_ge(s["lined"], i + 1)
                    dve.wait_ge(s["silu_done"], i + 1)
                    ge(dve, s["h_low"], i - 1)
                    nc.vector.scalar_tensor_tensor(out=hidden[j][:, :], in0=lin_ps[j][:, 0:KF * P],
                                                   scalar=H_SCALE / W_SCALE, in1=gate[j][:, :], op0=ALU.mult,
                                                   op1=ALU.mult).then_inc(s["hidden_done"], 1)

                def hidden_low(i, j):
                    dve.wait_ge(s["h_high"], i + 1)
                    ge(dve, s["downed"], i - 1)
                    nc.vector.tensor_tensor(ht[j][1][:, :], hidden[j][:, :], ht[j][0][:, :], ALU.subtract)\
                        .then_inc(s["h_low"], 1)

                def finish(i, j):
                    dve.wait_ge(s["downed"], i + 1)
                    nc.vector.tensor_scalar(core.y[:, i, :], y_ps[j][:, 0:D], 1.0 / (H_SCALE * W_SCALE), None, ALU.mult)\
                        .then_inc(s["y_done"], 1)

                def cut_low(k, u):
                    dve.wait_ge(next_high, k * UNROLL + (u + 1))
                    nc.vector.scalar_tensor_tensor(out=w_next.part(1, k, u), in0=staged_part(u), scalar=W_SCALE,
                                                   in1=w_next.part(0, k, u), op0=ALU.mult, op1=ALU.subtract)\
                        .then_inc(next_low, 1)

                def slot(k, u):
                    i, j = k * UNROLL + u, u % 2
                    half = k * (UNROLL // 2) + u // 2
                    if real(i - 2):
                        finish(i - 2, j)
                    if real(i + 3):
                        norm(i + 3, 1 - j, half + 1 + u % 2)
                    if real(i):
                        cut_low(k, u)
                    if real(i):
                        multiply(i, j)
                    if real(i + 2):
                        low(i + 2, j)
                    if real(i):
                        hidden_low(i, j)
                norm(0, 0, 0)
                norm(1, 1, 0)
                low(0, 0)
                norm(2, 0, 1)
                low(1, 1)
                slots(dve, slot)
                dve.wait_ge(s["y_done"], n)

            @block.tensor
            def _(pe):
                def turn(i, j):
                    pe.wait_ge(s["x_ready"], i + 1)
                    ge(pe, s["xt_low"], i - 1)
                    for k in range(KD):
                        last = nc.tensor.transpose(xt_ps[j][:, k * P:(k + 1) * P], x_in[j][:, k * P:(k + 1) * P],
                                                   core.ident[:, :])
                    last.then_inc(s["x_turned"], 1)

                def three(out, left, right, blocks):
                    m = 0
                    for k in range(blocks):
                        for a, b in ((0, 0), (1, 0), (0, 1)):
                            m += 1
                            last = nc.tensor.matmul(out, left(a, k), right(b, k), start=(m == 1), stop=(m == 3 * blocks))
                    return last

                def up(out, j, column):
                    for f in range(KF):
                        at = column + f * P
                        last = three(out[:, f * P:(f + 1) * P], lambda a, k: w.up[a][:, 0, k, at:at + P],
                                     lambda b, k: xt[j][b][:, k, :], KD)
                    return last

                def down(i, j):
                    pe.wait_ge(s["h_low"], i + 1)
                    ge(pe, s["y_done"], i - 1)
                    three(y_ps[j][:, 0:D], lambda a, k: ht[j][a][:, k * P:(k + 1) * P],
                          lambda b, k: w.down[b][:, 0, k, :], KF).then_inc(s["downed"], 1)

                def slot(k, u):
                    i, j = k * UNROLL + u, u % 2
                    if real(i):
                        pe.wait_ge(s["xt_low"], i + 1)
                        ge(pe, s["silu_done"], i - 1)
                        up(gate_ps[j], j, F).then_inc(s["gated"], 1)
                        ge(pe, s["hidden_done"], i - 1)
                        up(lin_ps[j], j, 0).then_inc(s["lined"], 1)
                    if real(i + 2):
                        turn(i + 2, j)
                    if real(i - 1):
                        down(i - 1, 1 - j)
                turn(0, 0)
                turn(1, 1)
                slots(pe, slot)


def routed_experts(core, name, w, x_rows, y_rows, expert_of):
    nc = core.nc
    F, KF = w.F, w.KF
    n = SLOT_TILES
    with Phase(nc, name) as ph:
        x_in = [ph.sb(f"x_in{j}", [P, D]) for j in range(2)]
        xt = [[ph.sb(f"xt_{x}{j}", [P, KD, P], F16) for x in ("high", "low")] for j in range(2)]
        gate = [ph.sb(f"gate{j}", [P, F]) for j in range(2)]
        hidden = [ph.sb(f"hidden{j}", [P, F]) for j in range(2)]
        ht = [[ph.sb(f"ht_{x}{j}", [P, KF, P], F16) for x in ("high", "low")] for j in range(2)]
        y_sb = [ph.sb(f"y_sb{j}", [P, D]) for j in range(2)]
        xt_ps = ph.ps()
        lin_ps = [ph.ps() for j in range(2)]
        gate_ps = ph.ps()
        ht_ps = ph.ps()
        y_ps = [ph.ps() for j in range(2)]
        s = {k: ph.sem(k) for k in ("x_turned", "xt_high", "xt_low", "gated", "lined", "silu_done",
                                    "hidden_done", "h_turned", "ht_high", "ht_low", "downed", "y_done")}
        x_loaded = [ph.sem("x_loaded0"), ph.sem("x_loaded1")]
        y_stored = [ph.sem("y_stored0"), ph.sem("y_stored1")]

        def pairs(eng, pair):
            for k in range(2):
                pair(k)
            with eng.Fori(2, n // 2 - 1) as k:
                pair(k)
            pair(n // 2 - 1)

        def blocks(ap):
            return ap.rearrange("p (k t) -> p k t", t=P)

        pieces = [(slice(0, F // P), P)] if F >= P else []
        if F % P:
            pieces.append((slice(F // P, KF), F % P))

        with ph.block() as block:
            @block.sync
            def _(sp):
                def load(i, j):
                    ge(sp, s["x_turned"], i - 1)
                    sp.dma_start(x_in[j][:, :], x_rows[i, :, :]).then_inc(x_loaded[j], 16)

                tiles(sp, n, 2, load)

            @block.gpsimd
            def _(pool):
                def store(i, j):
                    pool.wait_ge(s["y_done"], i + 1)
                    pool.dma_start(y_rows[i, :, :], y_sb[j][:, :]).then_inc(y_stored[j], 16)

                tiles(pool, n, 2, store)
                for j in range(2):
                    pool.wait_ge(y_stored[j], n // 2 * 16)

            @block.scalar
            def _(act):
                def high(i, j):
                    act.wait_ge(s["x_turned"], i + 1)
                    ge(act, s["lined"], i - 1)
                    nc.scalar.activation(xt[j][0][:, :, :], blocks(xt_ps[:, 0:D]), ACT.Copy).then_inc(s["xt_high"], 1)

                def silu(i, j):
                    act.wait_ge(s["gated"], i + 1)
                    ge(act, s["hidden_done"], i - 1)
                    nc.scalar.activation(gate[j][:, :], gate_ps[:, 0:F], ACT.Silu, scale=1.0 / W_SCALE)\
                        .then_inc(s["silu_done"], 1)

                def hidden_high(i, j):
                    act.wait_ge(s["h_turned"], i + 1)
                    ge(act, s["downed"], i - 1)
                    for at, rows in pieces:
                        last = nc.scalar.activation(ht[j][0][0:rows, at, :], blocks(ht_ps[0:rows, 0:KF * P])[:, at, :],
                                                    ACT.Copy)
                    last.then_inc(s["ht_high"], 1)

                def pair(k):
                    for j in range(2):
                        i = k * 2 + j
                        silu(i, j)
                        if not (isinstance(i, int) and i == 0):
                            hidden_high(i - 1, 1 - j)
                        if not (isinstance(i, int) and i == n - 1):
                            high(i + 1, 1 - j)
                high(0, 0)
                pairs(act, pair)
                hidden_high(n - 1, 1)

            @block.vector
            def _(dve):
                def low(i, j):
                    dve.wait_ge(s["xt_high"], i + 1)
                    ge(dve, s["lined"], i - 1)
                    nc.vector.tensor_tensor(xt[j][1][:, :, :], blocks(xt_ps[:, 0:D]), xt[j][0][:, :, :],
                                            ALU.subtract).then_inc(s["xt_low"], 1)

                def multiply(i, j):
                    dve.wait_ge(s["lined"], i + 1)
                    dve.wait_ge(s["silu_done"], i + 1)
                    ge(dve, s["h_turned"], i - 1)
                    nc.vector.scalar_tensor_tensor(out=hidden[j][:, :], in0=lin_ps[j][:, 0:F], scalar=H_SCALE / W_SCALE,
                                                   in1=gate[j][:, :], op0=ALU.mult, op1=ALU.mult)\
                        .then_inc(s["hidden_done"], 1)

                def hidden_low(i, j):
                    dve.wait_ge(s["ht_high"], i + 1)
                    ge(dve, s["downed"], i - 1)
                    for at, rows in pieces:
                        last = nc.vector.tensor_tensor(ht[j][1][0:rows, at, :], blocks(ht_ps[0:rows, 0:KF * P])[:, at, :],
                                                       ht[j][0][0:rows, at, :], ALU.subtract)
                    last.then_inc(s["ht_low"], 1)

                def finish(i, j, before):
                    dve.wait_ge(s["downed"], i + 1)
                    ge(dve, y_stored[j], before * 16)
                    nc.vector.tensor_scalar(y_sb[j][:, :], y_ps[j][:, 0:D], 1.0 / (H_SCALE * W_SCALE), None, ALU.mult)\
                        .then_inc(s["y_done"], 1)

                def pair(k):
                    for j in range(2):
                        i = k * 2 + j
                        peeled = isinstance(i, int)
                        if not (peeled and i == 0):
                            hidden_low(i - 1, 1 - j)
                        if not (peeled and i == n - 1):
                            low(i + 1, 1 - j)
                        multiply(i, j)
                        if not (peeled and i < 2):
                            finish(i - 2, j, k - 1)
                low(0, 0)
                pairs(dve, pair)
                hidden_low(n - 1, 1)
                finish(n - 2, 0, n // 2 - 1)
                finish(n - 1, 1, n // 2 - 1)
                dve.wait_ge(s["y_done"], n)

            @block.tensor
            def _(pe):
                def turn(i, j, before):
                    pe.wait_ge(x_loaded[j], before * 16 + 16)
                    ge(pe, s["xt_low"], i)
                    for k in range(KD):
                        last = nc.tensor.transpose(xt_ps[:, k * P:(k + 1) * P], x_in[j][:, k * P:(k + 1) * P],
                                                   core.ident[:, :])
                    last.then_inc(s["x_turned"], 1)
                def three(out, left, right, stop_at):
                    m = 0
                    for k in range(stop_at):
                        for a, b in ((0, 0), (1, 0), (0, 1)):
                            m += 1
                            last = nc.tensor.matmul(out, left(a, k), right(b, k), start=(m == 1), stop=(m == 3 * stop_at))
                    return last

                def experts(k):
                    packed = pe.value_load(expert_of[0:1, bass.ds(k, 1)], min_val=0, max_val=E ** 4 - 1)
                    bits = E.bit_length() - 1
                    return [pe.snap((packed >> digit * bits) & (E - 1)) for digit in range(4)]

                def gate_up(i, j, e):
                    pe.wait_ge(s["xt_low"], i + 1)
                    ge(pe, s["silu_done"], i)
                    three(gate_ps[:, 0:F], lambda a, k: xt[j][a][:, k, :],
                          lambda b, k: w.up[b][:, e, k, F:2 * F], KD).then_inc(s["gated"], 1)

                def line_up(i, j, e):
                    ge(pe, s["hidden_done"], i - 1)
                    three(lin_ps[j][:, 0:F], lambda a, k: xt[j][a][:, k, :],
                          lambda b, k: w.up[b][:, e, k, 0:F], KD).then_inc(s["lined"], 1)

                def turn_hidden(i, j):
                    pe.wait_ge(s["hidden_done"], i + 1)
                    ge(pe, s["ht_low"], i)
                    for k in range(KF):
                        last = nc.tensor.transpose(ht_ps[0:w.rows(k), k * P:(k + 1) * P],
                                                   hidden[j][:, k * P:k * P + w.rows(k)], core.ident[:, :])
                    last.then_inc(s["h_turned"], 1)

                def down(i, j, e):
                    pe.wait_ge(s["ht_low"], i + 1)
                    ge(pe, s["y_done"], i - 1)
                    three(y_ps[j][:, 0:D], lambda a, k: ht[j][a][0:w.rows(k), k, :],
                          lambda b, k: w.down[b][0:w.rows(k), e, k, :], KF).then_inc(s["downed"], 1)

                def pair(k):
                    e = experts(k)
                    for j in range(2):
                        i = k * 2 + j
                        peeled = isinstance(i, int)
                        gate_up(i, j, e[j + 2])
                        if not (peeled and i == 0):
                            turn_hidden(i - 1, 1 - j)
                        if not (peeled and i == n - 1):
                            turn(i + 1, 1 - j, k + j)
                        line_up(i, j, e[j + 2])
                        if not (peeled and i < 2):
                            down(i - 2, j, e[j])
                        if peeled and i == n - 1:
                            turn_hidden(i, j)
                            down(i - 1, 1 - j, e[j + 1])
                            down(i, j, e[j + 2])
                turn(0, 0, 0)
                pairs(pe, pair)


class Routing:

    def __init__(self, ph):
        self.logits = ph.sb("logits", [P, T, E])
        self.slots = ph.sb("slots", [P, T, 2], I32)
        self.weights = ph.sb("weights", [P, T, 2])
        self.expert_of = ph.sb("expert_of", [P, SLOT_TILES // 2], I32)


def route(core, name, r, normalise, bias_row):
    nc = core.nc
    with Phase(nc, name) as ph:
        bias = ph.sb("bias", [P, E])
        top = ph.sb("top", [P, T, 8])
        index = ph.sb("index", [P, T, 8], mybir.dt.uint32)
        index_f = ph.sb("index_f", [P, T, 2])
        expert_iota = ph.sb("expert_iota", [P, E])
        tile_iota = ph.sb("tile_iota", [P, SLOT_TILES])
        chosen = [ph.sb(f"chosen{c}", [P, T, E]) for c in range(2)]
        both = ph.sb("both", [P, T, E])
        before = ph.sb("before", [P, P])
        ones = ph.sb("ones", [P, P])
        total = ph.sb("total", [P, T, E])
        running = ph.sb("running", [P, T, E])
        count_i = ph.sb("count_i", [P, E], I32)
        n_tiles = ph.sb("n_tiles", [P, E])
        ends = ph.sb("ends", [P, E])
        starts = ph.sb("starts", [P, E])
        slot = ph.sb("slot", [P, T, E])
        picked = ph.sb("picked", [P, T, E])
        slot_f = ph.sb("slot_f", [P, T, 2])
        passed = ph.sb("passed", [P, SLOT_TILES, E])
        expert_f = ph.sb("expert_f", [P, SLOT_TILES])
        packed = ph.sb("packed", [P, SLOT_TILES // 2])
        shifted = ph.sb("shifted", [P, T, E])
        expd = ph.sb("expd", [P, T, E])
        denom = ph.sb("denom", [P, T, E])
        sums = ph.sb("sums", [P, T])
        rank_ps, total_ps = ph.ps(), ph.ps()
        bias_in, masks, counted = ph.sem("bias_in"), ph.sem("masks"), ph.sem("counted")
        chain, exp_ready, exp_done, both_done = ph.sem("chain"), ph.sem("exp_ready"), ph.sem("exp_done"), ph.sem("both")

        with ph.block() as block:
            @block.sync
            def _(sp):
                if bias_row is not None:
                    sp.dma_start(bias[:, :], bias_row.to_broadcast([P, E])).then_inc(bias_in, 16)

            @block.gpsimd
            def _(pool):
                nc.gpsimd.memset(ones[:, :], 1.0).then_inc(masks, 1)
                nc.gpsimd.memset(before[:, :], 1.0).then_inc(masks, 1)
                nc.gpsimd.iota(expert_iota[:, :], pattern=[[1, E]], base=0, channel_multiplier=0,
                               allow_small_or_imprecise_dtypes=True).then_inc(masks, 1)
                nc.gpsimd.iota(tile_iota[:, :], pattern=[[1, SLOT_TILES]], base=0, channel_multiplier=0,
                               allow_small_or_imprecise_dtypes=True).then_inc(masks, 1)
                pool.wait_ge(masks, 4)
                nc.gpsimd.affine_select(out=before[:, :], in_=before[:, :], compare_op=ALU.is_gt, fill=0.0, base=0,
                                        pattern=[[1, P]], channel_multiplier=-1).then_inc(masks, 1)

            @block.tensor
            def _(pe):
                pe.wait_ge(masks, 5)
                pe.wait_ge(both_done, 1)
                flat = both[:, :, :].rearrange("p t e -> p (t e)")
                nc.tensor.matmul(rank_ps[:, 0:T * E], before[:, :], flat, start=True, stop=True)
                nc.tensor.matmul(total_ps[:, 0:T * E], ones[:, :], flat, start=True, stop=True).then_inc(counted, 1)

            @block.scalar
            def _(act):
                act.wait_ge(exp_ready, 1)
                nc.scalar.activation(expd[:, :, :], shifted[:, :, :], ACT.Exp).then_inc(exp_done, 1)

            @block.vector
            def _(dve):
                steps = [0]

                def then(ins):
                    steps[0] += 1
                    ins.then_inc(chain, 1)
                    dve.wait_ge(chain, steps[0])

                dve.wait_ge(masks, 5)
                if bias_row is not None:
                    dve.wait_ge(bias_in, 16)
                    then(nc.vector.tensor_tensor(r.logits[:, :, :], r.logits[:, :, :],
                                                 bias[:, :].unsqueeze(1).to_broadcast([P, T, E]), ALU.add))
                for t in range(T):
                    last = nc.vector.max(top[:, t, :], r.logits[:, t, :])
                then(last)
                for t in range(T):
                    last = nc.vector.max_index(index[:, t, :], top[:, t, :], r.logits[:, t, :])
                then(last)
                then(nc.vector.tensor_copy(index_f[:, :, :], index[:, :, 0:2]))
                for c in range(2):
                    last = nc.vector.tensor_tensor(chosen[c][:, :, :],
                                                   expert_iota[:, :].unsqueeze(1).to_broadcast([P, T, E]),
                                                   index_f[:, :, c:c + 1].to_broadcast([P, T, E]), ALU.is_equal)
                then(last)
                nc.vector.tensor_tensor(both[:, :, :], chosen[0][:, :, :], chosen[1][:, :, :], ALU.add)\
                    .then_inc(both_done, 1)

                if normalise:
                    nc.vector.tensor_scalar(shifted[:, :, :], top[:, :, :], -1.0, None, ALU.mult).then_inc(exp_ready, 1)
                    dve.wait_ge(exp_done, 1)
                    then(nc.vector.tensor_scalar(denom[:, :, 0:2], expd[:, :, 0:2], 1.0, None, ALU.add))
                    then(nc.vector.reciprocal(r.weights[:, :, :], denom[:, :, 0:2]))
                    then(nc.vector.tensor_tensor(sums[:, :], r.weights[:, :, 0], r.weights[:, :, 1], ALU.add))
                    then(nc.vector.reciprocal(sums[:, :], sums[:, :]))
                    then(nc.vector.tensor_tensor(r.weights[:, :, :], r.weights[:, :, :],
                                                 sums[:, :].unsqueeze(2).to_broadcast([P, T, 2]), ALU.mult))
                else:
                    nc.vector.tensor_tensor(shifted[:, :, :], top[:, :, :], top[:, :, 0:1].to_broadcast([P, T, E]),
                                            ALU.subtract).then_inc(exp_ready, 1)
                    dve.wait_ge(exp_done, 1)
                    then(nc.vector.tensor_reduce(sums[:, :], expd[:, :, :], AX.X, ALU.add))
                    then(nc.vector.reciprocal(sums[:, :], sums[:, :]))
                    then(nc.vector.tensor_tensor(r.weights[:, :, :], expd[:, :, 0:2],
                                                 sums[:, :].unsqueeze(2).to_broadcast([P, T, 2]), ALU.mult))

                dve.wait_ge(counted, 1)
                then(nc.vector.tensor_copy(total[:, :, :], total_ps[:, 0:T * E].rearrange("p (t e) -> p t e", e=E)))
                for e in range(E):
                    last = nc.vector.tensor_tensor_scan(running[:, :, e], ones[:, 0:T], total[:, :, e], 0.0,
                                                        ALU.mult, ALU.add)
                then(last)
                then(nc.vector.tensor_scalar(count_i[:, :], running[:, T - 1, :], float(P - 1), None, ALU.add))
                then(nc.vector.tensor_scalar(count_i[:, :], count_i[:, :], P.bit_length() - 1, None,
                                             ALU.arith_shift_right))
                then(nc.vector.tensor_copy(n_tiles[:, :], count_i[:, :]))
                then(nc.vector.tensor_tensor_scan(ends[:, :], ones[:, 0:E], n_tiles[:, :], 0.0, ALU.mult, ALU.add))
                then(nc.vector.tensor_tensor(starts[:, :], ends[:, :], n_tiles[:, :], ALU.subtract))
                then(nc.vector.tensor_tensor(slot[:, :, :], running[:, :, :], total[:, :, :], ALU.subtract))
                then(nc.vector.tensor_tensor(slot[:, :, :], rank_ps[:, 0:T * E].rearrange("p (t e) -> p t e", e=E),
                                             slot[:, :, :], ALU.add))
                then(nc.vector.tensor_scalar(starts[:, :], starts[:, :], float(P), None, ALU.mult))
                then(nc.vector.tensor_tensor(slot[:, :, :], slot[:, :, :],
                                             starts[:, :].unsqueeze(1).to_broadcast([P, T, E]), ALU.add))
                for c in range(2):
                    then(nc.vector.tensor_tensor(picked[:, :, :], chosen[c][:, :, :], slot[:, :, :], ALU.mult))
                    then(nc.vector.tensor_reduce(slot_f[:, :, c], picked[:, :, :], AX.X, ALU.add))
                then(nc.vector.tensor_copy(r.slots[:, :, :], slot_f[:, :, :]))
                then(nc.vector.tensor_tensor(passed[:, :, :], ends[:, :].unsqueeze(1).to_broadcast([P, SLOT_TILES, E]),
                                             tile_iota[:, :].unsqueeze(2).to_broadcast([P, SLOT_TILES, E]), ALU.is_le))
                then(nc.vector.tensor_reduce(expert_f[:, :], passed[:, :, :], AX.X, ALU.add))
                then(nc.vector.tensor_scalar(expert_f[:, :], expert_f[:, :], float(E - 1), None, ALU.min))
                pairs = expert_f[:, :].rearrange("p (k c) -> p k c", c=2)
                then(nc.vector.scalar_tensor_tensor(out=packed[:, :], in0=pairs[:, :, 1], scalar=float(E),
                                                    in1=pairs[:, :, 0], op0=ALU.mult, op1=ALU.add))
                nc.vector.tensor_scalar(r.expert_of[:, 0:1], packed[:, 0:1], float(E * E), None, ALU.mult)
                then(nc.vector.scalar_tensor_tensor(out=r.expert_of[:, 1:], in0=packed[:, 1:], scalar=float(E * E),
                                                    in1=packed[:, 0:SLOT_TILES // 2 - 1], op0=ALU.mult,
                                                    op1=ALU.add))


def router_logits(core, name, router, logits):
    nc = core.nc
    G = 2
    NG = T // G
    with Phase(nc, name) as ph:
        xhat = [ph.sb(f"xhat{j}", [P, G, D]) for j in range(2)]
        xt = [[ph.sb(f"xt_{x}{j}", [P, G * KD, P], F16) for x in ("high", "low")] for j in range(2)]
        turn_ps = [ph.ps() for j in range(2)]
        logit_ps = ph.ps()
        s = {n: ph.sem(n) for n in ("xhat_done", "turned", "high", "low", "logged", "kept")}
        with ph.block() as block:
            @block.tensor
            def _(pe):
                def turn(g, j):
                    pe.wait_ge(s["xhat_done"], g * G + G)
                    ge(pe, s["low"], g - 1)
                    for u in range(G):
                        for k in range(KD):
                            at = u * KD + k
                            last = nc.tensor.transpose(turn_ps[j][:, at * P:(at + 1) * P],
                                                       xhat[j][:, u, k * P:(k + 1) * P], core.ident[:, :])
                    last.then_inc(s["turned"], 1)

                def multiply(g, j):
                    pe.wait_ge(s["low"], g + 1)
                    for u in range(G):
                        n = 0
                        for k in range(KD):
                            for a in range(2):
                                for b in range(2):
                                    n += 1
                                    last = nc.tensor.matmul(logit_ps[:, bass.ds(g * (G * E) + u * E, E)],
                                                            xt[j][a][:, u * KD + k, :], router[b][:, k, :],
                                                            start=(n == 1), stop=(n == 4 * KD))
                    last.then_inc(s["logged"], 1)

                def pair(k, more=True):
                    turn(k * 2 + 1, 1)
                    multiply(k * 2, 0)
                    if more:
                        turn(k * 2 + 2, 0)
                    multiply(k * 2 + 1, 1)
                turn(0, 0)
                pair(0)
                with pe.Fori(1, NG // 2 - 1) as k:
                    pair(k)
                pair(NG // 2 - 1, more=False)

            @block.scalar
            def _(act):
                def high(g, j):
                    act.wait_ge(s["turned"], g + 1)
                    ge(act, s["logged"], g - 1)
                    nc.scalar.activation(xt[j][0][:, :, :], turn_ps[j][:, :].rearrange("p (k t) -> p k t", t=P),
                                         ACT.Copy).then_inc(s["high"], 1)
                tiles(act, NG, 2, high)

            @block.vector
            def _(dve):
                def norm(g, j):
                    ge(dve, s["turned"], g - 1)
                    for u in range(G):
                        nc.vector.tensor_scalar(xhat[j][:, u, :], core.x[:, g * G + u, :],
                                                core.mean_var[:, g * G + u, 0:1],
                                                core.rstd[:, bass.ds(g * G + u, 1)], ALU.subtract, ALU.mult)\
                            .then_inc(s["xhat_done"], 1)

                def low(g, j):
                    dve.wait_ge(s["high"], g + 1)
                    ge(dve, s["logged"], g - 1)
                    nc.vector.tensor_tensor(xt[j][1][:, :, :], turn_ps[j][:, :].rearrange("p (k t) -> p k t", t=P),
                                            xt[j][0][:, :, :], ALU.subtract).then_inc(s["low"], 1)
                norm(0, 0)
                norm(1, 1)
                low(0, 0)
                norm(2, 0)
                low(1, 1)
                with dve.Fori(1, NG // 2 - 1) as k:
                    norm(k * 2 + 1, 1)
                    low(k * 2, 0)
                    norm(k * 2 + 2, 0)
                    low(k * 2 + 1, 1)
                norm(NG - 1, 1)
                low(NG - 2, 0)
                low(NG - 1, 1)
                dve.wait_ge(s["logged"], NG)
                nc.vector.tensor_scalar(logits[:, :, :], logit_ps[:, 0:T * E].rearrange("p (t e) -> p t e", e=E),
                                        1.0 / W_SCALE, None, ALU.mult).then_inc(s["kept"], 1)
                dve.wait_ge(s["kept"], 1)


@contextmanager
def mixture(core, nc, name, F, shared_F, normalise, router_dram, bias_row, up_s, down_s, up_r, down_r, x_rows, y_rows):
    with Phase(nc, name) as ph:
        r = Routing(ph)
        with Phase(nc, name + "w") as pw:
            w = Weights(pw, E, F)
            with Phase(nc, name + "s") as ps:
                w_shared = Weights(ps, 1, shared_F)
                with Phase(nc, name + "l") as pl:
                    router = [pl.sb(f"router_{x}", [P, KD, E], F16) for x in ("high", "low")]
                    split_scaled(core, name + "ws", w_shared.parts(up_s, down_s) +
                                 [(router_dram.rearrange("(k p) e -> p k e", p=P), router[0][:, :, :],
                                   router[1][:, :, :])])
                    router_logits(core, name + "rl", router, r.logits)
                    route(core, name + "r", r, normalise, bias_row)
                shared_expert(core, name + "fs", w_shared, x_rows, r.slots, w, (up_r, down_r))
            routed_experts(core, name + "fx", w, x_rows, y_rows, r.expert_of)
        Phase.clear_semaphores(nc)
        yield r


def build(nc, a, out):
    ctx = ExitStack()
    with ctx:
        Phase.taken_semaphores = []
        core = Core(nc, ctx)
        constants(core)
        x_dram = a["L0_attn_x"].rearrange("b (u p) d -> b p u d", p=P)
        out_dram = out.rearrange("b (u p) d -> b p u d", p=P)
        x_rows = nc.dram_tensor("x_rows", (SLOT_TILES, P, D), F32, kind="Internal").ap()
        y_rows = nc.dram_tensor("y_rows", (SLOT_TILES, P, D), F32, kind="Internal").ap()
        x_statistics(core, x_dram)
        with Phase(nc, "w0") as ph:
            qkv_high = ph.sb("qkv_high", [P, KD, 3 * D], F32R)
            qkv_low = ph.sb("qkv_low", [P, KD, 3 * D], F32R)
            wo_high = ph.sb("wo_high", [P, KD, D], F32R)
            wo_low = ph.sb("wo_low", [P, KD, D], F32R)
            parts = []
            for k in range(KD):
                parts.append((a["qkv0"][k * P:(k + 1) * P, :], qkv_high[:, k, :], qkv_low[:, k, :]))
                parts.append((a["L0_attn_wo"][k * P:(k + 1) * P, :], wo_high[:, k, :], wo_low[:, k, :]))
            split_weights(core, "w0s", parts)
            linear_attention(core, qkv_high, qkv_low, a["bias_q0"], a["bias_kv0"], x_rows)
            residual(core, "wo0", project=(wo_high, wo_low, a["bias_o0"]))
        q_dram = nc.dram_tensor("q_scratch", (2, D, B * N), F32, kind="Internal").ap()
        k_dram = nc.dram_tensor("k_scratch", (2, NKV * DH, B * N), F32, kind="Internal").ap()
        o_dram = nc.dram_tensor("o_scratch", (2 * B, NKV, P, N // 2), F32, kind="Internal").ap()
        negmax_dram = nc.dram_tensor("negmax_scratch", (2 * B, 2, HEADS, N // 2), F32, kind="Internal").ap()
        with mixture(core, nc, "m0", 512, 512, True, a["router0"], a["bias_r0"], a["up0s"], a["down0s"], a["up0"],
                     a["down0"], x_rows, y_rows) as r, Phase(nc, "v") as ph:
            v_all = ph.sb("v_all", [P, T, NKV, 32])
            with Phase(nc, "w2") as pw:
                high = pw.sb("high", [P, KD, 3 * P], F32R)
                low = pw.sb("low", [P, KD, 3 * P], F32R)
                split_weights(core, "w2s", [(a["qkv1"][k * P:(k + 1) * P, :], high[:, k, :], low[:, k, :])
                                            for k in range(KD)])
                residual(core, "m0g", gather=(r, y_rows), follow=lambda phase: AttentionProjections(
                    core, phase, high, low, a["bias_qkv1"], q_dram, k_dram, v_all))
            softmax_attention(core, q_dram, k_dram, v_all, negmax_dram,
                              o_dram.rearrange("(b h) k p t -> b h k p t", h=2))
        attention_normalised(core, o_dram)
        with Phase(nc, "w3") as pw:
            high = pw.sb("high", [P, KD, D], F32R)
            low = pw.sb("low", [P, KD, D], F32R)
            split_weights(core, "w3s", [(a["wo1"][k * P:(k + 1) * P, :], high[:, k, :], low[:, k, :])
                                        for k in range(KD)])
            residual(core, "wo1", project=(high, low, a["bias_o1"]))
        Phase.clear_semaphores(nc)
        with mixture(core, nc, "m1", 192, 384, False, a["router1"], None, a["up1s"], a["down1s"], a["up1"],
                     a["down1"], x_rows, y_rows) as r:
            residual(core, "m1g", gather=(r, y_rows), out_dram=out_dram)


def kernel(**inputs):
    import numpy as _np
    import concourse.bacc as _bacc
    from concourse import mybir as _mybir
    from concourse.bass_utils import run_bass_kernel_spmd as _run

    given = {k: _np.asarray(v) for k, v in inputs.items()}
    laid = {
        "L0_attn_x": given["L0_attn_x"],
        "qkv0": _np.concatenate([given["L0_attn_wq"], given["L0_attn_wk"], given["L0_attn_wv"]], axis=1),
        "bias_q0": given["L0_attn_bq"].reshape(KD, P).T,
        "bias_kv0": _np.concatenate([given["L0_attn_bk"], given["L0_attn_bv"]])[None, :],
        "L0_attn_wo": given["L0_attn_wo"],
        "bias_o0": given["L0_attn_bo"][None, :],
        "qkv1": _np.concatenate([given["L1_attn_Wq"], given["L1_attn_Wk"], given["L1_attn_Wv"]], axis=1),
        "bias_qkv1": _np.concatenate([given["L1_attn_bq"], given["L1_attn_bk"], given["L1_attn_bv"]])
        .reshape(3, P).T,
        "wo1": given["L1_attn_Wo"].reshape(GROUPS, NKV, DH, D).transpose(1, 0, 2, 3).reshape(D, D),
        "bias_o1": given["L1_attn_bo"][None, :],
        "router0": given["L0_ffn_router_w"].T,
        "bias_r0": given["L0_ffn_routing_bias"][None, :],
        "up0s": _np.concatenate([given["L0_ffn_su_w"], given["L0_ffn_sg_w"]], axis=0).T[None],
        "down0s": given["L0_ffn_sd_w"].T[None],
        "up0": _np.concatenate([given["L0_ffn_wu"], given["L0_ffn_wg"]], axis=1).transpose(0, 2, 1),
        "down0": given["L0_ffn_wd"].transpose(0, 2, 1),
        "router1": given["L1_ffn_gate_w"].T,
        "up1s": given["L1_ffn_Ws1"].T[None],
        "down1s": given["L1_ffn_Ws2"].T[None],
        "up1": given["L1_ffn_W1"].transpose(0, 2, 1),
        "down1": given["L1_ffn_W2"].transpose(0, 2, 1),
    }
    nc = _bacc.Bacc("TRN2", target_bir_lowering=False, num_devices=1)
    arrays, args = {}, {}
    for name, v in laid.items():
        v = _np.ascontiguousarray(v)
        arrays[f"in_{name}"] = v
        args[name] = nc.dram_tensor(f"in_{name}", v.shape, _mybir.dt.from_np(v.dtype), kind="ExternalInput").ap()
    out = nc.dram_tensor("out_x", (B, N, D), _mybir.dt.float32, kind="ExternalOutput").ap()
    build(nc, args, out)
    return _run(nc, [arrays], core_ids=[0]).results[0]["out_x"]
```
